# Optimizing a Trainium2 kernel written in Bass

```python
import numpy as np
import jax
import jax.numpy as jnp

def _softmax(x, axis=-1):
    return jax.nn.softmax(x, axis=axis)

def _gelu(x):
    return jax.nn.gelu(x, approximate=True)

def _silu(x):
    return jax.nn.silu(x)

def _sigmoid(x):
    return jax.nn.sigmoid(x)

def _layernorm(x, axis=-1, eps=1e-05):
    m = jnp.mean(x, axis=axis, keepdims=True)
    v = jnp.var(x, axis=axis, keepdims=True)
    return (x - m) / jnp.sqrt(v + eps)

def _scatter_add(tgt, idx, src, axis=0):
    return tgt.at[idx].add(src)

def _segment_sum(src, seg, n):
    return jax.ops.segment_sum(src, seg, n)
kernel_name = 'mk_gnn_resnorm_d2_gnn_r8_40231f'

def setup_inputs(seed: int=0):
    np.random.seed(seed)
    _w = jnp.asarray

    def _rec_inputs():
        import jax
        import jax.numpy as jnp
        _gk = jax.random.key(seed)
        x = -0.000202 + 1 * jax.random.normal(jax.random.fold_in(_gk, 1), (12500, 128), jnp.float32)
        src = jax.random.randint(jax.random.fold_in(_gk, 2), (200000,), 0, 12500, jnp.int32)
        dst = jax.random.randint(jax.random.fold_in(_gk, 3), (200000,), 0, 12500, jnp.int32)
        _o = jnp.argsort(dst, stable=True)
        src = src[_o]
        dst = dst[_o]
        edge_attr_128 = -8.16379e-05 + 0.999858 * jax.random.normal(jax.random.fold_in(_gk, 11), (200000, 128), jnp.float32)
        return (x, src, dst, edge_attr_128)
    x, src, dst, edge_attr_128 = _rec_inputs()

    def _L0_gnn_setup():
        import jax, jax.numpy as jnp
        import numpy as np
        N_NODES = 6250
        N_EDGES = 100000
        DIM = 128
        key = jax.random.key(seed)
        k1, k2, k3, k4, k5, k6 = jax.random.split(key, 6)
        node_emb = jax.random.normal(k1, (N_NODES, DIM), dtype=jnp.float32)
        edge_emb = jax.random.normal(k2, (N_EDGES, DIM), dtype=jnp.float32)
        W_att_w = jax.random.normal(k3, (2 * DIM,), dtype=jnp.float32) * 0.05
        W_att_b = jax.random.normal(k4, (1,), dtype=jnp.float32) * 0.05
        src = jax.random.randint(k5, (N_EDGES,), 0, N_NODES, dtype=jnp.int32)
        off = jax.random.randint(k6, (N_EDGES,), 1, N_NODES, dtype=jnp.int32)
        dst = (src + off) % N_NODES
        edge_list = jnp.stack([src, dst], axis=1)
        return {'node_emb': node_emb, 'edge_emb': edge_emb, 'W_att_w': W_att_w, 'W_att_b': W_att_b, 'edge_list': edge_list}
    _L0_gnn_all = _L0_gnn_setup()
    _L0_gnn_in = {k: v for k, v in _L0_gnn_all.items() if k in ('W_att_w', 'W_att_b')}
    del _L0_gnn_all

    def _L1_gnn_setup():
        import jax, jax.numpy as jnp
        import numpy as np
        N = 12500
        E = 200000
        IN = 128
        OUT = 128
        key = jax.random.key(seed)
        k1, k2, k3 = jax.random.split(key, 3)
        node_feature = jax.random.normal(k1, (N, IN), dtype=jnp.float32)
        edge_index = jax.random.randint(k2, (2, E), 0, N, dtype=jnp.int64)
        W = jax.random.normal(k3, (IN, OUT), dtype=jnp.float32) * (1.0 / np.sqrt(IN))
        b = jnp.zeros((OUT,), dtype=jnp.float32)
        return {'node_feature': node_feature, 'edge_index': edge_index, 'W': W, 'b': b}
    _L1_gnn_all = _L1_gnn_setup()
    _L1_gnn_in = {k: v for k, v in _L1_gnn_all.items() if k in ('W', 'b')}
    del _L1_gnn_all
    return {'x': x, 'src': src, 'dst': dst, 'edge_attr_128': edge_attr_128, 'L0_gnn_W_att_w': _L0_gnn_in['W_att_w'], 'L0_gnn_W_att_b': _L0_gnn_in['W_att_b'], 'L1_gnn_W': _L1_gnn_in['W'], 'L1_gnn_b': _L1_gnn_in['b']}

def reference(x, src, dst, edge_attr_128, L0_gnn_W_att_w, L0_gnn_W_att_b, L1_gnn_W, L1_gnn_b):
    import jax
    import jax.numpy as jnp

    def _L0_gnn_ref(node_emb, edge_emb, W_att_w, W_att_b, edge_list):
        import jax, jax.numpy as jnp
        import numpy as np
        N_NODES = 6250
        N_EDGES = 100000
        DIM = 128
        n_nodes, node_dim = node_emb.shape
        n_edges = edge_emb.shape[0]
        w_n = W_att_w[:node_dim]
        w_e = W_att_w[node_dim:]
        b = W_att_b[0]
        seg = jnp.concatenate([edge_list[:, 0], edge_list[:, 1]])
        s_node = node_emb @ w_n
        s_edge = edge_emb @ w_e
        raw = s_node[seg] + jnp.concatenate([s_edge, s_edge]) + b
        score = jax.nn.leaky_relu(raw, negative_slope=0.2)
        m = jax.ops.segment_max(score, seg, num_segments=n_nodes)
        m = jnp.where(jnp.isfinite(m), m, 0.0)
        ex = jnp.exp(score - m[seg])
        denom = jax.ops.segment_sum(ex, seg, num_segments=n_nodes)
        denom_safe = jnp.where(denom > 0, denom, 1.0)
        att = ex / denom_safe[seg]
        ee2 = jnp.concatenate([edge_emb, edge_emb], axis=0)
        agg = jax.ops.segment_sum(att[:, None] * ee2, seg, num_segments=n_nodes)
        out = jax.nn.gelu(agg, approximate=False)
        deg = jax.ops.segment_sum(jnp.ones_like(score), seg, num_segments=n_nodes)
        return jnp.where((deg > 0)[:, None], out, node_emb)

    def _L1_gnn_ref(node_feature, edge_index, W, b):
        import jax, jax.numpy as jnp
        import numpy as np
        N = 12500
        E = 200000
        IN = 128
        OUT = 128
        n = node_feature.shape[0]
        x = node_feature @ W
        loops = jnp.arange(n, dtype=edge_index.dtype)
        src = jnp.concatenate([edge_index[0], loops])
        dst = jnp.concatenate([edge_index[1], loops])
        deg = jax.ops.segment_sum(jnp.ones_like(src, dtype=x.dtype), dst, num_segments=n)
        dinv = jnp.where(deg > 0, jax.lax.rsqrt(deg), 0.0)
        norm = dinv[src] * dinv[dst]
        msg = x[src] * norm[:, None]
        agg = jax.ops.segment_sum(msg, dst, num_segments=n)
        out = agg + b
        return jax.nn.relu(out)
    edge_index = jnp.stack([src, dst])
    edge_index_t = jnp.stack([src, dst], axis=1)
    x = _layernorm(x + _L0_gnn_ref(x, edge_attr_128, L0_gnn_W_att_w, L0_gnn_W_att_b, edge_index_t), axis=-1)
    x = _layernorm(x + _L1_gnn_ref(x, edge_index, L1_gnn_W, L1_gnn_b), axis=-1)
    return x

_drawn_inputs = setup_inputs


def setup_inputs(seed=0):
    import zlib

    import numpy as np

    out = dict(_drawn_inputs(seed))
    spreads = {'L1_gnn_b': (0.0, 0.1)}
    factors = {}
    for name, (base, spread) in spreads.items():
        noise = np.random.default_rng([zlib.crc32(name.encode()), seed]).standard_normal(out[name].shape)
        drawn = base * np.exp(spread * noise) if base else spread * noise
        out[name] = jnp.asarray(drawn.astype(out[name].dtype))
    for name, factor in factors.items():
        out[name] = (out[name] * factor).astype(out[name].dtype)
    return out
```

```python
import concourse.bass as bass
from concourse import mybir
from contextlib import ExitStack

F32, BF16, I32 = mybir.dt.float32, mybir.dt.bfloat16, mybir.dt.int32
ALU = mybir.AluOpType
ACT = mybir.ActivationFunctionType
AX = mybir.AxisListType

P = 128
N, E, D = 12500, 200000, 128
NB = -(-N // P)
LAST_NODES = N - (NB - 1) * P
T = 4
GE = P * T
G = -(-E // GE)
GF = E // GE
LAST_P = (E - GF * GE) // T
C = T * G
E_PAD = G * GE
PAD_ROWS = E_PAD - E
S = G + NB - 1
ROW = D + 4
SCORE, SOURCE, TARGET, ONE = D, D + 1, D + 2, D + 3
NO_NODE = NB * P
BIG = 1e30
SLOPE, EPS = 0.2, 1e-5
U = 6
BR = 3
CH = 7
NCH = NB // CH
assert LAST_P * T == E - GF * GE and GF % BR == 0 and NB % CH == 0 and GF % 2 == 0
assert (S - 2) % U == 0 and U % 2 == 0 and U % 3 == 0


def resnorm_gnn_kernel(nc, x, src, dst, edge_attr, att_w, att_b, w1, b1, out):
    ctx = ExitStack()
    with ctx:
        def sb(name, shape, dt=F32):
            return ctx.enter_context(nc.sbuf_tensor(name, shape, dt))

        def pb(name, shape, dt=F32):
            return ctx.enter_context(nc.psum_tensor(name, shape, dt))

        def sem(name):
            return ctx.enter_context(nc.semaphore(name))

        def dram(name, shape):
            return nc.dram_tensor(name, shape, F32)

        ds = bass.ds
        SIDES = ("src", "dst")

        rows = {"src": dram("rows_by_source", (E_PAD, ROW)), "dst": dram("rows_by_target", (E_PAD, ROW)),
                "msg": dram("messages", (E_PAD, ROW))}
        sums = {k: dram(f"sums_{k}", (S, P, ROW)) for k in ("src", "dst", "msg")}
        table = dram("projected_nodes", ((NB + 1) * P, D))

        iota_f = sb("iota_f", [P, P])
        iota_p = sb("iota_p", [P, 1])
        iota_s = sb("iota_s", [P, S])
        ident = sb("ident", [P, P])
        identb = sb("identb", [P, P], BF16)
        below = sb("below", [P, P])
        upto = sb("upto", [P, P])
        ones = sb("ones", [P, P])
        half_n = sb("half_n", [P, NB])
        nodes = sb("nodes", [P, NB, D])
        ids = {k: sb(f"ids_{k}", [P, C], I32) for k in SIDES}
        blk = {k: sb(f"blk_{k}", [P, C]) for k in SIDES}
        w_node = sb("w_node", [P, D])
        w_edge = sb("w_edge", [P, D])
        att_bias = sb("att_bias", [P, 1])
        w_proj = sb("w_proj", [P, D])
        out_bias = sb("out_bias", [P, D])
        hot = {k: sb(f"hot_{k}", [P, 2, T, NB], BF16) for k in SIDES}
        low4 = sb("low4", [P, 2, T])
        hot_low = sb("hot_low", [P, 2, T, P], BF16)
        count = {k: sb(f"count_{k}", [P, NB]) for k in SIDES}
        total = {k: sb(f"total_{k}", [P, 1]) for k in SIDES}
        total_b = {k: sb(f"total_b_{k}", [P, P]) for k in SIDES}
        nextpos = {k: sb(f"nextpos_{k}", [P, NB]) for k in SIDES}
        cumi = {k: sb(f"cumi_{k}", [P, 1], I32) for k in SIDES}
        last = {k: sb(f"last_{k}", [P, 1]) for k in SIDES}
        last_i = {k: sb(f"last_i_{k}", [1, NB], I32) for k in SIDES}
        done = {k: sb(f"done_{k}", [P, S]) for k in SIDES}
        first_node = {k: sb(f"first_node_{k}", [P, S]) for k in SIDES}
        keep = {k: sb(f"keep_{k}", [P, S]) for k in SIDES}
        drop = {k: sb(f"drop_{k}", [P, S]) for k in SIDES}
        group_i = {k: sb(f"group_i_{k}", [1, S], I32) for k in SIDES}
        s_node = sb("s_node", [P, NB])
        s_nodeT = sb("s_nodeT", [P, P])
        s_step = {k: sb(f"s_step_{k}", [P, S]) for k in SIDES}
        degT = sb("degT", [P, P])
        dinv = sb("dinv", [P, NB])
        deal = sb("deal", [P, BR, T, ROW])
        prod = sb("prod", [P, T, D])
        junk = sb("junk", [P, 2, NB])
        posf = sb("posf", [P, 2 * T])
        pos = sb("pos", [P, BR, 2 * T], I32)
        ring = sb("ring", [P, U, T, ROW])
        local = sb("local", [P, 2, T])
        away = sb("away", [P, T, P])
        masked = sb("masked", [P, 2, T, P])
        mx = sb("mx", [P, U])
        top = sb("top", [P, U])
        zneg = sb("zneg", [P, U])
        negm = sb("negm", [P, U])
        bias_hi = sb("bias_hi", [P, U])
        bias_lo = sb("bias_lo", [P, U])
        shift = sb("shift", [P, U])
        corr = sb("corr", [P, U])
        exp_hi = sb("exp_hi", [P, 2, GE])
        exp_lo = sb("exp_lo", [P, 2, GE])
        wT = sb("wT", [P, 2, GE])
        wgt = sb("wgt", [P, 2, GE])
        acc = sb("acc", [P, 3, ROW])
        part = {k: sb(f"part_{k}", [P, CH, ROW]) for k in SIDES}
        small = sb("small", [P, 8, CH])
        scale2 = sb("scale2", [P, 2, CH])
        agg = sb("agg", [P, CH, D])
        sq = sb("sq", [P, CH, D])

        bank = [pb(f"bank{i}", [P, 512]) for i in range(8)]
        tbank, qbank, obank = bank[0:2], bank[2:4], bank[4:6]

        sems = {}

        def sm(name):
            if name not in sems:
                sems[name] = sem(name)
            return sems[name]

        def pair(view, n, k):
            return view.unsqueeze(1).to_broadcast([view.shape[0], n, k])

        def spread(view, n, k):
            return view.unsqueeze(2).to_broadcast([view.shape[0], n, k])

        class Chain:

            def __init__(self, eng, name, base=0):
                self.eng, self.sem, self.n = eng, sm(name), base

            def __call__(self, ins):
                self.n = self.n + 1
                ins.then_inc(self.sem, 1)
                self.eng.wait_ge(self.sem, self.n)

        block = ctx.enter_context(nc.Block())

        @block.sync
        def _(sp):
            sp.wait_ge(sm("pads_set"), 3)
            for k, a in (("src", src), ("dst", dst)):
                sp.dma_start(ids[k][:, 0:T * GF], a[0:GE * GF].rearrange("(p c) -> p c", p=P)).then_inc(sm("ids_in"), 16)
                sp.dma_start(ids[k][0:LAST_P, T * GF:C], a[GE * GF:E].rearrange("(p c) -> p c", c=T)).then_inc(sm("ids_in"), 16)
            sp.dma_start(w_node[:, :], att_w[0:D].partition_broadcast(P)).then_inc(sm("weights_in"), 16)
            sp.dma_start(w_edge[:, :], att_w[D:2 * D].partition_broadcast(P)).then_inc(sm("weights_in"), 16)
            sp.dma_start(att_bias[:, :], att_b[0:1].partition_broadcast(P)).then_inc(sm("weights_in"), 16)
            sp.dma_start(w_proj[:, :], w1[:, :]).then_inc(sm("weights_in"), 16)
            sp.dma_start(out_bias[:, :], b1[:].partition_broadcast(P)).then_inc(sm("weights_in"), 16)
            sp.dma_start(nodes[:, 0:NB - 1, :], x[0:(NB - 1) * P, :].rearrange("(b p) f -> p b f", p=P)).then_inc(sm("nodes_in"), 16)
            sp.dma_start(nodes[0:LAST_NODES, NB - 1, :], x[(NB - 1) * P:N, :]).then_inc(sm("nodes_in"), 16)

            sp.wait_ge(sm("pad_rows_set"), 1)
            for k in SIDES:
                sp.dma_start(rows[k][E:E_PAD, :].rearrange("(p j) f -> p (j f)", p=PAD_ROWS // T),
                             ring[0:PAD_ROWS // T, 0, :, :].rearrange("p j f -> p (j f)")).then_inc(sm("pad_rows_out"), 16)
            sp.dma_start(table[NB * P:(NB + 1) * P, :], agg[:, 0, :]).then_inc(sm("pad_rows_out"), 16)

            full = edge_attr[0:GE * GF, :].rearrange("(p c) f -> p c f", p=P)
            with sp.Fori(0, GF // BR) as it:
                for k in range(BR):
                    sp.wait_ge(sm(f"dealt{k}"), it * (16 * 2 * T))
                    sp.dma_start(deal[:, k, :, 0:D], full[:, ds(it * (BR * T) + k * T, T), :]).then_inc(sm(f"edges_in{k}"), 16)
            sp.wait_ge(sm("dealt0"), (GF // BR) * 16 * 2 * T)
            sp.dma_start(deal[0:LAST_P, 0, :, 0:D],
                         edge_attr[GE * GF:E, :].rearrange("(p c) f -> p c f", c=T)).then_inc(sm("edges_in0"), 16)

            sp.wait_ge(sm("pad_rows_out"), 48)
            for k in range(BR):
                sp.wait_ge(sm(f"dealt{k}"), (GF // BR + (k == 0)) * 16 * 2 * T)

            def load(walk, side, i, off):
                n = i * U + off
                view = rows[walk][:, :].rearrange("(g p j) f -> g p (j f)", p=P, j=T)
                g = sp.value_load(group_i[side][0:1, ds(n, 1)], min_val=0, max_val=G - 1)
                sp.dma_start(ring[:, off % U, :, :].rearrange("p j f -> p (j f)"),
                             view[ds(g, 1), :, :].rearrange("a p f -> (a p) f")).then_inc(sm(f"{walk}_in{off % U}"), 16)

            def walk_loads(walk):
                for s in range(U):
                    if walk == "dst":
                        sp.wait_ge(sm("src_summed"), S)
                    load(walk, walk, 0, s)
                with sp.Fori(0, S // U - 1) as i:
                    for k in range(U):
                        sp.wait_ge(sm(f"{walk}_summed"), i * U + k + 1)
                        load(walk, walk, i, U + k)
                for s in range(S // U * U, S):
                    sp.wait_ge(sm(f"{walk}_summed"), s - U + 1)
                    load(walk, walk, 0, s)

            sp.wait_ge(sm("tables_ready"), 2)
            for walk in SIDES:
                walk_loads(walk)

            for k in SIDES:
                for r in range(3):
                    sp.wait_ge(sm(f"{k}_sums_out{r}"), 16 * ((S - r + 2) // 3))
            with sp.Fori(0, NCH) as it:
                sp.wait_ge(sm("chunk_used"), it)
                for k in SIDES:
                    for j in range(CH):
                        at = sp.value_load(last_i[k][0:1, ds(it * CH + j, 1)], min_val=0, max_val=S - 1)
                        sp.dma_start(part[k][:, j, :], sums[k][ds(at, 1), :, :].rearrange("a p f -> (a p) f")).then_inc(sm("chunk_in"), 16)
                sp.wait_ge(sm("projected"), it + 1)
                sp.dma_start(table[0:NB * P, :].rearrange("(b p) f -> p b f", p=P)[:, ds(it * CH, CH), :], agg[:, :, :]).then_inc(sm("table_out"), 16)

            def load_msg(i, off, wait):
                if wait:
                    sp.wait_ge(sm(f"msg_out{off % 3}"), (i * (U // 3) + off // 3 + 1) * 16)
                load("msg", "dst", i, off)

            def store_sums(i, off):
                sp.wait_ge(sm("msg_added"), i * U + off + 1)
                sp.dma_start(sums["msg"][ds(i * U + off, 1), :, 0:D].rearrange("a p f -> (a p) f"), acc[:, off % 3, 0:D]).then_inc(sm(f"msg_sums_out{off % 3}"), 16)

            def walk_step(i, off, wait):
                sp.wait_ge(sm("msg_summed"), i * U + (off - U + 1))
                load_msg(i, off, wait)
                store_sums(i, off - 3)

            for s in range(U):
                load_msg(0, s, True)
                if s >= 3:
                    store_sums(0, s - 3)
            with sp.Fori(1, GF // U) as i:
                for k in range(U):
                    walk_step(i, k, True)
            walk_step(0, GF, True)
            for s in range(GF + 1, GF + U):
                walk_step(0, s, False)
            with sp.Fori(GF // U + 1, S // U) as i:
                for k in range(U):
                    walk_step(i, k, False)
            for s in range(S // U * U, S):
                walk_step(0, s, False)
            for s in range(S - 3, S):
                store_sums(0, s)

            for r in range(3):
                sp.wait_ge(sm(f"msg_sums_out{r}"), 16 * ((S - r + 2) // 3))

            def chunk_in(it):
                sp.wait_ge(sm("chunk2_used"), it)
                for j in range(CH):
                    at = sp.value_load(last_i["dst"][0:1, ds(it * CH + j, 1)], min_val=0, max_val=S - 1)
                    sp.dma_start(part["src"][:, j, 0:D], sums["msg"][ds(at, 1), :, 0:D].rearrange("a p f -> (a p) f")).then_inc(sm("chunk2_in"), 16)
                sp.dma_start(part["dst"][:, :, 0:D], table[0:NB * P, :].rearrange("(b p) f -> p b f", p=P)[:, ds(it * CH, CH), :]).then_inc(sm("chunk2_in"), 16)

            with sp.Fori(0, NCH - 1) as it:
                chunk_in(it)
                sp.wait_ge(sm("result_ready"), it + 1)
                sp.dma_start(out[0:(NCH - 1) * CH * P, :].rearrange("(b p) f -> p b f", p=P)[:, ds(it * CH, CH), :], agg[:, :, :]).then_inc(sm("result_out"), 16)
            chunk_in(NCH - 1)
            sp.wait_ge(sm("result_ready"), NCH)
            b0 = (NCH - 1) * CH
            sp.dma_start(out[b0 * P:(NB - 1) * P, :].rearrange("(b p) f -> p b f", p=P), agg[:, 0:CH - 1, :]).then_inc(sm("result_out"), 16)
            sp.dma_start(out[(NB - 1) * P:N, :], agg[0:LAST_NODES, CH - 1, :]).then_inc(sm("result_out"), 16)
            sp.wait_ge(sm("result_out"), 16 * (NCH + 1))

        @block.gpsimd
        def _(pool):
            pool.iota(iota_f[:, :], [[1, P]], base=0, channel_multiplier=0, allow_small_or_imprecise_dtypes=True).then_inc(sm("iotas"), 1)
            pool.iota(iota_p[:, :], [[0, 1]], base=0, channel_multiplier=1, allow_small_or_imprecise_dtypes=True).then_inc(sm("iotas"), 1)
            pool.iota(iota_s[:, :], [[1, S]], base=0, channel_multiplier=0, allow_small_or_imprecise_dtypes=True).then_inc(sm("iotas"), 1)
            pool.memset(half_n[:, :], -0.5).then_inc(sm("half_set"), 1)

            pool.wait_ge(sm("half_set"), 1)
            pool.wait_ge(sm("deg_ready"), 1)
            pool.tensor_tensor(dinv[:, :], dinv[:, :], half_n[:, :], ALU.pow).then_inc(sm("dinv_ready"), 1)

            def deal_out(p, k, n):
                pool.wait_ge(sm("rows_made"), n + 1)
                pool.wait_ge(sm("places_made"), n + 1)
                pool.sem_inc(sm("deal_begun"), 1)
                for w, side in enumerate(SIDES):
                    for j in range(T):
                        pool.indirect_dma_start(
                            out=rows[side][:, :], out_offset=bass.IndirectOffsetOnAxis(ap=pos[0:p, k, w * T + j:w * T + j + 1], axis=0),
                            in_=deal[0:p, k, j, :], in_offset=None).then_inc(sm(f"dealt{k}"), 16)

            with pool.Fori(0, GF // BR) as it:
                for k in range(BR):
                    deal_out(P, k, it * BR + k)
            deal_out(LAST_P, 0, GF)

            for walk in SIDES:
                def store(i, off):
                    pool.wait_ge(sm(f"{walk}_added"), i * U + off + 1)
                    pool.dma_start(sums[walk][ds(i * U + off, 1), :, :].rearrange("a p f -> (a p) f"), acc[:, off % 3, :]).then_inc(sm(f"{walk}_sums_out{off % 3}"), 16)

                with pool.Fori(0, S // U) as i:
                    for k in range(U):
                        store(i, k)
                for s in range(S // U * U, S):
                    store(0, s)

            with pool.Fori(0, NCH) as it:
                pool.wait_ge(sm("var_ready"), it + 1)
                pool.tensor_tensor(small[:, 7, :], small[:, 6, :], half_n[:, 0:CH], ALU.pow).then_inc(sm("rstd_ready"), 1)

            pool.wait_ge(sm("table_out"), 16 * NCH)

            def gather(k, n):
                pool.wait_ge(sm("sources_ready"), n + 1)
                pool.sem_inc(sm("gather_begun"), 1)
                for j in range(T):
                    pool.indirect_dma_start(
                        out=deal[:, k, j, 0:D], out_offset=None, in_=table[:, :],
                        in_offset=bass.IndirectOffsetOnAxis(ap=pos[:, k, j:j + 1], axis=0)).then_inc(sm(f"gathered{k}"), 16)

            with pool.Fori(0, GF // BR) as it:
                for k in range(BR):
                    gather(k, it * BR + k)
            gather(0, GF)

            with pool.Fori(0, NCH) as it:
                pool.wait_ge(sm("var2_ready"), it + 1)
                pool.tensor_tensor(small[:, 7, :], small[:, 6, :], half_n[:, 0:CH], ALU.pow).then_inc(sm("rstd2_ready"), 1)

        @block.scalar
        def _(act):
            def exps(walk, i, off):
                n, b, c = i * U + off, off % 2, off % U
                act.wait_ge(sm(f"{walk}_bias_ready"), n + 1)
                if off >= 2:
                    act.wait_ge(sm(f"{walk}_weights_ready"), n - 1)
                act.activation(exp_hi[:, b, :], tbank[b][:, :], ACT.Exp, bias=bias_hi[:, c:c + 1])
                act.activation(exp_lo[:, b, :], tbank[b][:, :], ACT.Exp, bias=bias_lo[:, c:c + 1], scale=SLOPE)
                act.activation(corr[:, c:c + 1], shift[:, c:c + 1], ACT.Exp).then_inc(sm(f"{walk}_exps_ready"), 1)

            def copy_weights(walk, i, off):
                n, b = i * U + off, off % 2
                act.wait_ge(sm(f"{walk}_turned_back"), n + 1)
                if off >= 2:
                    act.wait_ge(sm(f"{walk}_summed"), n - 1)
                act.activation(wgt[:, b, :], qbank[b][:, :], ACT.Copy).then_inc(sm(f"{walk}_weights_out"), 1)

            for walk in SIDES:
                exps(walk, 0, 0)
                exps(walk, 0, 1)
                copy_weights(walk, 0, 0)
                with act.Fori(0, (S - 2) // U - 1) as i:
                    for k in range(2, U + 2):
                        exps(walk, i, k)
                        copy_weights(walk, i, k - 1)
                for s in range(S - U, S):
                    exps(walk, 0, s)
                    copy_weights(walk, 0, s - 1)
                copy_weights(walk, 0, S - 1)

            with act.Fori(0, NCH) as it:
                act.wait_ge(sm("merge_ready"), it + 1)
                act.activation(scale2[:, :, :], scale2[:, :, :], ACT.Exp).then_inc(sm("merge_exp"), 1)
                act.wait_ge(sm("agg_ready"), it + 1)
                act.activation(agg[:, :, :], agg[:, :, :], ACT.Gelu).then_inc(sm("gelu_done"), 1)

            by_group = {k: rows[k][:, :].rearrange("(g p j) f -> g p j f", p=P, j=T) for k in ("dst", "msg")}

            def numbers_in(it, off):
                act.dma_start(deal[:, off % BR, :, D:ROW],
                              by_group["dst"][ds(it * BR + off, 1), :, :, D:ROW].rearrange("a p j f -> (a p) j f")).then_inc(sm(f"numbers_in{off % BR}"), 16)

            def sources(it, off):
                act.wait_ge(sm(f"numbers_in{off % BR}"), (it + off // BR + 1) * 16)
                act.activation(pos[:, off % BR, 0:T], deal[:, off % BR, :, SOURCE], ACT.Copy).then_inc(sm("sources_ready"), 1)

            def message_out(it, off):
                act.wait_ge(sm(f"gathered{off % BR}"), (it + off // BR + 1) * (16 * T))
                act.dma_start(by_group["msg"][ds(it * BR + off, 1), :, :, :].rearrange("a p j f -> (a p) (j f)"),
                              deal[:, off % BR, :, :].rearrange("p j f -> p (j f)")).then_inc(sm(f"msg_out{off % BR}"), 16)

            def message(it, off, numbers, source):
                if numbers:
                    act.wait_ge(sm(f"msg_out{(off - 1) % BR}"), (it + (off - 1) // BR + 1) * 16)
                    numbers_in(it, off + 2)
                if source:
                    sources(it, off + 1)
                message_out(it, off)

            act.wait_ge(sm("table_out"), 16 * NCH)
            numbers_in(0, 0)
            numbers_in(0, 1)
            sources(0, 0)
            with act.Fori(0, GF // BR - 1) as it:
                for k in range(BR):
                    message(it, k, True, True)
            for g in range(GF - BR, G):
                message(0, g, g + 2 < G, g + 1 < G)

        @block.tensor
        def _(pe):
            pe.wait_ge(sm("constants_ready"), 1)

            def count_group(i, off, first=False, last=False):
                b = off % 2
                pe.wait_ge(sm("hot_ready"), i * 2 + off + 1)
                for w, k in enumerate(SIDES):
                    pe.matmul(bank[w][:, 0:T * NB], identb[:, :], hot[k][:, b, :, :].rearrange("p j b -> p (j b)"), start=first, stop=last)
                for j in range(T):
                    ins = pe.matmul(bank[2][0:NB, 0:P], hot["dst"][:, b, j, :], hot_low[:, b, j, :],
                                    start=first and j == 0, stop=last and j == T - 1)
                ins.then_inc(sm("hot_used"), 1)

            count_group(0, 0, first=True)
            count_group(0, 1)
            with pe.Fori(1, GF // 2) as i:
                for b in range(2):
                    count_group(i, b)
            count_group(0, GF, last=True)

            pe.wait_ge(sm("counts_ready"), 1)
            for w, k in enumerate(SIDES):
                ins = pe.matmul(bank[3][0:NB, w:w + 1], count[k][:, :], ones[:, 0:1], start=True, stop=True)
            ins.then_inc(sm("totals_ready"), 1)
            pe.wait_ge(sm("totals_copied"), 1)
            for w, k in enumerate(SIDES):
                pe.matmul(bank[4 + w][:, 0:NB], below[:, :], count[k][:, :], start=True, stop=False)
                pe.matmul(bank[4 + w][:, 0:NB], total_b[k][0:NB, :], below[0:NB, 0:NB], start=False, stop=True)
                ins = pe.matmul(bank[3][0:NB, 4 + w:5 + w], upto[0:NB, 0:NB], total[k][0:NB, :], start=True, stop=True)
            ins.then_inc(sm("starts_ready"), 1)

            pe.wait_ge(sm("deg_copied"), 1)
            pe.transpose(bank[0][:, 0:NB], degT[0:NB, :], ident[0:NB, 0:NB]).then_inc(sm("deg_turned"), 1)
            pe.wait_ge(sm("node_scores_ready"), NCH)
            pe.transpose(bank[1][0:NB, 0:P], s_node[:, :], ident[:, :]).then_inc(sm("node_scores_turned"), 1)

            pe.wait_ge(sm("done_ready"), 1)
            for w, k in enumerate(SIDES):
                pe.matmul(bank[6 + w][:, 0:S], ones[0:NB, :], done[k][0:NB, :], start=True, stop=True)
                ins = pe.matmul(bank[2][0:1, w * P:w * P + NB], last[k][0:NB, :], ident[0:NB, 0:NB], start=True, stop=True)
            ins.then_inc(sm("steps_ready"), 1)
            pe.wait_ge(sm("step_blocks_ready"), 1)
            for w, k in enumerate(SIDES):
                ins = pe.matmul(bank[4 + w][:, 0:S], s_nodeT[0:NB, :], done[k][0:NB, :], start=True, stop=True)
            ins.then_inc(sm("step_scores_ready"), 1)

            def turn(walk, i, off):
                n, b = i * U + off, off % 2
                pe.wait_ge(sm(f"{walk}_scores_ready"), n + 1)
                if off >= 2:
                    pe.wait_ge(sm(f"{walk}_exps_ready"), n - 1)
                for j in range(T):
                    ins = pe.transpose(tbank[b][:, j * P:(j + 1) * P], masked[:, b, j, :], ident[:, :])
                ins.then_inc(sm(f"{walk}_turned"), 1)

            def turn_back(walk, i, off):
                n, b = i * U + off, off % 2
                pe.wait_ge(sm(f"{walk}_weights_ready"), n + 1)
                if off >= 2:
                    pe.wait_ge(sm(f"{walk}_weights_out"), n - 1)
                for j in range(T):
                    ins = pe.transpose(qbank[b][:, j * P:(j + 1) * P], wT[:, b, j * P:(j + 1) * P], ident[:, :])
                ins.then_inc(sm(f"{walk}_turned_back"), 1)

            def sum_rows(walk, i, off):
                n, b = i * U + off, off % 2
                pe.wait_ge(sm(f"{walk}_weights_out"), n + 1)
                if off >= 2:
                    pe.wait_ge(sm(f"{walk}_added"), n - 1)
                for j in range(T):
                    ins = pe.matmul(obank[b][:, 0:ROW], wgt[:, b, j * P:(j + 1) * P], ring[:, off % U, j, :], start=j == 0, stop=j == T - 1)
                ins.then_inc(sm(f"{walk}_summed"), 1)

            for walk in SIDES:
                if walk == "dst":
                    pe.wait_ge(sm("src_added"), S)
                turn(walk, 0, 0)
                turn(walk, 0, 1)
                turn_back(walk, 0, 0)
                turn(walk, 0, 2)
                turn_back(walk, 0, 1)
                sum_rows(walk, 0, 0)
                with pe.Fori(0, (S - 2) // U - 1) as i:
                    for k in range(2, U + 2):
                        turn(walk, i, k + 1)
                        turn_back(walk, i, k)
                        sum_rows(walk, i, k - 1)
                for s in range(S - U, S):
                    if s + 1 < S:
                        turn(walk, 0, s + 1)
                    turn_back(walk, 0, s)
                    sum_rows(walk, 0, s - 1)
                sum_rows(walk, 0, S - 1)

            with pe.Fori(0, NCH) as it:
                pe.wait_ge(sm("first_result_ready"), it + 1)
                for j in range(CH):
                    ins = pe.transpose(tbank[j // T][:, j % T * P:(j % T + 1) * P], sq[:, j, :], ident[:, :])
                ins.then_inc(sm("result_turned"), 1)
                pe.wait_ge(sm("result_copied"), it + 1)
                for j in range(CH):
                    ins = pe.matmul(qbank[j // T][:, j % T * P:(j % T + 1) * P], wT[:, j // T, j % T * P:(j % T + 1) * P], w_proj[:, :], start=True, stop=True)
                ins.then_inc(sm("projection_ready"), 1)

            def sum_messages(i, off):
                n, b = i * U + off, off % 2
                pe.wait_ge(sm("msg_hot"), n + 1)
                if off >= 2:
                    pe.wait_ge(sm("msg_added"), n - 1)
                for j in range(T):
                    ins = pe.matmul(obank[b][:, 0:D], masked[:, b, j, :], ring[:, off % U, j, 0:D], start=j == 0, stop=j == T - 1)
                ins.then_inc(sm("msg_summed"), 1)

            sum_messages(0, 0)
            sum_messages(0, 1)
            with pe.Fori(0, (S - 2) // U) as i:
                for k in range(2, U + 2):
                    sum_messages(i, k)

        @block.vector
        def _(dve):
            pads = slice(P // 2, P)
            for k in SIDES:
                dve.memset(ids[k][pads, T * GF:C], NO_NODE).then_inc(sm("pads_set"), 1)
            dve.memset(nodes[pads, NB - 1, :], 0.0).then_inc(sm("pads_set"), 1)
            c = Chain(dve, "setup")
            c(dve.memset(ring[:, 0, :, :], 0.0))
            dve.memset(agg[:, 0, :], 0.0)
            dve.memset(ring[:, 0, :, SOURCE:TARGET + 1], float(NO_NODE)).then_inc(sm("pad_rows_set"), 1)
            dve.memset(deal[:, :, :, ONE:ONE + 1], 1.0)
            dve.memset(acc[:, :, :], 0.0)
            dve.memset(top[:, :], 0.0)
            dve.memset(negm[:, :], 0.0)
            for k in SIDES:
                dve.memset(keep[k][:, 0:1], 0.0)
            dve.memset(ones[:, :], 1.0)
            dve.wait_ge(sm("iotas"), 3)
            for m, op in ((ident, ALU.is_equal), (identb, ALU.is_equal), (below, ALU.is_gt), (upto, ALU.is_ge)):
                ins = dve.tensor_scalar(m[:, :], iota_f[:, :], iota_p[:, 0:1], None, op)
            ins.then_inc(sm("constants_ready"), 1)

            dve.wait_ge(sm("ids_in"), 64)
            for k in SIDES:
                c(dve.tensor_scalar(blk[k][:, :].bitcast(I32), ids[k][:, :], P.bit_length() - 1, None, ALU.arith_shift_right))
                c(dve.tensor_copy(blk[k][:, :], blk[k][:, :].bitcast(I32)))

            def hot_group(i, off):
                n, b = i * 2 + off, off % 2
                if off >= 2:
                    dve.wait_ge(sm("hot_used"), n - 1)
                cols = ds(n * T, T)
                dve.scalar_tensor_tensor(low4[:, b, :], blk["dst"][:, cols], float(-P), ids["dst"][:, cols], ALU.mult, ALU.add).then_inc(sm("low_ready"), 1)
                for k in SIDES:
                    dve.tensor_tensor(hot[k][:, b, :, :], pair(iota_f[:, 0:NB], T, NB), spread(blk[k][:, cols], T, NB), ALU.is_equal)
                dve.wait_ge(sm("low_ready"), n + 1)
                dve.tensor_tensor(hot_low[:, b, :, :], pair(iota_f[:, :], T, P), spread(low4[:, b, :], T, P), ALU.is_equal).then_inc(sm("hot_ready"), 1)

            hot_group(0, 0)
            hot_group(0, 1)
            with dve.Fori(0, GF // 2 - 1) as i:
                for b in range(2, 4):
                    hot_group(i, b)
            hot_group(0, GF)

            dve.wait_ge(sm("weights_in"), 80)
            dve.wait_ge(sm("nodes_in"), 32)
            with dve.Fori(0, NCH) as it:
                chunk = ds(it * CH, CH)
                c2 = Chain(dve, "node_score", it * 2)
                c2(dve.tensor_tensor(sq[:, :, :], nodes[:, chunk, :], pair(w_node[:, :], CH, D), ALU.mult))
                c2(dve.reduce_sum(small[:, 0, :], sq[:, :, :], AX.X))
                dve.tensor_scalar(s_node[:, chunk], small[:, 0, :], att_bias[:, 0:1], None, ALU.add).then_inc(sm("node_scores_ready"), 1)

            dve.wait_ge(sm("hot_used"), G)
            dve.tensor_copy(degT[0:NB, :], bank[2][0:NB, 0:P]).then_inc(sm("deg_copied"), 1)
            for w, k in enumerate(SIDES):
                ins = dve.reduce_sum(count[k][:, :], bank[w][:, 0:T * NB].rearrange("p (j b) -> p b j", b=NB), AX.X)
            ins.then_inc(sm("counts_ready"), 1)
            dve.wait_ge(sm("totals_ready"), 1)
            for w, k in enumerate(SIDES):
                c(dve.tensor_copy(total[k][0:NB, :], bank[3][0:NB, w:w + 1]))
                ins = dve.tensor_scalar(total_b[k][0:NB, :], ones[0:NB, :], total[k][0:NB, 0:1], None, ALU.mult)
            ins.then_inc(sm("totals_copied"), 1)
            dve.wait_ge(sm("starts_ready"), 1)
            for w, k in enumerate(SIDES):
                dve.tensor_copy(nextpos[k][:, :], bank[4 + w][:, 0:NB])
                c(dve.tensor_copy(cumi[k][0:NB, :], bank[3][0:NB, 4 + w:5 + w]))
                c(dve.tensor_scalar(cumi[k][0:NB, :], cumi[k][0:NB, :], GE.bit_length() - 1, None, ALU.arith_shift_right))
                c(dve.tensor_copy(last[k][0:NB, :], cumi[k][0:NB, :]))
                c(dve.tensor_scalar(last[k][0:NB, :], last[k][0:NB, :], float(G - 1), iota_p[0:NB, 0:1], ALU.min, ALU.add))
                ins = dve.tensor_scalar(done[k][0:NB, :], iota_s[0:NB, :], last[k][0:NB, 0:1], None, ALU.is_gt)
            ins.then_inc(sm("done_ready"), 1)
            dve.wait_ge(sm("deg_turned"), 1)
            dve.tensor_scalar(dinv[:, :], bank[0][:, 0:NB], 1.0, None, ALU.add).then_inc(sm("deg_ready"), 1)
            dve.wait_ge(sm("node_scores_turned"), 1)
            dve.tensor_copy(s_nodeT[0:NB, :], bank[1][0:NB, 0:P])
            dve.wait_ge(sm("steps_ready"), 1)
            for w, k in enumerate(SIDES):
                c(dve.tensor_scalar(first_node[k][:, :], bank[6 + w][:, 0:S], float(P), None, ALU.mult))
                dve.tensor_copy(last_i[k][0:1, :], bank[2][0:1, w * P:w * P + NB])
                c(dve.tensor_tensor(keep[k][:, 1:S], first_node[k][:, 1:S], first_node[k][:, 0:S - 1], ALU.is_equal))
                dve.tensor_scalar(drop[k][:, :], keep[k][:, :], -1.0, BIG, ALU.add, ALU.mult)
                dve.scalar_tensor_tensor(group_i[k][0:1, :], first_node[k][0:1, :], -1.0 / P, iota_s[0:1, :], ALU.mult, ALU.add).then_inc(sm("tables_ready"), 1)
                c(dve.tensor_scalar(low4[0:NB, 0, w:w + 1], iota_p[0:NB, :], float(P), None, ALU.mult))
                ins = dve.tensor_scalar(done[k][0:NB, :], first_node[k][0:NB, :], low4[0:NB, 0, w:w + 1], None, ALU.is_equal)
            ins.then_inc(sm("step_blocks_ready"), 1)
            dve.wait_ge(sm("step_scores_ready"), 1)
            for w, k in enumerate(SIDES):
                c(dve.tensor_copy(s_step[k][:, :], bank[4 + w][:, 0:S]))

            def deal_rows(p, it, off):
                k, n = off % BR, it * BR + off
                cols = ds(n * T, T)
                dve.wait_ge(sm(f"edges_in{k}"), (it + off // BR + 1) * 16)
                dve.tensor_tensor(prod[0:p, :, :], deal[0:p, k, :, 0:D], pair(w_edge[0:p, :], T, D), ALU.mult).then_inc(sm("products_ready"), 1)
                dve.tensor_copy(deal[0:p, k, :, SOURCE:SOURCE + 1], ids["src"][0:p, cols].unsqueeze(2))
                dve.tensor_copy(deal[0:p, k, :, TARGET:TARGET + 1], ids["dst"][0:p, cols].unsqueeze(2))
                dve.wait_ge(sm("products_ready"), n + 1)
                dve.reduce_sum(deal[0:p, k, :, SCORE:SCORE + 1], prod[0:p, :, :], AX.X).then_inc(sm("rows_made"), 1)
                for j in range(T):
                    for w, side in enumerate(SIDES):
                        col = blk[side][:, ds(n * T + j, 1)]
                        if off or j:
                            dve.wait_ge(sm(f"counted_{side}"), n * T + j)
                        dve.scalar_tensor_tensor(junk[:, w, :], iota_f[:, 0:NB], col, nextpos[side][:, :], ALU.is_equal, ALU.mult, accum_out=posf[:, w * T + j:w * T + j + 1]).then_inc(sm("placed"), 1)
                        dve.scalar_tensor_tensor(nextpos[side][:, :], iota_f[:, 0:NB], col, nextpos[side][:, :], ALU.is_equal, ALU.add).then_inc(sm(f"counted_{side}"), 1)
                dve.wait_ge(sm("placed"), n * (2 * T) + 2 * T)
                dve.tensor_copy(pos[:, k, :], posf[:, :]).then_inc(sm("places_made"), 1)

            with dve.Fori(0, GF // BR) as it:
                for k in range(BR):
                    deal_rows(P, it, k)
            deal_rows(LAST_P, 0, GF)

            def scores(walk, i, off):
                n, b, k = i * U + off, off % 2, off % U
                col = SOURCE if walk == "src" else TARGET
                dve.wait_ge(sm(f"{walk}_in{k}"), (i + off // U + 1) * 16)
                dve.tensor_scalar(local[:, b, :], ring[:, k, :, col], first_node[walk][:, ds(n, 1)], None, ALU.subtract).then_inc(sm(f"{walk}_local"), 1)
                dve.wait_ge(sm(f"{walk}_local"), n + 1)
                dve.tensor_tensor(away[:, :, :], pair(iota_f[:, :], T, P), spread(local[:, b, :], T, P), ALU.not_equal).then_inc(sm(f"{walk}_away"), 1)
                if off >= 2:
                    dve.wait_ge(sm(f"{walk}_turned"), n - 1)
                dve.wait_ge(sm(f"{walk}_away"), n + 1)
                dve.scalar_tensor_tensor(masked[:, b, :, :], away[:, :, :], -BIG, spread(ring[:, k, :, SCORE], T, P), ALU.mult, ALU.add).then_inc(sm(f"{walk}_scores_ready"), 1)

            def maxima(walk, i, off):
                n, b, k, o = i * U + off, off % 2, off % U, (off - 1) % U
                now, old = slice(k, k + 1), slice(o, o + 1)
                dropped, node = drop[walk][:, ds(n, 1)], s_step[walk][:, ds(n, 1)]
                c = Chain(dve, f"{walk}_maxima", n * 4)
                dve.tensor_scalar(zneg[:, now], top[:, old], dropped, None, ALU.add)
                dve.wait_ge(sm(f"{walk}_turned"), n + 1)
                c(dve.reduce_max(mx[:, now], tbank[b][:, :], AX.X))
                c(dve.tensor_scalar(top[:, now], mx[:, now], -1e-10 * BIG, zneg[:, now], ALU.max, ALU.max))
                c(dve.tensor_scalar(zneg[:, now], top[:, now], node, -1.0, ALU.add, ALU.mult))
                c(dve.scalar_tensor_tensor(negm[:, now], zneg[:, now], SLOPE, zneg[:, now], ALU.mult, ALU.min))
                dve.tensor_tensor(bias_hi[:, now], node, negm[:, now], ALU.add)
                dve.scalar_tensor_tensor(bias_lo[:, now], node, SLOPE, negm[:, now], ALU.mult, ALU.add)
                dve.tensor_scalar(shift[:, now], negm[:, now], negm[:, old], dropped, ALU.subtract, ALU.min).then_inc(sm(f"{walk}_bias_ready"), 1)

            def weights(walk, i, off):
                n, b = i * U + off, off % 2
                dve.wait_ge(sm(f"{walk}_exps_ready"), n + 1)
                if off >= 2:
                    dve.wait_ge(sm(f"{walk}_turned_back"), n - 1)
                dve.tensor_tensor(wT[:, b, :], exp_hi[:, b, :], exp_lo[:, b, :], ALU.max).then_inc(sm(f"{walk}_weights_ready"), 1)

            def add(walk, i, off):
                n, b, k, r = i * U + off, off % 2, off % U, off % 3
                dve.wait_ge(sm(f"{walk}_summed"), n + 1)
                dve.wait_ge(sm(f"{walk}_sums_out{r}"), (i * (U // 3) + off // 3) * 16)
                if off:
                    dve.wait_ge(sm(f"{walk}_added"), n)
                dve.scalar_tensor_tensor(acc[:, r, :], acc[:, (off - 1) % 3, :], corr[:, k:k + 1], obank[b][:, 0:ROW], ALU.mult, ALU.add).then_inc(sm(f"{walk}_rescaled"), 1)
                dve.wait_ge(sm(f"{walk}_rescaled"), n + 1)
                dve.tensor_copy(acc[:, r, SCORE:SCORE + 1], negm[:, k:k + 1]).then_inc(sm(f"{walk}_added"), 1)

            for walk in SIDES:
                if walk == "dst":
                    for r in range(3):
                        dve.wait_ge(sm(f"src_sums_out{r}"), 16 * ((S - r + 2) // 3))
                scores(walk, 0, 0)
                for s in range(2):
                    maxima(walk, 0, s)
                    scores(walk, 0, s + 1)
                    weights(walk, 0, s)
                with dve.Fori(0, (S - 2) // U - 1) as i:
                    for k in range(2, U + 2):
                        maxima(walk, i, k)
                        scores(walk, i, k + 1)
                        weights(walk, i, k)
                        add(walk, i, k - 2)
                for s in range(S - U, S):
                    maxima(walk, 0, s)
                    if s + 1 < S:
                        scores(walk, 0, s + 1)
                    weights(walk, 0, s)
                    add(walk, 0, s - 2)
                for s in range(S - 2, S):
                    add(walk, 0, s)

            with dve.Fori(0, NCH) as it:
                chunk = ds(it * CH, CH)
                h = nodes[:, chunk, :]
                c = Chain(dve, "first_nodes", it * 14)
                dve.wait_ge(sm("chunk_in"), it * (32 * CH) + 32 * CH)
                c(dve.tensor_tensor(small[:, 0, :], part["src"][:, :, SCORE], part["dst"][:, :, SCORE], ALU.min))
                for w, k in enumerate(SIDES):
                    ins = dve.tensor_tensor(scale2[:, w, :], small[:, 0, :], part[k][:, :, SCORE], ALU.subtract)
                ins.then_inc(sm("merge_ready"), 1)
                dve.wait_ge(sm("merge_exp"), it + 1)
                for w, k in enumerate(SIDES):
                    c(dve.tensor_tensor(part[k][:, :, :], part[k][:, :, :], spread(scale2[:, w, :], CH, ROW), ALU.mult))
                c(dve.tensor_tensor(part["src"][:, :, :], part["src"][:, :, :], part["dst"][:, :, :], ALU.add))
                weight = part["src"][:, :, ONE]
                c(dve.scalar_tensor_tensor(small[:, 1, :], weight, 0.0, weight, ALU.is_equal, ALU.add))
                c(dve.reciprocal(small[:, 2, :], small[:, 1, :]))
                c(dve.tensor_scalar(small[:, 3, :], weight, 0.0, 1.0, ALU.is_equal, ALU.add))
                dve.wait_ge(sm("table_out"), it * 16)
                c(dve.tensor_tensor(agg[:, :, :], part["src"][:, :, 0:D], spread(small[:, 2, :], CH, D), ALU.mult))
                dve.tensor_tensor(sq[:, :, :], h, spread(small[:, 3, :], CH, D), ALU.mult).then_inc(sm("agg_ready"), 1)
                dve.wait_ge(sm("gelu_done"), it + 1)
                c(dve.tensor_tensor(sq[:, :, :], sq[:, :, :], agg[:, :, :], ALU.add))
                c(dve.reduce_sum(small[:, 4, :], sq[:, :, :], AX.X))
                c(dve.tensor_scalar(small[:, 4, :], small[:, 4, :], -1.0 / D, None, ALU.mult))
                c(dve.tensor_tensor(sq[:, :, :], sq[:, :, :], spread(small[:, 4, :], CH, D), ALU.add))
                c(dve.tensor_tensor(agg[:, :, :], sq[:, :, :], sq[:, :, :], ALU.mult))
                c(dve.reduce_sum(small[:, 5, :], agg[:, :, :], AX.X))
                dve.tensor_scalar(small[:, 6, :], small[:, 5, :], 1.0 / D, EPS, ALU.mult, ALU.add).then_inc(sm("var_ready"), 1)
                dve.wait_ge(sm("rstd_ready"), it + 1)
                dve.tensor_tensor(sq[:, :, :], sq[:, :, :], spread(small[:, 7, :], CH, D), ALU.mult).then_inc(sm("first_result_ready"), 1)
                dve.wait_ge(sm("first_result_ready"), it + 1)
                dve.tensor_scalar(h, sq[:, :, :], 1.0, None, ALU.mult)
                dve.wait_ge(sm("result_turned"), it + 1)
                dve.tensor_copy(wT[:, 0, :], tbank[0][:, :])
                dve.tensor_copy(wT[:, 1, 0:(CH - T) * P], tbank[1][:, 0:(CH - T) * P]).then_inc(sm("result_copied"), 1)
                dve.wait_ge(sm("projection_ready"), it + 1)
                dve.tensor_tensor(agg[:, 0:T, :], qbank[0][:, :].rearrange("p (j f) -> p j f", f=D), spread(dinv[:, ds(it * CH, T)], T, D), ALU.mult)
                dve.tensor_tensor(agg[:, T:CH, :], qbank[1][:, 0:(CH - T) * P].rearrange("p (j f) -> p j f", f=D),
                                  spread(dinv[:, ds(it * CH + T, CH - T)], CH - T, D), ALU.mult).then_inc(sm("projected"), 1)
                dve.wait_ge(sm("projected"), it + 1)
                dve.sem_inc(sm("chunk_used"), 1)

            def hot_targets(i, off):
                n, b, k = i * U + off, off % 2, off % U
                dve.wait_ge(sm(f"msg_in{k}"), (i + off // U + 1) * 16)
                dve.tensor_scalar(local[:, b, :], ring[:, k, :, TARGET], first_node["dst"][:, ds(n, 1)], None, ALU.subtract).then_inc(sm("msg_local"), 1)
                if off >= 2:
                    dve.wait_ge(sm("msg_summed"), n - 1)
                dve.wait_ge(sm("msg_local"), n + 1)
                dve.tensor_tensor(masked[:, b, :, :], pair(iota_f[:, :], T, P), spread(local[:, b, :], T, P), ALU.is_equal).then_inc(sm("msg_hot"), 1)

            def add_messages(i, off):
                n, b, r = i * U + off, off % 2, off % 3
                dve.wait_ge(sm("msg_summed"), n + 1)
                dve.wait_ge(sm(f"msg_sums_out{r}"), (i * (U // 3) + off // 3) * 16)
                if off:
                    dve.wait_ge(sm("msg_added"), n)
                dve.scalar_tensor_tensor(acc[:, r, 0:D], acc[:, (off - 1) % 3, 0:D], keep["dst"][:, ds(n, 1)], obank[b][:, 0:D], ALU.mult, ALU.add).then_inc(sm("msg_added"), 1)

            for r in range(3):
                dve.wait_ge(sm(f"dst_sums_out{r}"), 16 * ((S - r + 2) // 3))
            hot_targets(0, 0)
            hot_targets(0, 1)
            add_messages(0, 0)
            with dve.Fori(0, (S - 2) // U) as i:
                for k in range(2, U + 2):
                    hot_targets(i, k)
                    add_messages(i, k - 1)
            add_messages(0, S - 1)

            with dve.Fori(0, NCH) as it:
                chunk = ds(it * CH, CH)
                c = Chain(dve, "second_nodes", it * 9)
                dve.wait_ge(sm("chunk2_in"), it * (16 * (CH + 1)) + 16 * (CH + 1))
                c(dve.tensor_tensor(sq[:, :, :], part["src"][:, :, 0:D], part["dst"][:, :, 0:D], ALU.add))
                c(dve.tensor_tensor(sq[:, :, :], sq[:, :, :], spread(dinv[:, chunk], CH, D), ALU.mult))
                c(dve.tensor_tensor(sq[:, :, :], sq[:, :, :], pair(out_bias[:, :], CH, D), ALU.add))
                c(dve.scalar_tensor_tensor(sq[:, :, :], sq[:, :, :], 0.0, nodes[:, chunk, :], ALU.max, ALU.add))
                c(dve.reduce_sum(small[:, 4, :], sq[:, :, :], AX.X))
                c(dve.tensor_scalar(small[:, 4, :], small[:, 4, :], -1.0 / D, None, ALU.mult))
                c(dve.tensor_tensor(sq[:, :, :], sq[:, :, :], spread(small[:, 4, :], CH, D), ALU.add))
                dve.wait_ge(sm("result_out"), it * 16)
                c(dve.tensor_tensor(agg[:, :, :], sq[:, :, :], sq[:, :, :], ALU.mult))
                c(dve.reduce_sum(small[:, 5, :], agg[:, :, :], AX.X))
                dve.tensor_scalar(small[:, 6, :], small[:, 5, :], 1.0 / D, EPS, ALU.mult, ALU.add).then_inc(sm("var2_ready"), 1)
                dve.wait_ge(sm("rstd2_ready"), it + 1)
                dve.tensor_tensor(agg[:, :, :], sq[:, :, :], spread(small[:, 7, :], CH, D), ALU.mult).then_inc(sm("result_ready"), 1)
                dve.wait_ge(sm("result_ready"), it + 1)
                dve.sem_inc(sm("chunk2_used"), 1)

    return nc


_INS = ["x", "src", "dst", "edge_attr_128", "L0_gnn_W_att_w", "L0_gnn_W_att_b", "L1_gnn_W", "L1_gnn_b"]


def kernel(**inputs):
    import numpy as _np
    import concourse.bacc as _bacc
    from concourse import mybir as _mybir
    from concourse.bass_utils import run_bass_kernel_spmd as _run

    nc = _bacc.Bacc("TRN2", target_bir_lowering=False, num_devices=1)
    arrays, args = {}, []
    for name in _INS:
        a = _np.ascontiguousarray(inputs[name])
        arrays[f"in_{name}"] = a
        args.append(nc.dram_tensor(f"in_{name}", a.shape, _mybir.dt.from_np(a.dtype), kind="ExternalInput").ap())
    args.append(nc.dram_tensor("out_nodes", (N, D), F32, kind="ExternalOutput").ap())
    resnorm_gnn_kernel(nc, *args)
    return _run(nc, [arrays], core_ids=[0]).results[0]["out_nodes"]
```

```python
import concourse.bass as bass
from concourse import mybir
from contextlib import ExitStack

F32, BF16, I32 = mybir.dt.float32, mybir.dt.bfloat16, mybir.dt.int32
ALU = mybir.AluOpType
ACT = mybir.ActivationFunctionType
AX = mybir.AxisListType

P = 128
N, E, D = 12500, 200000, 128
NB = -(-N // P)
LAST_NODES = N - (NB - 1) * P
T = 4
GE = P * T
G = -(-E // GE)
E_PAD = G * GE
AGAIN = E_PAD - E
AGAIN_P = AGAIN // T
S = G + NB - 1
ROW = D + 4
ONE, SCORE, SOURCE = D, D + 1, D + 2
LEAST, DEGREE = D + 1, D + 2
NO_NODE = NB * P
BIG = 1e30
FLOOR = -1e20
SLOPE, EPS = 0.2, 1e-5
LIFT = 2.0 ** 20
U = 6
BODY = {"dst": U, "src": 2 * U}
BACK = {"dst": 1, "src": 2}
LAG = 5
CH = 7
NCH = NB // CH
R = 98
Q = -(-G // R)
OP, OC = 125, 1600
LOG_P, LOG_GE = P.bit_length() - 1, GE.bit_length() - 1
assert AGAIN_P * T == AGAIN and NB % CH == 0 and OP * OC == E and E < LIFT and NB < R + 1
assert (S - 2) % U == 0 and U % 2 == 0 and U % 3 == 0 and (G - 2 * U) % U == 1 and (S - G + 1) % U == 2


def resnorm_gnn_kernel(nc, x, src, dst, edge_attr, att_w, att_b, w1, b1, out):
    ctx = ExitStack()
    with ctx:
        def sb(name, shape, dt=F32):
            return ctx.enter_context(nc.sbuf_tensor(name, shape, dt))

        def pb(name, shape, dt=F32):
            return ctx.enter_context(nc.psum_tensor(name, shape, dt))

        def dram(name, shape, dt=F32):
            return nc.dram_tensor(name, shape, dt)

        ds = bass.ds
        SIDES = ("src", "dst")
        BEFORE = {"dst": 0, "src": S}
        given = {"src": src, "dst": dst, "edges": edge_attr}

        ordered = {"src": dram("ordered_src", (E, 1), I32), "dst": dram("ordered_dst", (E, 1), I32),
                   "edges": dram("ordered_edges", (E, D))}
        by_source = dram("rows_by_source", (E_PAD, ROW))
        notes = dram("notes_by_target", (E_PAD, 2))
        messages = dram("messages", (E_PAD, D))
        sums = {k: dram(f"sums_{k}", (S, P, ROW)) for k in ("src", "dst", "msg")}
        table = dram("projected_nodes", ((NB + 1) * P, D))

        iota_f = sb("iota_f", [P, P])
        iota_p = sb("iota_p", [P, 1])
        iota_s = sb("iota_s", [P, S])
        iota_n = sb("iota_n", [P, P, T], BF16)
        iota_b = sb("iota_b", [P, NB, T], BF16)
        ident = sb("ident", [P, P])
        lifted = sb("lifted", [P, P], BF16)
        lower = sb("lower", [P, P], BF16)
        rest = sb("rest", [P, P], BF16)
        below = sb("below", [P, P])
        ones = sb("ones", [P, 512])
        onesb = sb("onesb", [P, P], BF16)
        counts = sb("counts", [P, 2], BF16)
        half_n = sb("half_n", [P, CH])
        minus_lift = sb("minus_lift", [P, 1])
        spare = sb("spare", [P, T])
        nodes = sb("nodes", [P, NB, D])
        w_node = sb("w_node", [P, D])
        w_edge = sb("w_edge", [P, D])
        att_bias = sb("att_bias", [P, 1])
        w_proj = sb("w_proj", [P, D])
        out_bias = sb("out_bias", [P, D])
        here = sb("here", [P, OC], I32)
        there = sb("there", [P, OC], I32)
        unsorted = sb("unsorted", [P, 1])
        flag_i = sb("flag_i", [1, 1], I32)
        lying = {k: sb(f"lying_{k}", [R, Q, GE], I32) for k in SIDES}
        ids = {k: sb(f"ids_{k}", [P, Q * R * T]) for k in SIDES}
        blk = sb("blk", [P, Q * R * T], BF16)
        hot = sb("hot", [P, 3, NB, T], BF16)
        total = sb("total", [P, NB, T])
        upto = sb("upto", [P, NB, T])
        ends_i = sb("ends_i", [R, Q], I32)
        ends = sb("ends", [R, Q])
        passed = sb("passed", [R, Q, NB])
        cum_i = sb("cum_i", [P, NB], I32)
        last = {k: sb(f"last_{k}", [P, NB]) for k in SIDES}
        last_col = {k: sb(f"last_col_{k}", [P, 1]) for k in SIDES}
        last_i = {k: sb(f"last_i_{k}", [1, NB], I32) for k in SIDES}
        done = sb("done", [P, 2, S])
        first_of = sb("first_of", [P, 1])
        first_node = {k: sb(f"first_node_{k}", [P, S]) for k in SIDES}
        keep = {k: sb(f"keep_{k}", [P, S]) for k in SIDES}
        limit = {k: sb(f"limit_{k}", [P, S]) for k in SIDES}
        group_i = {k: sb(f"group_i_{k}", [1, S], I32) for k in SIDES}
        row_i = sb("row_i", [1, S], I32)
        s_node = sb("s_node", [P, NB])
        s_nodeT = sb("s_nodeT", [P, P])
        s_step = {k: sb(f"s_step_{k}", [P, S]) for k in SIDES}
        dinv = sb("dinv", [P, NB])
        deal = sb("deal", [P, U, T, ROW])
        prod = sb("prod", [P, T, D])
        picked = sb("picked", [P, T, NB])
        posf = sb("posf", [P, 2, T])
        pos = sb("pos", [P, U, T], I32)
        note = sb("note", [P, U, T, 2])
        ring = sb("ring", [P, U, T, ROW])
        ring_note = sb("ring_note", [P, U, T, 2])
        local = sb("local", [P, 2, T], BF16)
        away = sb("away", [P, U, P, T], BF16)
        masked = sb("masked", [P, 2, P, T])
        hot_rows = masked[:, :, :, :].rearrange("p b n j -> p b (n j)").rearrange("p b (j n) -> p b j n", j=T)
        mx = sb("mx", [P, U])
        top = sb("top", [P, U])
        zneg = sb("zneg", [P, U])
        least = sb("least", [P, U])
        bias_hi = sb("bias_hi", [P, U])
        bias_lo = sb("bias_lo", [P, U])
        shift = sb("shift", [P, U])
        corr = sb("corr", [P, U])
        exp_hi = sb("exp_hi", [P, 2, GE])
        exp_lo = sb("exp_lo", [P, 2, GE])
        wT = sb("wT", [P, 2, GE])
        wgt = sb("wgt", [P, 2, GE])
        acc = sb("acc", [P, 3, ROW])
        both = sb("both", [P, 2, CH, ROW])
        part = {k: both[:, w, :, :] for w, k in enumerate(SIDES)}
        apart = both[:, :, :, :].rearrange("p w b f -> p (w b f)")[:, 0:OC]
        small = sb("small", [P, 8, CH])
        scale2 = sb("scale2", [P, 2, CH])
        agg = sb("agg", [P, CH, D])
        sq = exp_lo[:, :, :].rearrange("p b e -> p (b e)")[:, 0:CH * D].rearrange("p (b f) -> p b f", f=D)

        bank = [pb(f"bank{i}", [P, 512]) for i in range(8)]
        tbank, qbank, obank = (bank[0], bank[1], bank[6]), bank[2:4], bank[4:6]
        placebank = bank[7]
        places = placebank[:, 0:NB * T].rearrange("p (b j) -> p b j", j=T)

        sems = {}

        def sm(name):
            if name not in sems:
                sems[name] = ctx.enter_context(nc.semaphore(name))
            return sems[name]

        def pair(view, n, k):
            return view.unsqueeze(1).to_broadcast([view.shape[0], n, k])

        def spread(view, n, k):
            return view.unsqueeze(2).to_broadcast([view.shape[0], n, k])

        def turns(i, off, m, body=U):
            return i * (body // m) + off // m

        def fillings(k, n):
            return (n - 1 - k) // U + 1

        def source_rows(off):
            return (ring if off % (2 * U) < U else deal)[:, off % U, :, :]

        def source_rows_in(i, off):
            k, count = off % U, (turns(i, off, 2 * U, 2 * U) + 1) * 16
            if off % (2 * U) < U:
                return sm(f"rows_in{k}"), count + 16 * fillings(k, S)
            return sm(f"edges_in{k}"), count + 16 * fillings(k, G)

        def before_messages(k):
            return 16 * fillings(k, S) + 16 * ((S - 1 - k) // (2 * U) + 1)

        def rows_of(view):
            return view.rearrange("a p f -> (a p) f")

        class Chain:

            def __init__(self, eng, name, base=0):
                self.eng, self.sem, self.n = eng, sm(name), base

            def __call__(self, ins):
                self.n = self.n + 1
                ins.then_inc(self.sem, 1)
                self.eng.wait_ge(self.sem, self.n)

        note_groups = notes[:, :].rearrange("(g p j) f -> g p (j f)", p=P, j=T)
        source_groups = by_source[:, :].rearrange("(g p j) f -> g p (j f)", p=P, j=T)
        message_groups = messages[:, :].rearrange("(g p j) f -> g p (j f)", p=P, j=T)
        table_blocks = table[0:NB * P, :].rearrange("(b p) f -> p b f", p=P)
        TAIL = E - 1 - P * (OC - T * 10)
        CHECK = OC - T * 10
        TAIL_P, TAIL_C = 29, 11
        assert TAIL == TAIL_P * TAIL_C and CHECK + TAIL_C <= OC

        block = ctx.enter_context(nc.Block())

        @block.sync
        def _(sp):
            sp.wait_ge(sm("pads_set"), 5)
            for t, a in ((here, 0), (there, 1)):
                sp.dma_start(t[:, 0:CHECK], dst[a:a + P * CHECK].rearrange("(p c) -> p c", p=P)).then_inc(sm("check_in"), 16)
                sp.dma_start(t[0:TAIL_P, CHECK:CHECK + TAIL_C], dst[P * CHECK + a:P * CHECK + a + TAIL].rearrange("(p c) -> p c", c=TAIL_C)).then_inc(sm("check_in"), 16)
            sp.dma_start(w_node[:, :], att_w[0:D].partition_broadcast(P)).then_inc(sm("weights_in"), 16)
            sp.dma_start(w_edge[:, :], att_w[D:2 * D].partition_broadcast(P)).then_inc(sm("weights_in"), 16)
            sp.dma_start(att_bias[:, :], att_b[0:1].partition_broadcast(P)).then_inc(sm("weights_in"), 16)
            sp.dma_start(w_proj[:, :], w1[:, :]).then_inc(sm("weights_in"), 16)
            sp.dma_start(out_bias[:, :], b1[:].partition_broadcast(P)).then_inc(sm("weights_in"), 16)
            sp.dma_start(nodes[:, 0:NB - 1, :], x[0:(NB - 1) * P, :].rearrange("(b p) f -> p b f", p=P)).then_inc(sm("nodes_in"), 16)
            sp.dma_start(nodes[0:LAST_NODES, NB - 1, :], x[(NB - 1) * P:N, :]).then_inc(sm("nodes_in"), 16)
            sp.dma_start(table[NB * P:(NB + 1) * P, :], agg[:, 0, :]).then_inc(sm("no_node_out"), 16)

            sp.wait_ge(sm("flag_ready"), 1)
            flag = sp.to_reg(sp.value_load(flag_i[0:1, 0:1], min_val=0, max_val=P))

            with sp.If_ne(flag, 0):
                sp.dma_start(here[0:OP, :], dst[:].rearrange("(p c) -> p c", p=OP)).then_inc(sm("order_ids"), 16)
                sp.dma_start(there[0:OP, :], src[:].rearrange("(p c) -> p c", p=OP)).then_inc(sm("order_ids"), 16)
                columns = edge_attr[:, :].rearrange("(p c) f -> p c f", p=OP)
                sp.dma_start(prod[0:OP, 0, :], columns[:, 0, :]).then_inc(sm("order_in"), 16)
                with sp.Fori(1, OC) as c:
                    for what in ("edges", "dst", "src"):
                        sp.wait_ge(sm(f"order_out_{what}"), c * 16)
                    sp.sem_inc(sm("waited"), 1)
                    sp.dma_start(prod[0:OP, 0, :], columns[:, ds(c, 1), :].rearrange("p a f -> p (a f)")).then_inc(sm("order_in"), 16)
                for what in ("edges", "dst", "src"):
                    sp.wait_ge(sm(f"order_out_{what}"), OC * 16)

            def of_edges(make):
                with sp.If_eq(flag, 0):
                    make(given)
                with sp.Else():
                    make(ordered)

            def load_numbers(a):
                for k in SIDES:
                    ids_1d = a[k][:] if a is given else a[k][:, :].rearrange("e a -> (e a)")
                    sp.dma_start(lying[k][:, 0:Q - 1, :], ids_1d[0:(Q - 1) * R * GE].rearrange("(q r c) -> r q c", q=Q - 1, r=R)).then_inc(sm("numbers_in"), 16)
                    sp.dma_start(lying[k][0:G - 1 - (Q - 1) * R, Q - 1, :], ids_1d[(Q - 1) * R * GE:(G - 1) * GE].rearrange("(r c) -> r c", c=GE)).then_inc(sm("numbers_in"), 16)
                    sp.dma_start(lying[k][G - 1 - (Q - 1) * R:G - (Q - 1) * R, Q - 1, :], ids_1d[E - GE:E].rearrange("(r c) -> r c", c=GE)).then_inc(sm("numbers_in"), 16)

            of_edges(load_numbers)

            def edges(a, i, off):
                k, n = off % U, i * U + off
                if off >= U:
                    sp.wait_ge(sm(f"dealt{k}"), turns(i, off, U) * (16 * T))
                if isinstance(n, int):
                    row = min(n * GE, E - GE)
                    view = a["edges"][row:row + GE, :].rearrange("(p j) f -> p j f", j=T)
                else:
                    view = a["edges"][0:(G - 1) * GE, :].rearrange("(g p j) f -> g p j f", p=P, j=T)[ds(n, 1), :, :, :].rearrange("a p j f -> (a p) j f")
                sp.dma_start(deal[:, k, :, 0:D], view).then_inc(sm(f"edges_in{k}"), 16)

            def load_notes(i, off):
                k, n = off % U, i * U + off
                if off >= U:
                    sp.wait_ge(sm("dst_scores_ready"), n - (U - 1))
                    sp.sem_inc(sm("waited"), 1)
                g = sp.value_load(group_i["dst"][0:1, ds(n, 1)], min_val=0, max_val=G - 1)
                sp.dma_start(ring_note[:, k, :, :].rearrange("p j f -> p (j f)"), rows_of(note_groups[ds(g, 1), :, :])).then_inc(sm(f"notes_in{k}"), 16)

            def load_rows(a, i, off):
                k, n = off % U, i * U + off
                if off >= U:
                    sp.wait_ge(sm("dst_summed"), n - (U - 1))
                    sp.sem_inc(sm("waited"), 1)
                row = sp.value_load(row_i[0:1, ds(n, 1)], min_val=0, max_val=E - GE)
                sp.dma_start(ring[:, k, :, 0:D], a["edges"][ds(row, GE), :].rearrange("(p j) f -> p j f", j=T)).then_inc(sm(f"rows_in{k}"), 16)

            def store_sums(walk, i, off, width):
                n, r = i * BODY.get(walk, U) + off, off % 3
                sp.wait_ge(sm(f"{walk}_added"), n + 1)
                sp.dma_start(rows_of(sums[walk][ds(n, 1), :, 0:width]), acc[:, r, 0:width]).then_inc(sm(f"{walk}_sums_out{r}"), 16)

            def notes_written(i, off):
                sp.wait_ge(sm(f"note_out{off % U}"), (turns(i, off, U) + 1) * 16)
                if off >= U:
                    sp.sem_inc(sm("waited"), 1)

            def merged(a, i, off):
                if not isinstance(i, int) or off + 2 < G:
                    edges(a, i, off + 2)
                if off >= 2:
                    notes_written(i, off - 2)
                    load_notes(i, off - 2)
                if off >= 4:
                    load_rows(a, i, off - 4)
                if off >= LAG + 4:
                    store_sums("dst", i, off - (LAG + 4), ROW)

            def rest_step(a, i, off):
                if not isinstance(i, int) or off < S:
                    load_notes(i, off)
                load_rows(a, i, off - 2)
                store_sums("dst", i, off - (LAG + 2), ROW)

            sp.wait_ge(sm("tables_ready"), 2)

            def walk_by_target(a):
                edges(a, 0, 0)
                edges(a, 0, 1)
                for n in range(2 * U):
                    merged(a, 0, n)
                with sp.Fori(0, (G - 2 * U) // U - 1) as i:
                    for k in range(2 * U, 3 * U):
                        merged(a, i, k)
                for n in range(G - 1 - U, G):
                    merged(a, 0, n)
                notes_written(0, G - 2)
                notes_written(0, G - 1)
                rest_step(a, 0, G - 2)
                with sp.Fori(G // U - 2, S // U - 2) as i:
                    for k in range(2 * U, 3 * U):
                        rest_step(a, i, k)
                for s in range(S // U * U, S + 2):
                    rest_step(a, 0, s)
                for s in range(S - LAG, S):
                    store_sums("dst", 0, s, ROW)

            of_edges(walk_by_target)

            for k in range(U):
                sp.wait_ge(sm(f"dealt{k}"), ((G - 1 - k) // U + 1) * (16 * T))
            sp.wait_ge(sm("dst_summed"), S)

            def load_by_source(i, off):
                n = i * (2 * U) + off
                if off >= 2 * U:
                    sp.wait_ge(sm("src_summed"), n - (2 * U - 1))
                    sp.sem_inc(sm("waited"), 1)
                g = sp.value_load(group_i["src"][0:1, ds(n, 1)], min_val=0, max_val=G - 1)
                sp.dma_start(source_rows(off).rearrange("p j f -> p (j f)"), rows_of(source_groups[ds(g, 1), :, :])).then_inc(source_rows_in(i, off)[0], 16)

            AFTER = 2 * U + 2

            def source_step(i, off):
                load_by_source(i, off)
                if off >= AFTER:
                    store_sums("src", i, off - AFTER, ROW)

            for s in range(4 * U):
                source_step(0, s)
            with sp.Fori(0, S // (2 * U) - 2) as i:
                for k in range(4 * U, 6 * U):
                    source_step(i, k)
            for s in range(S // (2 * U) * (2 * U), S):
                source_step(0, s)
            for s in range(S - AFTER, S):
                store_sums("src", 0, s, ROW)

            for k in SIDES:
                for r in range(3):
                    sp.wait_ge(sm(f"{k}_sums_out{r}"), 16 * ((S - r + 2) // 3))

            def sums_in(i, off):
                it = i + off
                if off:
                    sp.wait_ge(sm("chunk_used"), it)
                for k in SIDES:
                    for j in range(CH):
                        at = sp.value_load(last_i[k][0:1, ds(it * CH + j, 1)], min_val=0, max_val=S - 1)
                        sp.dma_start(part[k][:, j, :], rows_of(sums[k][ds(at, 1), :, :])).then_inc(sm("chunk_in"), 16)

            def table_out(it):
                sp.wait_ge(sm("projected"), it + 1)
                sp.dma_start(table_blocks[:, ds(it * CH, CH), :], agg[:, :, :]).then_inc(sm("table_out"), 16)

            sums_in(0, 0)
            with sp.Fori(0, NCH - 1) as i:
                sums_in(i, 1)
                table_out(i)
            table_out(NCH - 1)

            def load_messages(i, off):
                k, n = off % U, i * U + off
                if off >= U:
                    sp.wait_ge(sm("msg_summed"), n - (U - 1))
                    sp.sem_inc(sm("waited"), 1)
                g = sp.value_load(group_i["dst"][0:1, ds(n, 1)], min_val=0, max_val=G - 1)
                sp.wait_ge(sm("messages_stored"), g + 1)
                sp.dma_start(ring[:, k, :, 0:D], message_groups[ds(g, 1), :, :].rearrange("a p (j f) -> (a p) j f", j=T)).then_inc(sm(f"rows_in{k}"), 16)
                sp.dma_start(ring_note[:, k, :, :].rearrange("p j f -> p (j f)"), rows_of(note_groups[ds(g, 1), :, :])).then_inc(sm(f"notes_in{k}"), 16)

            def message_step(i, off):
                load_messages(i, off)
                if off >= 3:
                    store_sums("msg", i, off - 3, D)

            for s in range(U):
                message_step(0, s)
            with sp.Fori(0, S // U - 1) as i:
                for k in range(U, 2 * U):
                    message_step(i, k)
            for s in range(S // U * U, S):
                message_step(0, s)
            for s in range(S - 3, S):
                store_sums("msg", 0, s, D)

            for r in range(3):
                sp.wait_ge(sm(f"msg_sums_out{r}"), 16 * ((S - r + 2) // 3))

            def messages_in(i, off):
                it = i + off
                if off:
                    sp.wait_ge(sm("chunk_used"), it + NCH)
                for j in range(CH):
                    at = sp.value_load(last_i["dst"][0:1, ds(it * CH + j, 1)], min_val=0, max_val=S - 1)
                    sp.dma_start(part["src"][:, j, 0:D], rows_of(sums["msg"][ds(at, 1), :, 0:D])).then_inc(sm("chunk2_in"), 16)
                sp.dma_start(part["dst"][:, :, 0:D], table_blocks[:, ds(it * CH, CH), :]).then_inc(sm("chunk2_in"), 16)

            messages_in(0, 0)
            with sp.Fori(0, NCH - 1) as i:
                messages_in(i, 1)
                sp.wait_ge(sm("result_ready"), i + 1)
                sp.dma_start(out[0:(NCH - 1) * CH * P, :].rearrange("(b p) f -> p b f", p=P)[:, ds(i * CH, CH), :], agg[:, :, :]).then_inc(sm("result_out"), 16)
            sp.wait_ge(sm("result_ready"), NCH)
            b0 = (NCH - 1) * CH
            sp.dma_start(out[b0 * P:(NB - 1) * P, :].rearrange("(b p) f -> p b f", p=P), agg[:, 0:CH - 1, :]).then_inc(sm("result_out"), 16)
            sp.dma_start(out[(NB - 1) * P:N, :], agg[0:LAST_NODES, CH - 1, :]).then_inc(sm("result_out"), 16)
            sp.wait_ge(sm("no_node_out"), 16)
            sp.wait_ge(sm("result_out"), 16 * (NCH + 1))

        @block.gpsimd
        def _(pool):
            loose = dict(allow_small_or_imprecise_dtypes=True)
            pool.iota(iota_f[:, :], [[1, P]], base=0, channel_multiplier=0, **loose).then_inc(sm("iotas"), 1)
            pool.iota(iota_p[:, :], [[0, 1]], base=0, channel_multiplier=1, **loose).then_inc(sm("iotas"), 1)
            pool.iota(iota_s[:, :], [[1, S]], base=0, channel_multiplier=0, **loose).then_inc(sm("iotas"), 1)
            pool.iota(iota_b[:, :, :], [[1, NB], [0, T]], base=0, channel_multiplier=0, **loose).then_inc(sm("iotas"), 1)
            pool.iota(iota_n[:, :, :], [[1, P], [0, T]], base=0, channel_multiplier=0, **loose).then_inc(sm("iotas"), 1)
            pool.iota(spare[:, :], [[1, T]], base=E, channel_multiplier=T, **loose).then_inc(sm("iotas"), 1)
            pool.memset(half_n[:, :], -0.5).then_inc(sm("iotas"), 1)

            pool.wait_ge(sm("flag_ready"), 1)
            flag = pool.to_reg(pool.value_load(flag_i[0:1, 0:1], min_val=0, max_val=P))
            with pool.If_ne(flag, 0):
                with pool.Fori(0, OC) as c:
                    pool.wait_ge(sm("order_placed"), c + 1)
                    pool.wait_ge(sm("order_in"), c * 16 + 16)
                    pool.sem_inc(sm("waited"), 1)
                    place = bass.IndirectOffsetOnAxis(ap=pos[0:OP, 0, 0:1], axis=0)
                    for what, of in (("edges", prod[0:OP, 0, :]), ("dst", pos[0:OP, 0, 1:2]), ("src", pos[0:OP, 0, 2:3])):
                        pool.indirect_dma_start(out=ordered[what][:, :], out_offset=place, in_=of, in_offset=None).then_inc(sm(f"order_out_{what}"), 16)

            def deal_out(i, off):
                n, k = i * U + off, off % U
                pool.wait_ge(sm("sources_in_rows"), n + 1)
                pool.wait_ge(sm("placed"), n + 1)
                pool.sem_inc(sm("waited"), 1)
                for j in range(T):
                    pool.indirect_dma_start(
                        out=by_source[:, :], out_offset=bass.IndirectOffsetOnAxis(ap=pos[:, k, j:j + 1], axis=0),
                        in_=deal[:, k, j, :], in_offset=None).then_inc(sm(f"dealt{k}"), 16)

            with pool.Fori(0, G // U) as i:
                for k in range(U):
                    deal_out(i, k)
            for n in range(G // U * U, G):
                deal_out(0, n)

            def weights(i, off):
                n, b = i * U + off, off % 2
                if off >= 2:
                    pool.wait_ge(sm("src_turned_back"), n - 1)
                pool.wait_ge(sm("src_exps_ready"), n + 1)
                pool.tensor_tensor(wT[:, b, :], exp_hi[:, b, :], exp_lo[:, b, :], ALU.mult).then_inc(sm("src_weights_ready"), 1)

            for s in range(U):
                weights(0, s)
            with pool.Fori(0, S // U - 1) as i:
                for k in range(U, 2 * U):
                    weights(i, k)
            for s in range(S // U * U, S):
                weights(0, s)

            pool.wait_ge(sm("iotas"), 7)
            with pool.Fori(0, NCH) as it:
                pool.wait_ge(sm("deg_ready"), it + 1)
                pool.tensor_tensor(small[:, 0, :], small[:, 3, :], half_n[:, :], ALU.pow).then_inc(sm("dinv_ready"), 1)
                pool.wait_ge(sm("var_ready"), it + 1)
                pool.tensor_tensor(small[:, 7, :], small[:, 6, :], half_n[:, :], ALU.pow).then_inc(sm("rstd_ready"), 1)

            pool.wait_ge(sm("table_out"), 16 * NCH)
            pool.wait_ge(sm("no_node_out"), 16)

            def gather(i, off):
                n, k = i * U + off, off % U
                if off >= U:
                    pool.wait_ge(sm(f"msg_out{k}"), turns(i, off, U) * 16)
                pool.wait_ge(sm("sources_ready"), n + 1)
                pool.sem_inc(sm("waited"), 1)
                for j in range(T):
                    pool.indirect_dma_start(
                        out=deal[:, k, j, 0:D], out_offset=None, in_=table[:, :],
                        in_offset=bass.IndirectOffsetOnAxis(ap=pos[:, k, j:j + 1], axis=0)).then_inc(sm(f"gathered{k}"), 16)

            for n in range(U):
                gather(0, n)
            with pool.Fori(0, G // U - 1) as i:
                for k in range(U, 2 * U):
                    gather(i, k)
            for n in range(G // U * U, G):
                gather(0, n)

            with pool.Fori(0, NCH) as it:
                pool.wait_ge(sm("var_ready"), it + (NCH + 1))
                pool.tensor_tensor(small[:, 7, :], small[:, 6, :], half_n[:, :], ALU.pow).then_inc(sm("rstd_ready"), 1)

        @block.scalar
        def _(act):
            def pick_places(i, off, final=False):
                n, b, k = i * U + off, off % 2, off % U
                act.wait_ge(sm("places_lifted"), n + 1)
                if off >= 1:
                    act.wait_ge(sm("places_picked"), n)
                for j in range(T):
                    ins = act.activation(picked[:, j, :], places[:, :, j], ACT.Relu, bias=minus_lift[:, 0:1], accum_out=posf[:, b, j:j + 1])
                ins.then_inc(sm("places_picked"), 1)
                if off >= U:
                    act.wait_ge(sm(f"dealt{k}"), turns(i, off, U) * (16 * T))
                act.wait_ge(sm("places_picked"), n + 1)
                if final:
                    for j in range(T):
                        ins = act.activation(pos[:, k, j:j + 1], posf[:, b, j:j + 1], ACT.Relu, bias=spare[:, j:j + 1])
                else:
                    ins = act.activation(pos[:, k, :], posf[:, b, :], ACT.Copy)
                ins.then_inc(sm("placed"), 1)

            def make_notes(i, off):
                n, k = i * U + off, off % U
                act.wait_ge(sm("scored"), n + 1)
                if off >= U:
                    act.wait_ge(sm(f"note_out{k}"), turns(i, off, U) * 16)
                cols = ds(n * T, T)
                act.activation(deal[:, k, :, SOURCE], ids["src"][:, cols], ACT.Copy).then_inc(sm("sources_in_rows"), 1)
                act.activation(note[:, k, :, 0], deal[:, k, :, SCORE], ACT.Copy)
                act.activation(note[:, k, :, 1], ids["dst"][:, cols], ACT.Copy).then_inc(sm("notes_made"), 1)
                act.wait_ge(sm("notes_made"), n + 1)
                act.dma_start(rows_of(note_groups[ds(n, 1), :, :]), note[:, k, :, :].rearrange("p j f -> p (j f)")).then_inc(sm(f"note_out{k}"), 16)

            def exps(walk, i, off):
                n, b, c = i * BODY[walk] + off, off % 2, off % U
                scores = tbank[off % 3][:, :]
                act.wait_ge(sm(f"{walk}_bias_ready"), n + 1)
                if off >= 2:
                    act.wait_ge(sm(f"{walk}_weights_ready"), n - 1)
                if walk == "dst":
                    act.activation(exp_hi[:, b, :], scores, ACT.Exp, bias=bias_hi[:, c:c + 1])
                    act.activation(exp_lo[:, b, :], scores, ACT.Exp, bias=bias_lo[:, c:c + 1], scale=SLOPE)
                else:
                    act.activation(exp_hi[:, b, :], scores, ACT.Relu, bias=s_step[walk][:, ds(n, 1)]).then_inc(sm("src_relu"), 1)
                    act.activation(exp_lo[:, b, :], scores, ACT.Exp, bias=bias_lo[:, c:c + 1], scale=SLOPE)
                    act.wait_ge(sm("src_relu"), n + 1)
                    act.activation(exp_hi[:, b, :], exp_hi[:, b, :], ACT.Exp, bias=bias_hi[:, c:c + 1], scale=1.0 - SLOPE)
                act.activation(corr[:, c:c + 1], shift[:, c:c + 1], ACT.Exp).then_inc(sm(f"{walk}_exps_ready"), 1)

            def copy_weights(walk, i, off):
                n, b = i * BODY[walk] + off, off % 2
                act.wait_ge(sm(f"{walk}_turned_back"), n + 1)
                if off >= 2:
                    act.wait_ge(sm(f"{walk}_summed"), n - 1)
                act.activation(wgt[:, b, :], qbank[b][:, :], ACT.Copy).then_inc(sm(f"{walk}_weights_out"), 1)

            def walk_step(walk, i, off):
                exps(walk, i, off)
                if off >= BACK[walk]:
                    copy_weights(walk, i, off - BACK[walk])

            def walk_end(walk):
                for s in range(S - BACK[walk], S):
                    copy_weights(walk, 0, s)

            def merged(i, off):
                if off >= 1:
                    pick_places(i, off - 1)
                if off >= LAG:
                    walk_step("dst", i, off - LAG)
                make_notes(i, off)

            for n in range(2 * U):
                merged(0, n)
            with act.Fori(0, (G - 2 * U) // U) as i:
                for k in range(2 * U, 3 * U):
                    merged(i, k)
            merged(0, G - 1)
            pick_places(0, G - 1, True)
            for s in range(G - LAG, G - 1):
                walk_step("dst", 0, s)
            with act.Fori(G // U - 1, S // U - 1) as i:
                for k in range(U, 2 * U):
                    walk_step("dst", i, k)
            for s in range(S // U * U, S):
                walk_step("dst", 0, s)
            walk_end("dst")

            for s in range(2 * U):
                walk_step("src", 0, s)
            with act.Fori(0, S // (2 * U) - 1) as i:
                for k in range(2 * U, 4 * U):
                    walk_step("src", i, k)
            for s in range(S // (2 * U) * (2 * U), S):
                walk_step("src", 0, s)
            walk_end("src")

            with act.Fori(0, NCH) as it:
                act.wait_ge(sm("merge_ready"), it + 1)
                act.activation(scale2[:, :, :], scale2[:, :, :], ACT.Exp).then_inc(sm("merge_exp"), 1)
                act.wait_ge(sm("agg_ready"), it + 1)
                act.activation(agg[:, :, :], agg[:, :, :], ACT.Gelu).then_inc(sm("gelu_done"), 1)

            def sources(i, off):
                n, k = i * U + off, off % U
                if off >= U:
                    act.wait_ge(sm(f"gathered{k}"), turns(i, off, U) * (16 * T))
                act.activation(pos[:, k, :], ids["src"][:, ds(n * T, T)], ACT.Copy).then_inc(sm("sources_ready"), 1)

            def message_out(i, off):
                n, k = i * U + off, off % U
                act.wait_ge(sm(f"gathered{k}"), (turns(i, off, U) + 1) * (16 * T))
                act.dma_start(message_groups[ds(n, 1), :, :].rearrange("a p (j f) -> (a p) j f", j=T), deal[:, k, :, 0:D]).then_inc(sm(f"msg_out{k}"), 16)

            def message_stored(i, off):
                act.wait_ge(sm(f"msg_out{off % U}"), (turns(i, off, U) + 1) * 16)
                act.sem_inc(sm("messages_stored"), 1)

            for k in range(U):
                act.wait_ge(sm(f"dealt{k}"), ((G - 1 - k) // U + 1) * (16 * T))
            for n in range(3):
                sources(0, n)
            for n in range(U - 3):
                message_out(0, n)
                if n >= 1:
                    message_stored(0, n - 1)
                sources(0, n + 3)
            with act.Fori(0, G // U - 1) as i:
                for k in range(U, 2 * U):
                    message_out(i, k - 3)
                    message_stored(i, k - 4)
                    sources(i, k)
            for n in range(G // U * U, G):
                message_out(0, n - 3)
                message_stored(0, n - 4)
                sources(0, n)
            for n in range(G - 3, G):
                message_out(0, n)
                message_stored(0, n - 1)
            message_stored(0, G - 1)

        @block.tensor
        def _(pe):
            pe.wait_ge(sm("constants_ready"), 1)
            pe.wait_ge(sm("apart_ready"), 1)
            pe.matmul(bank[0][0:1, 0:1], unsorted[:, :], ones[:, 0:1], start=True, stop=True).then_inc(sm("flag_summed"), 1)
            pe.wait_ge(sm("flag_ready"), 1)
            flag = pe.to_reg(pe.value_load(flag_i[0:1, 0:1], min_val=0, max_val=P))

            with pe.If_ne(flag, 0):
                pe.wait_ge(sm("order_counted"), OC)
                pe.matmul(bank[0][0:NB, 0:1], total[0:OP, :, 0], ones[0:OP, 0:1], start=True, stop=True).then_inc(sm("order_totals"), 1)
                pe.wait_ge(sm("order_totals_out"), 1)
                pe.matmul(bank[1][0:OP, 0:NB], below[0:OP, 0:OP], total[0:OP, :, 0], start=True, stop=False)
                pe.matmul(bank[1][0:OP, 0:NB], s_nodeT[0:NB, 0:OP], below[0:NB, 0:NB], start=False, stop=True).then_inc(sm("order_starts"), 1)

            pe.wait_ge(sm("numbers_ready"), 2)
            for w, k in enumerate(SIDES):
                for q in range(Q):
                    for j in range(T):
                        ins = pe.transpose(bank[w * Q + q][:, j * R:(j + 1) * R],
                                           lying[k][:, q, :].bitcast(F32).rearrange("r (p j) -> r j p", j=T)[:, j, :], ident[0:R, 0:R])
                    ins.then_inc(sm("numbers_turned"), 1)

            def count_group(i, off, first=False, stop=False):
                b = off % 3
                pe.wait_ge(sm("hot_ready"), i * U + off + 1)
                pe.matmul(bank[0][:, 0:NB * T], onesb[:, :], hot[:, b, :, :].rearrange("p b j -> p (b j)"), start=first, stop=stop).then_inc(sm("hot_used"), 1)

            pe.wait_ge(sm("numbers_out"), 1)
            count_group(0, 0, first=True)
            for n in range(1, U):
                count_group(0, n)
            with pe.Fori(1, G // U) as i:
                for k in range(U):
                    count_group(i, k)
            count_group(0, G - 1, stop=True)

            pe.wait_ge(sm("starts_ready"), 1)
            pe.matmul(placebank[:, 0:NB * T], ident[:, :], total[:, :, :].rearrange("p b j -> p (b j)"), start=True, stop=True)
            for q in range(Q):
                ins = pe.matmul(bank[1][:, 0:NB], ones[0:R, 0:P], passed[:, q, :], start=q == 0, stop=q == Q - 1)
            ins.then_inc(sm("passed_summed"), 1)
            pe.wait_ge(sm("lasts_ready"), 1)
            for w, k in enumerate(SIDES):
                ins = pe.transpose(bank[2][0:NB, w * P:(w + 1) * P], last[k][:, :], ident[:, :])
            ins.then_inc(sm("lasts_turned"), 1)
            pe.wait_ge(sm("node_scores_ready"), NCH)
            pe.transpose(bank[3][0:NB, 0:P], s_node[:, :], ident[:, :]).then_inc(sm("node_scores_turned"), 1)
            pe.wait_ge(sm("done_ready"), 1)
            for w, k in enumerate(SIDES):
                ins = pe.matmul(bank[4 + w][:, 0:S], ones[0:NB, 0:P], done[0:NB, w, :], start=True, stop=True)
            ins.then_inc(sm("steps_ready"), 1)
            pe.wait_ge(sm("step_blocks_ready"), 1)
            for w, k in enumerate(SIDES):
                ins = pe.matmul(bank[w][:, 0:S], s_nodeT[0:NB, :], done[0:NB, w, :], start=True, stop=True)
            ins.then_inc(sm("step_scores_ready"), 1)

            flat = hot[:, :, :, :].rearrange("p r b j -> p r (b j)")

            def lift_places(i, off):
                n, b = i * U + off, off % 3
                pe.wait_ge(sm("hot_ready"), n + (G + 1))
                pe.matmul(placebank[:, 0:NB * T], lifted[:, :], flat[:, b, :], start=False, stop=True, skip_group_check=True).then_inc(sm("places_lifted"), 1)

            def count_on(i, off):
                n, b = i * U + off, off % 3
                pe.wait_ge(sm("places_picked"), n + 1)
                pe.matmul(placebank[:, 0:NB * T], rest[:, :], flat[:, b, :], start=False, stop=False, skip_group_check=True)
                pe.matmul(placebank[:, 0:NB * T], lower[:, :], flat[:, b, :], start=False, stop=True, skip_group_check=True).then_inc(sm("hot_used"), 1)

            def turn(walk, i, off):
                n, b, c = i * BODY[walk] + off, off % 2, off % 3
                pe.wait_ge(sm(f"{walk}_scores_ready"), n + 1)
                if off >= 3:
                    pe.wait_ge(sm(f"{walk}_exps_ready"), n - 2)
                for j in range(T):
                    ins = pe.transpose(tbank[c][:, j * P:(j + 1) * P], masked[:, b, :, j], ident[:, :])
                ins.then_inc(sm(f"{walk}_turned"), 1)

            def turn_back(walk, i, off):
                n, b = i * BODY[walk] + off, off % 2
                pe.wait_ge(sm(f"{walk}_weights_ready"), n + 1)
                if off >= 2:
                    pe.wait_ge(sm(f"{walk}_weights_out"), n - 1)
                for j in range(T):
                    ins = pe.transpose(qbank[b][:, j * P:(j + 1) * P], wT[:, b, j * P:(j + 1) * P], ident[:, :])
                ins.then_inc(sm(f"{walk}_turned_back"), 1)

            def sum_rows(walk, i, off):
                n, b = i * BODY[walk] + off, off % 2
                pe.wait_ge(sm(f"{walk}_weights_out"), n + 1)
                if off >= 2:
                    pe.wait_ge(sm(f"{walk}_added"), n - 1)
                rows = source_rows(off) if walk == "src" else ring[:, off % U, :, :]
                if walk == "dst":
                    pe.wait_ge(sm(f"rows_in{off % U}"), (turns(i, off, U) + 1) * 16)
                for j in range(T):
                    ins = pe.matmul(obank[b][:, 0:D + 1], wgt[:, b, j * P:(j + 1) * P], rows[:, j, 0:D + 1], start=j == 0, stop=j == T - 1)
                if walk == "dst":
                    degree = obank[b][:, DEGREE:DEGREE + 1]
                    pe.matmul(degree, onesb[:, :], counts[:, 1:2], start=True, stop=False)
                    for j in range(T):
                        ins = pe.matmul(degree, away[:, off % U, :, j], counts[:, 0:1], start=False, stop=j == T - 1)
                ins.then_inc(sm(f"{walk}_summed"), 1)

            def walk_step(walk, i, off, more=True):
                if isinstance(i, int) and off == 0:
                    turn(walk, i, 0)
                    turn(walk, i, 1)
                if more:
                    turn(walk, i, off + 2)
                if off >= BACK[walk]:
                    turn_back(walk, i, off - BACK[walk])
                if off >= BACK[walk] + 1:
                    sum_rows(walk, i, off - BACK[walk] - 1)

            def walk_end(walk):
                for s in range(S - BACK[walk], S):
                    turn_back(walk, 0, s)
                    sum_rows(walk, 0, s - 1)
                sum_rows(walk, 0, S - 1)

            def merged(i, off):
                if off >= LAG:
                    walk_step("dst", i, off - LAG)
                if off >= 1:
                    count_on(i, off - 1)
                lift_places(i, off)

            pe.wait_ge(sm("step_scores_out"), 1)
            for n in range(2 * U):
                merged(0, n)
            with pe.Fori(0, (G - 2 * U) // U) as i:
                for k in range(2 * U, 3 * U):
                    merged(i, k)
            merged(0, G - 1)
            for s in range(G - LAG, G - 1):
                walk_step("dst", 0, s)
            with pe.Fori(G // U - 1, S // U - 1) as i:
                for k in range(U, 2 * U):
                    walk_step("dst", i, k)
            for s in range(S // U * U, S):
                walk_step("dst", 0, s, s + 2 < S)
            walk_end("dst")

            pe.wait_ge(sm("dst_added"), S)
            for s in range(2 * U):
                walk_step("src", 0, s)
            with pe.Fori(0, S // (2 * U) - 1) as i:
                for k in range(2 * U, 4 * U):
                    walk_step("src", i, k)
            for s in range(S // (2 * U) * (2 * U), S):
                walk_step("src", 0, s, s + 2 < S)
            walk_end("src")

            with pe.Fori(0, NCH) as it:
                pe.wait_ge(sm("first_result_ready"), it + 1)
                for j in range(CH):
                    ins = pe.transpose(tbank[j // T][:, j % T * P:(j % T + 1) * P], sq[:, j, :], ident[:, :])
                ins.then_inc(sm("result_turned"), 1)
                pe.wait_ge(sm("result_copied"), it + 1)
                for j in range(CH):
                    ins = pe.matmul(qbank[j // T][:, j % T * P:(j % T + 1) * P], wT[:, j // T, j % T * P:(j % T + 1) * P], w_proj[:, :], start=True, stop=True)
                ins.then_inc(sm("projection_ready"), 1)

            def sum_messages(i, off):
                n, b = i * U + off, off % 2
                pe.wait_ge(sm("msg_hot"), n + 1)
                k = off % U
                pe.wait_ge(sm(f"rows_in{k}"), (turns(i, off, U) + 1) * 16 + before_messages(k))
                if off >= 2:
                    pe.wait_ge(sm("msg_added"), n - 1)
                for j in range(T):
                    ins = pe.matmul(obank[b][:, 0:D], hot_rows[:, b, j, :], ring[:, off % U, j, 0:D], start=j == 0, stop=j == T - 1)
                ins.then_inc(sm("msg_summed"), 1)

            sum_messages(0, 0)
            sum_messages(0, 1)
            with pe.Fori(0, (S - 2) // U) as i:
                for k in range(2, U + 2):
                    sum_messages(i, k)

        @block.vector
        def _(dve):
            c = Chain(dve, "setup")
            c(dve.memset(ones[:, :], 1.0))
            for t in (here, there):
                dve.memset(t[:, CHECK:CHECK + TAIL_C], 0).then_inc(sm("pads_set"), 1)
            for k in SIDES:
                dve.memset(lying[k][R - 2:R, Q - 1, :], NO_NODE).then_inc(sm("pads_set"), 1)
            dve.memset(nodes[P // 2:P, NB - 1, :], 0.0)
            dve.memset(agg[:, 0, :], 0.0).then_inc(sm("pads_set"), 1)
            dve.memset(deal[:, :, :, D:ROW], 1.0)
            dve.memset(ring[:, :, :, D:ROW], 1.0)
            dve.memset(onesb[:, :], 1.0)
            dve.memset(counts[:, 0:1], -1.0)
            dve.memset(counts[:, 1:2], float(T))
            dve.memset(minus_lift[:, :], -LIFT)
            dve.memset(acc[:, :, :], 0.0)
            dve.memset(top[:, :], 0.0)
            dve.memset(least[:, :], 0.0)
            for k in SIDES:
                dve.memset(keep[k][:, 0:1], 0.0)
            dve.wait_ge(sm("iotas"), 7)
            for m, op in ((ident, ALU.is_equal), (below, ALU.is_gt), (rest, ALU.is_le)):
                dve.tensor_scalar(m[:, :], iota_f[:, :], iota_p[:, 0:1], None, op)
            c(dve.tensor_scalar(lower[:, :], iota_f[:, :], iota_p[:, 0:1], -LIFT, ALU.is_equal, ALU.mult))
            c(dve.tensor_tensor(lifted[:, :], below[:, :], lower[:, :], ALU.subtract))
            c(dve.tensor_scalar(first_of[:, :], iota_p[:, :], float(AGAIN_P), None, ALU.is_lt))
            c(dve.tensor_scalar(spare[:, :], spare[:, :], first_of[:, 0:1], None, ALU.mult))
            c(dve.tensor_scalar(first_of[:, :], iota_p[:, :], float(P), None, ALU.mult))
            dve.sem_inc(sm("constants_ready"), 1)

            dve.wait_ge(sm("check_in"), 64)
            c(dve.tensor_tensor(apart[:, 0:CHECK + TAIL_C], here[:, 0:CHECK + TAIL_C], there[:, 0:CHECK + TAIL_C], ALU.is_gt))
            dve.reduce_max(unsorted[:, :], apart[:, 0:CHECK + TAIL_C], AX.X).then_inc(sm("apart_ready"), 1)
            dve.wait_ge(sm("flag_summed"), 1)
            dve.tensor_copy(flag_i[0:1, 0:1], bank[0][0:1, 0:1]).then_inc(sm("flag_ready"), 1)
            dve.wait_ge(sm("flag_ready"), 1)
            flag = dve.to_reg(dve.value_load(flag_i[0:1, 0:1], min_val=0, max_val=P))

            with dve.If_ne(flag, 0):
                c2 = Chain(dve, "order_chain")
                dve.wait_ge(sm("order_ids"), 32)
                c2(dve.tensor_scalar(apart[0:OP, :].bitcast(I32), here[0:OP, :], LOG_P, None, ALU.arith_shift_right))
                c2(dve.tensor_copy(apart[0:OP, :], apart[0:OP, :].bitcast(I32)))
                c2(dve.memset(total[:, :, :], 0.0))
                edge_block = apart[0:OP, :]
                start, tally = total[0:OP, :, 0], iota_f[0:OP, 0:NB]
                dve.scalar_tensor_tensor(start, tally, edge_block[:, 0:1], start, ALU.is_equal, ALU.add).then_inc(sm("order_counted"), 1)
                with dve.Fori(1, OC) as col:
                    dve.wait_ge(sm("order_counted"), col)
                    dve.scalar_tensor_tensor(start, tally, edge_block[:, ds(col, 1)], start, ALU.is_equal, ALU.add).then_inc(sm("order_counted"), 1)
                dve.wait_ge(sm("order_totals"), 1)
                c2(dve.tensor_copy(unsorted[0:NB, :], bank[0][0:NB, 0:1]))
                dve.tensor_scalar(s_nodeT[0:NB, 0:OP], ones[0:NB, 0:OP], unsorted[0:NB, 0:1], None, ALU.mult).then_inc(sm("order_totals_out"), 1)
                dve.wait_ge(sm("order_starts"), 1)
                c2(dve.tensor_copy(start, bank[1][0:OP, 0:NB]))

                def order_column(at, done_before):
                    col = edge_block[:, ds(at, 1)]
                    if done_before:
                        dve.wait_ge(sm("order_next"), at)
                        for what in ("edges", "dst", "src"):
                            dve.wait_ge(sm(f"order_out_{what}"), at * 16)
                    dve.scalar_tensor_tensor(upto[0:OP, :, 0], tally, col, start, ALU.is_equal, ALU.mult, accum_out=posf[0:OP, 0, 0:1]).then_inc(sm("order_picked"), 1)
                    dve.scalar_tensor_tensor(start, tally, col, start, ALU.is_equal, ALU.add).then_inc(sm("order_next"), 1)
                    dve.tensor_copy(pos[0:OP, 0, 1:2], here[0:OP, ds(at, 1)])
                    dve.tensor_copy(pos[0:OP, 0, 2:3], there[0:OP, ds(at, 1)])
                    dve.wait_ge(sm("order_picked"), at + 1)
                    dve.tensor_copy(pos[0:OP, 0, 0:1], posf[0:OP, 0, 0:1]).then_inc(sm("order_placed"), 1)

                order_column(0, False)
                with dve.Fori(1, OC) as col:
                    order_column(col, True)

            dve.wait_ge(sm("numbers_in"), 96)
            c(dve.tensor_scalar(ends_i[:, :], lying["dst"][:, :, GE - 1], LOG_P, None, ALU.arith_shift_right))
            c(dve.tensor_copy(ends[:, :], ends_i[:, :]))
            for k in SIDES:
                dve.tensor_copy(lying[k][:, :, :].bitcast(F32), lying[k][:, :, :]).then_inc(sm("numbers_ready"), 1)
            for w, k in enumerate(SIDES):
                for q in range(Q):
                    dve.wait_ge(sm("numbers_turned"), w * Q + q + 1)
                    ins = dve.tensor_copy(ids[k][:, q * R * T:(q + 1) * R * T].rearrange("p (g j) -> p j g", j=T),
                                          bank[w * Q + q][:, 0:R * T].rearrange("p (j g) -> p j g", j=T))
            c(ins)
            dve.sem_inc(sm("numbers_out"), 1)
            for k in SIDES:
                c(dve.memset(ids[k][0:AGAIN_P, (G - 1) * T:G * T], float(NO_NODE)))
            width = Q * R * T
            c(dve.tensor_copy(here[:, 0:width], ids["src"][:, :]))
            c(dve.tensor_scalar(here[:, 0:width], here[:, 0:width], LOG_P, None, ALU.arith_shift_right))
            c(dve.tensor_copy(blk[:, :], here[:, 0:width]))

            def hot_group(i, off, again):
                n, b = i * U + off, off % 3
                if off >= 3:
                    dve.wait_ge(sm("hot_used"), n + (G - 2) if again else n - 2)
                dve.tensor_tensor(hot[:, b, :, :], iota_b[:, :, :], pair(blk[:, ds(n * T, T)], NB, T), ALU.is_equal).then_inc(sm("hot_ready"), 1)

            for n in range(U):
                hot_group(0, n, False)
            with dve.Fori(0, G // U - 1) as i:
                for k in range(U, 2 * U):
                    hot_group(i, k, False)
            hot_group(0, G - 1, False)

            dve.wait_ge(sm("weights_in"), 80)
            dve.wait_ge(sm("nodes_in"), 32)
            with dve.Fori(0, NCH) as it:
                chunk = ds(it * CH, CH)
                c2 = Chain(dve, "node_score", it * 2)
                c2(dve.tensor_tensor(sq[:, :, :], nodes[:, chunk, :], pair(w_node[:, :], CH, D), ALU.mult))
                c2(dve.reduce_sum(small[:, 0, :], sq[:, :, :], AX.X))
                dve.tensor_scalar(s_node[:, chunk], small[:, 0, :], att_bias[:, 0:1], None, ALU.add).then_inc(sm("node_scores_ready"), 1)

            for q in range(Q):
                dve.tensor_scalar(passed[:, q, :], iota_f[0:R, 0:NB], ends[:, q:q + 1], None, ALU.is_ge)
            dve.wait_ge(sm("hot_used"), G)
            c(dve.tensor_copy(total[:, :, :].rearrange("p b j -> p (b j)"), bank[0][:, 0:NB * T]))
            c(dve.tensor_tensor_scan(upto[:, :, :].rearrange("p b j -> p (b j)"), ones[:, 0:NB * T], total[:, :, :].rearrange("p b j -> p (b j)"), 0.0, ALU.mult, ALU.add))
            dve.tensor_tensor(total[:, :, :], upto[:, :, :], total[:, :, :], ALU.subtract).then_inc(sm("starts_ready"), 1)
            c(dve.tensor_copy(cum_i[:, :], upto[:, :, T - 1]))
            c(dve.tensor_scalar(cum_i[:, :], cum_i[:, :], LOG_GE, None, ALU.arith_shift_right))
            c(dve.tensor_copy(last["src"][:, :], cum_i[:, :]))
            dve.wait_ge(sm("passed_summed"), 1)
            c(dve.tensor_copy(last["dst"][:, :], bank[1][:, 0:NB]))
            for k in SIDES:
                c(dve.scalar_tensor_tensor(last[k][:, :], last[k][:, :], float(G - 1), iota_f[:, 0:NB], ALU.min, ALU.add))
                dve.tensor_copy(last_i[k][0:1, :], last[k][0:1, :])
            dve.sem_inc(sm("lasts_ready"), 1)
            dve.wait_ge(sm("lasts_turned"), 1)
            for w, k in enumerate(SIDES):
                c(dve.tensor_copy(last_col[k][0:NB, :], bank[2][0:NB, w * P:w * P + 1]))
                ins = dve.tensor_scalar(done[0:NB, w, :], iota_s[0:NB, :], last_col[k][0:NB, 0:1], None, ALU.is_gt)
            ins.then_inc(sm("done_ready"), 1)
            dve.wait_ge(sm("node_scores_turned"), 1)
            c(dve.tensor_copy(s_nodeT[0:NB, :], bank[3][0:NB, 0:P]))
            dve.wait_ge(sm("steps_ready"), 1)
            for w, k in enumerate(SIDES):
                c(dve.tensor_scalar(first_node[k][:, :], bank[4 + w][:, 0:S], float(P), None, ALU.mult))
                c(dve.tensor_tensor(keep[k][:, 1:S], first_node[k][:, 1:S], first_node[k][:, 0:S - 1], ALU.is_equal))
                dve.tensor_scalar(limit[k][:, :], keep[k][:, :], BIG, FLOOR, ALU.mult, ALU.add)
                c(dve.scalar_tensor_tensor(s_step[k][0:1, :], first_node[k][0:1, :], -1.0 / P, iota_s[0:1, :], ALU.mult, ALU.add))
                if k == "dst":
                    dve.tensor_scalar(row_i[0:1, :], s_step[k][0:1, :], float(GE), float(E - GE), ALU.mult, ALU.min)
                c(dve.tensor_copy(group_i[k][0:1, :], s_step[k][0:1, :]))
                dve.sem_inc(sm("tables_ready"), 1)
                ins = dve.tensor_scalar(done[0:NB, w, :], first_node[k][0:NB, :], first_of[0:NB, 0:1], None, ALU.is_equal)
            ins.then_inc(sm("step_blocks_ready"), 1)
            dve.wait_ge(sm("step_scores_ready"), 1)
            for w, k in enumerate(SIDES):
                c(dve.tensor_copy(s_step[k][:, :], bank[w][:, 0:S]))
            dve.sem_inc(sm("step_scores_out"), 1)

            def score(i, off):
                n, k = i * U + off, off % U
                dve.wait_ge(sm(f"edges_in{k}"), (turns(i, off, U) + 1) * 16)
                if off >= 1:
                    dve.wait_ge(sm("scored"), n)
                for j in range(T):
                    ins = dve.scalar_tensor_tensor(prod[:, j, :], deal[:, k, j, 0:D], 1.0, w_edge[:, :], ALU.mult, ALU.mult,
                                                   accum_out=deal[:, k, j, SCORE:SCORE + 1])
                ins.then_inc(sm("scored"), 1)

            class Step:

                def __init__(self, walk, i, off):
                    self.walk, self.i, self.off = walk, i, off
                    self.n, self.m = i * BODY[walk] + off, i * BODY[walk] + off + BEFORE[walk]
                    self.b, self.k, self.o = off % 2, off % U, (off - 1) % U
                    self.now, self.old = slice(off % U, off % U + 1), slice((off - 1) % U, (off - 1) % U + 1)

                def nodes_of_edges(self):
                    walk, k = self.walk, self.k
                    if walk == "src":
                        of = source_rows(self.off)[:, :, SOURCE]
                        here_sem, count = source_rows_in(self.i, self.off)
                        dve.wait_ge(here_sem, count)
                    else:
                        of = ring_note[:, k, :, 1]
                        dve.wait_ge(sm(f"notes_in{k}"), (turns(self.i, self.off, U) + 1) * 16)
                    dve.tensor_scalar(local[:, self.b, :], of, first_node[walk][:, ds(self.n, 1)], None, ALU.subtract).then_inc(sm("walk_local"), 1)

                def whose(self):
                    if self.off >= 2:
                        dve.wait_ge(sm(f"{self.walk}_turned"), self.n - 1)
                    if self.walk == "dst" and self.off >= U:
                        dve.wait_ge(sm("dst_summed"), self.n - (U - 1))
                    dve.wait_ge(sm("walk_local"), self.m + 1)
                    dve.tensor_tensor(away[:, self.k, :, :], iota_n[:, :, :], pair(local[:, self.b, :], P, T), ALU.not_equal).then_inc(sm("walk_away"), 1)

                def scores(self):
                    each = source_rows(self.off)[:, :, SCORE] if self.walk == "src" else ring_note[:, self.k, :, 0]
                    dve.wait_ge(sm("walk_away"), self.m + 1)
                    dve.scalar_tensor_tensor(masked[:, self.b, :, :], away[:, self.k, :, :], -BIG, pair(each, P, T), ALU.mult, ALU.add).then_inc(sm(f"{self.walk}_scores_ready"), 1)

                def maxima(self):
                    dve.wait_ge(sm(f"{self.walk}_turned"), self.n + 1)
                    dve.reduce_max(mx[:, self.now], tbank[self.off % 3][:, :], AX.X).then_inc(sm("walk_max"), 1)

                def tops(self):
                    dve.wait_ge(sm("walk_max"), self.m + 1)
                    dve.scalar_tensor_tensor(top[:, self.now], top[:, self.old], limit[self.walk][:, ds(self.n, 1)], mx[:, self.now], ALU.min, ALU.max).then_inc(sm("walk_top"), 1)

                def lift(self):
                    dve.wait_ge(sm("walk_top"), self.m + 1)
                    dve.tensor_scalar(zneg[:, self.now], top[:, self.now], s_step[self.walk][:, ds(self.n, 1)], -1.0, ALU.add, ALU.mult).then_inc(sm("walk_zneg"), 1)

                def bend(self):
                    dve.wait_ge(sm("walk_zneg"), self.m + 1)
                    dve.scalar_tensor_tensor(least[:, self.now], zneg[:, self.now], SLOPE, zneg[:, self.now], ALU.mult, ALU.min).then_inc(sm("walk_least"), 1)

                def biases(self):
                    walk, k, now = self.walk, self.k, self.now
                    node, neg = s_step[walk][:, ds(self.n, 1)], least[:, now]
                    dve.wait_ge(sm("walk_least"), self.m + 1)
                    if walk == "dst":
                        dve.tensor_tensor(bias_hi[:, now], node, neg, ALU.add)
                        dve.scalar_tensor_tensor(bias_lo[:, now], node, SLOPE, neg, ALU.mult, ALU.add)
                    else:
                        dve.scalar_tensor_tensor(bias_hi[:, now], zneg[:, now], -SLOPE, neg, ALU.mult, ALU.add)
                        dve.tensor_scalar(bias_lo[:, now], top[:, now], -SLOPE, None, ALU.mult)
                    dve.tensor_scalar(shift[:, now], neg, least[:, self.old], limit[walk][:, ds(self.n, 1)], ALU.subtract, ALU.min).then_inc(sm(f"{walk}_bias_ready"), 1)

                def weights(self):
                    walk, n, b = self.walk, self.n, self.b
                    dve.wait_ge(sm(f"{walk}_exps_ready"), n + 1)
                    if self.off >= 2:
                        dve.wait_ge(sm(f"{walk}_turned_back"), n - 1)
                    dve.tensor_tensor(wT[:, b, :], exp_hi[:, b, :], exp_lo[:, b, :], ALU.max).then_inc(sm(f"{walk}_weights_ready"), 1)

                def add(self):
                    walk, n, r = self.walk, self.n, self.off % 3
                    dve.wait_ge(sm(f"{walk}_summed"), n + 1)
                    if self.off >= 3:
                        dve.wait_ge(sm(f"{walk}_sums_out{r}"), turns(self.i, self.off, 3, BODY[walk]) * 16)
                    if self.off >= 1:
                        dve.wait_ge(sm(f"{walk}_added"), n)
                    before = (self.off - 1) % 3
                    dve.tensor_copy(acc[:, r, LEAST:LEAST + 1], least[:, self.now])
                    if walk == "dst":
                        dve.scalar_tensor_tensor(acc[:, r, DEGREE:DEGREE + 1], acc[:, before, DEGREE:DEGREE + 1], keep[walk][:, ds(n, 1)], obank[self.b][:, DEGREE:DEGREE + 1], ALU.mult, ALU.add)
                    dve.scalar_tensor_tensor(acc[:, r, 0:D + 1], acc[:, before, 0:D + 1], corr[:, self.now], obank[self.b][:, 0:D + 1],
                                             ALU.mult, ALU.add).then_inc(sm(f"{walk}_added"), 1)

            def walk_step(walk, i, off, more=True):
                now = Step(walk, i, off)
                if isinstance(i, int) and off == 0:
                    for s in range(2):
                        first = Step(walk, i, s)
                        first.nodes_of_edges()
                        first.whose()
                        first.scores()
                later = Step(walk, i, off + 2)
                now.maxima()
                if more:
                    later.nodes_of_edges()
                now.tops()
                if more:
                    later.whose()
                now.lift()
                if more:
                    later.scores()
                now.bend()
                if off >= 1 and walk == "dst":
                    Step(walk, i, off - 1).weights()
                now.biases()
                if off >= BACK[walk] + 2:
                    Step(walk, i, off - BACK[walk] - 2).add()

            def walk_end(walk):
                if walk == "dst":
                    Step(walk, 0, S - 1).weights()
                for s in range(S - BACK[walk] - 2, S):
                    Step(walk, 0, s).add()

            def merged(i, off):
                hot_group(i, off, True)
                score(i, off)
                if off >= LAG:
                    walk_step("dst", i, off - LAG)

            for n in range(2 * U):
                merged(0, n)
            with dve.Fori(0, (G - 2 * U) // U) as i:
                for k in range(2 * U, 3 * U):
                    merged(i, k)
            merged(0, G - 1)
            for s in range(G - LAG, G - 1):
                walk_step("dst", 0, s)
            with dve.Fori(G // U - 1, S // U - 1) as i:
                for k in range(U, 2 * U):
                    walk_step("dst", i, k)
            for s in range(S // U * U, S):
                walk_step("dst", 0, s, s + 2 < S)
            walk_end("dst")

            for r in range(3):
                dve.wait_ge(sm(f"dst_sums_out{r}"), 16 * ((S - r + 2) // 3))
            for s in range(2 * U):
                walk_step("src", 0, s)
            with dve.Fori(0, S // (2 * U) - 1) as i:
                for k in range(2 * U, 4 * U):
                    walk_step("src", i, k)
            for s in range(S // (2 * U) * (2 * U), S):
                walk_step("src", 0, s, s + 2 < S)
            walk_end("src")

            def first_nodes(i, off):
                it = i + off
                chunk = ds(it * CH, CH)
                c = Chain(dve, "first_nodes", it * 15)
                dve.wait_ge(sm("chunk_in"), it * (32 * CH) + 32 * CH)
                c(dve.tensor_tensor(small[:, 0, :], part["src"][:, :, LEAST], part["dst"][:, :, LEAST], ALU.min))
                for w, k in enumerate(SIDES):
                    ins = dve.tensor_tensor(scale2[:, w, :], small[:, 0, :], part[k][:, :, LEAST], ALU.subtract)
                ins.then_inc(sm("merge_ready"), 1)
                c(dve.tensor_scalar(small[:, 3, :], part["dst"][:, :, DEGREE], 1.0, None, ALU.add))
                dve.sem_inc(sm("deg_ready"), 1)
                dve.wait_ge(sm("merge_exp"), it + 1)
                for w, k in enumerate(SIDES):
                    c(dve.tensor_tensor(part[k][:, :, :], part[k][:, :, :], spread(scale2[:, w, :], CH, ROW), ALU.mult))
                c(dve.tensor_tensor(part["src"][:, :, :], part["src"][:, :, :], part["dst"][:, :, :], ALU.add))
                weight = part["src"][:, :, ONE]
                dve.wait_ge(sm("dinv_ready"), it + 1)
                dve.tensor_scalar(dinv[:, chunk], small[:, 0, :], 1.0, None, ALU.mult)
                c(dve.scalar_tensor_tensor(small[:, 1, :], weight, 0.0, weight, ALU.is_equal, ALU.add))
                c(dve.reciprocal(small[:, 2, :], small[:, 1, :]))
                c(dve.tensor_scalar(small[:, 3, :], weight, 0.0, 1.0, ALU.is_equal, ALU.add))
                if off:
                    dve.wait_ge(sm("table_out"), it * 16)
                c(dve.tensor_tensor(agg[:, :, :], part["src"][:, :, 0:D], spread(small[:, 2, :], CH, D), ALU.mult))
                dve.sem_inc(sm("chunk_used"), 1)
                dve.tensor_tensor(sq[:, :, :], nodes[:, chunk, :], spread(small[:, 3, :], CH, D), ALU.mult).then_inc(sm("agg_ready"), 1)
                dve.wait_ge(sm("gelu_done"), it + 1)
                c(dve.tensor_tensor(sq[:, :, :], sq[:, :, :], agg[:, :, :], ALU.add))
                c(dve.reduce_sum(small[:, 4, :], sq[:, :, :], AX.X))
                c(dve.tensor_scalar(small[:, 4, :], small[:, 4, :], -1.0 / D, None, ALU.mult))
                c(dve.tensor_tensor(sq[:, :, :], sq[:, :, :], spread(small[:, 4, :], CH, D), ALU.add))
                c(dve.tensor_tensor(agg[:, :, :], sq[:, :, :], sq[:, :, :], ALU.mult))
                c(dve.reduce_sum(small[:, 5, :], agg[:, :, :], AX.X))
                dve.tensor_scalar(small[:, 6, :], small[:, 5, :], 1.0 / D, EPS, ALU.mult, ALU.add).then_inc(sm("var_ready"), 1)
                dve.wait_ge(sm("rstd_ready"), it + 1)
                dve.tensor_tensor(sq[:, :, :], sq[:, :, :], spread(small[:, 7, :], CH, D), ALU.mult).then_inc(sm("first_result_ready"), 1)
                dve.wait_ge(sm("first_result_ready"), it + 1)
                dve.tensor_scalar(nodes[:, chunk, :], sq[:, :, :], 1.0, None, ALU.mult)
                dve.wait_ge(sm("result_turned"), it + 1)
                dve.tensor_copy(wT[:, 0, :], tbank[0][:, :])
                dve.tensor_copy(wT[:, 1, 0:(CH - T) * P], tbank[1][:, 0:(CH - T) * P]).then_inc(sm("result_copied"), 1)
                dve.wait_ge(sm("projection_ready"), it + 1)
                dve.tensor_tensor(agg[:, 0:T, :], qbank[0][:, :].rearrange("p (j f) -> p j f", f=D), spread(dinv[:, ds(it * CH, T)], T, D), ALU.mult)
                dve.tensor_tensor(agg[:, T:CH, :], qbank[1][:, 0:(CH - T) * P].rearrange("p (j f) -> p j f", f=D),
                                  spread(dinv[:, ds(it * CH + T, CH - T)], CH - T, D), ALU.mult).then_inc(sm("projected"), 1)

            first_nodes(0, 0)
            with dve.Fori(0, NCH - 1) as i:
                first_nodes(i, 1)

            def hot_targets(i, off):
                n, b, k = i * U + off, off % 2, off % U
                dve.wait_ge(sm(f"notes_in{k}"), (turns(i, off, U) + 1) * 16 + 16 * fillings(k, S))
                dve.tensor_scalar(local[:, b, :], ring_note[:, k, :, 1], first_node["dst"][:, ds(n, 1)], None, ALU.subtract).then_inc(sm("msg_local"), 1)
                if off >= 2:
                    dve.wait_ge(sm("msg_summed"), n - 1)
                dve.wait_ge(sm("msg_local"), n + 1)
                dve.tensor_tensor(hot_rows[:, b, :, :], pair(iota_f[:, :], T, P), spread(local[:, b, :], T, P), ALU.is_equal).then_inc(sm("msg_hot"), 1)

            def add_messages(i, off):
                n, b, r = i * U + off, off % 2, off % 3
                dve.wait_ge(sm("msg_summed"), n + 1)
                if off >= 3:
                    dve.wait_ge(sm(f"msg_sums_out{r}"), turns(i, off, 3) * 16)
                if off >= 1:
                    dve.wait_ge(sm("msg_added"), n)
                dve.scalar_tensor_tensor(acc[:, r, 0:D], acc[:, (off - 1) % 3, 0:D], keep["dst"][:, ds(n, 1)], obank[b][:, 0:D], ALU.mult, ALU.add).then_inc(sm("msg_added"), 1)

            for r in range(3):
                dve.wait_ge(sm(f"src_sums_out{r}"), 16 * ((S - r + 2) // 3))
            for s in range(U):
                hot_targets(0, s)
                if s:
                    add_messages(0, s - 1)
            with dve.Fori(0, S // U - 1) as i:
                for k in range(U, 2 * U):
                    hot_targets(i, k)
                    add_messages(i, k - 1)
            for s in range(S // U * U, S):
                hot_targets(0, s)
                add_messages(0, s - 1)
            add_messages(0, S - 1)

            def second_nodes(i, off):
                it = i + off
                chunk = ds(it * CH, CH)
                c = Chain(dve, "second_nodes", it * 9)
                if off:
                    dve.wait_ge(sm("result_ready"), it)
                dve.wait_ge(sm("chunk2_in"), it * (16 * (CH + 1)) + 16 * (CH + 1))
                c(dve.tensor_tensor(sq[:, :, :], part["src"][:, :, 0:D], part["dst"][:, :, 0:D], ALU.add))
                dve.sem_inc(sm("chunk_used"), 1)
                c(dve.tensor_tensor(sq[:, :, :], sq[:, :, :], spread(dinv[:, chunk], CH, D), ALU.mult))
                c(dve.tensor_tensor(sq[:, :, :], sq[:, :, :], pair(out_bias[:, :], CH, D), ALU.add))
                c(dve.scalar_tensor_tensor(sq[:, :, :], sq[:, :, :], 0.0, nodes[:, chunk, :], ALU.max, ALU.add))
                c(dve.reduce_sum(small[:, 4, :], sq[:, :, :], AX.X))
                c(dve.tensor_scalar(small[:, 4, :], small[:, 4, :], -1.0 / D, None, ALU.mult))
                c(dve.tensor_tensor(sq[:, :, :], sq[:, :, :], spread(small[:, 4, :], CH, D), ALU.add))
                if off:
                    dve.wait_ge(sm("result_out"), it * 16)
                c(dve.tensor_tensor(agg[:, :, :], sq[:, :, :], sq[:, :, :], ALU.mult))
                c(dve.reduce_sum(small[:, 5, :], agg[:, :, :], AX.X))
                dve.tensor_scalar(small[:, 6, :], small[:, 5, :], 1.0 / D, EPS, ALU.mult, ALU.add).then_inc(sm("var_ready"), 1)
                dve.wait_ge(sm("rstd_ready"), it + (NCH + 1))
                dve.tensor_tensor(agg[:, :, :], sq[:, :, :], spread(small[:, 7, :], CH, D), ALU.mult).then_inc(sm("result_ready"), 1)

            second_nodes(0, 0)
            with dve.Fori(0, NCH - 1) as i:
                second_nodes(i, 1)

    return nc


_INS = ["x", "src", "dst", "edge_attr_128", "L0_gnn_W_att_w", "L0_gnn_W_att_b", "L1_gnn_W", "L1_gnn_b"]


def kernel(**inputs):
    import numpy as _np
    import concourse.bacc as _bacc
    from concourse import mybir as _mybir
    from concourse.bass_utils import run_bass_kernel_spmd as _run

    nc = _bacc.Bacc("TRN2", target_bir_lowering=False, num_devices=1)
    arrays, args = {}, []
    for name in _INS:
        a = _np.ascontiguousarray(inputs[name])
        arrays[f"in_{name}"] = a
        args.append(nc.dram_tensor(f"in_{name}", a.shape, _mybir.dt.from_np(a.dtype), kind="ExternalInput").ap())
    args.append(nc.dram_tensor("out_nodes", (N, D), F32, kind="ExternalOutput").ap())
    resnorm_gnn_kernel(nc, *args)
    return _run(nc, [arrays], core_ids=[0]).results[0]["out_nodes"]
```

```python
import concourse.bass as bass
from concourse import mybir
from contextlib import ExitStack

F32, BF16, I32 = mybir.dt.float32, mybir.dt.bfloat16, mybir.dt.int32
ALU = mybir.AluOpType
ACT = mybir.ActivationFunctionType
AX = mybir.AxisListType

P = 128
N, E, D = 12500, 200000, 128
NB = -(-N // P)
LAST_NODES = N - (NB - 1) * P
T = 4
GE = P * T
G = -(-E // GE)
E_PAD = G * GE
AGAIN = E_PAD - E
AGAIN_P = AGAIN // T
S = G + NB - 1
ROW = D + 4
ONE, SCORE, SOURCE = D, D + 1, D + 2
LEAST, DEGREE = D + 1, D + 2
NO_NODE = NB * P
BIG = 1e30
FLOOR = -1e20
SLOPE, EPS = 0.2, 1e-5
LIFT = 2.0 ** 20
U = 6
BODY = {"dst": U, "src": 2 * U}
BACK = {"dst": 1, "src": 2}
LAG = 5
CH = 7
NCH = NB // CH
R = 98
Q = -(-G // R)
OP, OC = 125, 1600
LOG_P, LOG_GE = P.bit_length() - 1, GE.bit_length() - 1
assert AGAIN_P * T == AGAIN and NB % CH == 0 and OP * OC == E and E < LIFT and NB < R + 1
assert (S - 2) % U == 0 and U % 2 == 0 and U % 3 == 0 and (G - 2 * U) % U == 1 and (S - G + 1) % U == 2


def resnorm_gnn_kernel(nc, x, src, dst, edge_attr, att_w, att_b, w1, b1, out):
    ctx = ExitStack()
    with ctx:
        def sb(name, shape, dt=F32):
            return ctx.enter_context(nc.sbuf_tensor(name, shape, dt))

        def pb(name, shape, dt=F32):
            return ctx.enter_context(nc.psum_tensor(name, shape, dt))

        def dram(name, shape, dt=F32):
            return nc.dram_tensor(name, shape, dt)

        ds = bass.ds
        SIDES = ("src", "dst")
        BEFORE = {"dst": 0, "src": S}
        given = {"src": src, "dst": dst, "edges": edge_attr}

        ordered = {"src": dram("ordered_src", (E, 1), I32), "dst": dram("ordered_dst", (E, 1), I32),
                   "edges": dram("ordered_edges", (E, D))}
        by_source = dram("rows_by_source", (E_PAD, ROW))
        notes = dram("notes_by_target", (2, E_PAD))
        messages = dram("messages", (E_PAD, D))
        sums = {k: dram(f"sums_{k}", (S, P, ROW)) for k in ("src", "dst", "msg")}
        table = dram("projected_nodes", ((NB + 1) * P, D))

        iota_f = sb("iota_f", [P, P])
        iota_p = sb("iota_p", [P, 1])
        iota_s = sb("iota_s", [P, S])
        minus_big = sb("minus_big", [P, P], BF16)
        iota_n = sb("iota_n", [P, P, T], BF16)
        iota_b = sb("iota_b", [P, NB, T], BF16)
        ident = sb("ident", [P, P])
        lifted = sb("lifted", [P, P], BF16)
        lower = sb("lower", [P, P], BF16)
        rest = sb("rest", [P, P], BF16)
        below = sb("below", [P, P])
        ones = sb("ones", [P, 512])
        onesb = sb("onesb", [P, P], BF16)
        counts = sb("counts", [P, 2], BF16)
        half_n = sb("half_n", [P, CH])
        minus_lift = sb("minus_lift", [P, 1])
        spare = sb("spare", [P, T])
        nodes = sb("nodes", [P, NB, D])
        w_node = sb("w_node", [P, D])
        w_edge = sb("w_edge", [P, D])
        att_bias = sb("att_bias", [P, 1])
        w_proj = sb("w_proj", [P, D])
        out_bias = sb("out_bias", [P, D])
        here = sb("here", [P, OC], I32)
        there = sb("there", [P, OC], I32)
        unsorted = sb("unsorted", [P, 1])
        flag_i = sb("flag_i", [1, 1], I32)
        lying = {k: sb(f"lying_{k}", [R, Q, GE], I32) for k in SIDES}
        ids = {k: sb(f"ids_{k}", [P, Q * R * T]) for k in SIDES}
        blk = sb("blk", [P, Q * R * T], BF16)
        hot = sb("hot", [P, 3, NB, T], BF16)
        total = sb("total", [P, NB, T])
        upto = sb("upto", [P, NB, T])
        ends_i = sb("ends_i", [R, Q], I32)
        ends = sb("ends", [R, Q])
        passed = sb("passed", [R, Q, NB])
        cum_i = sb("cum_i", [P, NB], I32)
        last = {k: sb(f"last_{k}", [P, NB]) for k in SIDES}
        last_col = {k: sb(f"last_col_{k}", [P, 1]) for k in SIDES}
        last_i = {k: sb(f"last_i_{k}", [1, NB], I32) for k in SIDES}
        done = sb("done", [P, 2, S])
        first_of = sb("first_of", [P, 1])
        first_node = {k: sb(f"first_node_{k}", [P, S]) for k in SIDES}
        keep = {k: sb(f"keep_{k}", [P, S]) for k in SIDES}
        limit = {k: sb(f"limit_{k}", [P, S]) for k in SIDES}
        group_i = {k: sb(f"group_i_{k}", [1, S], I32) for k in SIDES}
        row_i = sb("row_i", [1, S], I32)
        s_node = sb("s_node", [P, NB])
        s_nodeT = sb("s_nodeT", [P, P])
        s_step = {k: sb(f"s_step_{k}", [P, S]) for k in SIDES}
        dinv = sb("dinv", [P, NB])
        deal = sb("deal", [P, U, T, ROW])
        prod = sb("prod", [P, T, D])
        picked = sb("picked", [P, T, NB])
        posf = sb("posf", [P, 2, T])
        pos = sb("pos", [P, U, T], I32)
        note = sb("note", [P, U, 2, T])
        ring = sb("ring", [P, U, T, ROW])
        ring_target = sb("ring_target", [P, U, T])
        local = sb("local", [P, 2, T], BF16)
        away = sb("away", [P, U, P, T], BF16)
        masked = sb("masked", [P, 2, P, T])
        hot_rows = masked[:, :, :, :].rearrange("p b n j -> p b (n j)").rearrange("p b (j n) -> p b j n", j=T)
        mx = sb("mx", [P, U])
        top = sb("top", [P, U])
        zneg = sb("zneg", [P, U])
        least = sb("least", [P, U])
        bias_hi = sb("bias_hi", [P, U])
        bias_lo = sb("bias_lo", [P, U])
        shift = sb("shift", [P, U])
        corr = sb("corr", [P, U])
        exp_hi = sb("exp_hi", [P, 2, GE])
        exp_lo = sb("exp_lo", [P, 2, GE])
        wT = sb("wT", [P, 2, GE])
        wgt = sb("wgt", [P, 2, GE])
        acc = sb("acc", [P, U, ROW])
        both = sb("both", [P, 2, CH, ROW])
        turn_of = (both[:, :, :, :], ring[:, :, :, :].rearrange("p u j f -> p (u j f)")[:, 0:2 * CH * ROW].rearrange("p (w b f) -> p w b f", w=2, b=CH))
        score_row = both[0:1, :, :, :].rearrange("p w b f -> p (w b f)")[:, 0:3 * GE].rearrange("p (s e) -> p s e", s=3)
        parts = [{k: t[:, w, :, :] for w, k in enumerate(SIDES)} for t in turn_of]
        projected = deal[:, :, :, :].rearrange("p u j f -> p (u j f)")[:, 0:2 * CH * D].rearrange("p (s b f) -> p s b f", s=2, b=CH)
        apart = both[:, :, :, :].rearrange("p w b f -> p (w b f)")[:, 0:OC]
        small = sb("small", [P, 8, CH])
        keeps = sb("keeps", [P, CH])
        dinv_now = sb("dinv_now", [P, 2, CH])
        scale2 = sb("scale2", [P, 2, CH])
        agg = sb("agg", [P, CH, D])
        sq = exp_lo[:, :, :].rearrange("p b e -> p (b e)")[:, 0:CH * D].rearrange("p (b f) -> p b f", f=D)

        bank = [pb(f"bank{i}", [P, 512]) for i in range(8)]
        tbank, qbank, obank = (bank[0], bank[1], bank[6]), bank[2:4], bank[4:6]
        placebank = bank[7]
        places = placebank[:, 0:NB * T].rearrange("p (b j) -> p b j", j=T)

        sems = {}

        def sm(name):
            if name not in sems:
                sems[name] = ctx.enter_context(nc.semaphore(name))
            return sems[name]

        def pair(view, n, k):
            return view.unsqueeze(1).to_broadcast([view.shape[0], n, k])

        def spread(view, n, k):
            return view.unsqueeze(2).to_broadcast([view.shape[0], n, k])

        def turns(i, off, m, body=U):
            return i * (body // m) + off // m

        def fillings(k, n):
            return (n - 1 - k) // U + 1

        def source_rows(off):
            return (ring if off % (2 * U) < U else deal)[:, off % U, :, :]

        def source_rows_in(i, off):
            k, count = off % U, (turns(i, off, 2 * U, 2 * U) + 1) * 16
            if off % (2 * U) < U:
                return sm(f"rows_in{k}"), count + 16 * fillings(k, S)
            return sm(f"edges_in{k}"), count + 16 * fillings(k, G)

        def sums_before(walk, r):
            return ("dst", "src", "msg", "end").index(walk) * 16 * fillings(r, S)

        def before_messages(k):
            return 16 * fillings(k, S) + 16 * ((S - 1 - k) // (2 * U) + 1)

        def rows_of(view):
            return view.rearrange("a p f -> (a p) f")

        class Chain:

            def __init__(self, eng, name, base=0):
                self.eng, self.sem, self.n = eng, sm(name), base

            def __call__(self, ins):
                self.n = self.n + 1
                ins.then_inc(self.sem, 1)
                self.eng.wait_ge(self.sem, self.n)

        score_rows = notes[0:1, :].rearrange("a (g e) -> g a e", e=GE)
        target_groups = notes[1, :].rearrange("(g p j) -> g p j", p=P, j=T)
        note_groups = notes[:, :].rearrange("f (g p j) -> g p f j", p=P, j=T)
        source_groups = by_source[:, :].rearrange("(g p j) f -> g p (j f)", p=P, j=T)
        message_groups = messages[:, :].rearrange("(g p j) f -> g p (j f)", p=P, j=T)
        table_blocks = table[0:NB * P, :].rearrange("(b p) f -> p b f", p=P)
        TAIL = E - 1 - P * (OC - T * 10)
        CHECK = OC - T * 10
        TAIL_P, TAIL_C = 29, 11
        assert TAIL == TAIL_P * TAIL_C and CHECK + TAIL_C <= OC

        block = ctx.enter_context(nc.Block())

        @block.sync
        def _(sp):
            sp.wait_ge(sm("pads_set"), 5)
            for t, a in ((here, 0), (there, 1)):
                sp.dma_start(t[:, 0:CHECK], dst[a:a + P * CHECK].rearrange("(p c) -> p c", p=P)).then_inc(sm("check_in"), 16)
                sp.dma_start(t[0:TAIL_P, CHECK:CHECK + TAIL_C], dst[P * CHECK + a:P * CHECK + a + TAIL].rearrange("(p c) -> p c", c=TAIL_C)).then_inc(sm("check_in"), 16)
            sp.dma_start(w_node[:, :], att_w[0:D].partition_broadcast(P)).then_inc(sm("weights_in"), 16)
            sp.dma_start(w_edge[:, :], att_w[D:2 * D].partition_broadcast(P)).then_inc(sm("weights_in"), 16)
            sp.dma_start(att_bias[:, :], att_b[0:1].partition_broadcast(P)).then_inc(sm("weights_in"), 16)
            sp.dma_start(w_proj[:, :], w1[:, :]).then_inc(sm("weights_in"), 16)
            sp.dma_start(out_bias[:, :], b1[:].partition_broadcast(P)).then_inc(sm("weights_in"), 16)
            sp.dma_start(nodes[:, 0:NB - 1, :], x[0:(NB - 1) * P, :].rearrange("(b p) f -> p b f", p=P)).then_inc(sm("nodes_in"), 16)
            sp.dma_start(nodes[0:LAST_NODES, NB - 1, :], x[(NB - 1) * P:N, :]).then_inc(sm("nodes_in"), 16)
            sp.dma_start(table[NB * P:(NB + 1) * P, :], agg[:, 0, :]).then_inc(sm("no_node_out"), 16)

            sp.wait_ge(sm("flag_ready"), 1)
            flag = sp.to_reg(sp.value_load(flag_i[0:1, 0:1], min_val=0, max_val=P))

            with sp.If_ne(flag, 0):
                sp.dma_start(here[0:OP, :], dst[:].rearrange("(p c) -> p c", p=OP)).then_inc(sm("order_ids"), 16)
                sp.dma_start(there[0:OP, :], src[:].rearrange("(p c) -> p c", p=OP)).then_inc(sm("order_ids"), 16)
                columns = edge_attr[:, :].rearrange("(p c) f -> p c f", p=OP)
                sp.dma_start(prod[0:OP, 0, :], columns[:, 0, :]).then_inc(sm("order_in"), 16)
                with sp.Fori(1, OC) as c:
                    for what in ("edges", "dst", "src"):
                        sp.wait_ge(sm(f"order_out_{what}"), c * 16)
                    sp.sem_inc(sm("waited"), 1)
                    sp.dma_start(prod[0:OP, 0, :], columns[:, ds(c, 1), :].rearrange("p a f -> p (a f)")).then_inc(sm("order_in"), 16)
                for what in ("edges", "dst", "src"):
                    sp.wait_ge(sm(f"order_out_{what}"), OC * 16)

            def of_edges(make):
                with sp.If_eq(flag, 0):
                    make(given)
                with sp.Else():
                    make(ordered)

            def load_numbers(a):
                for k in SIDES:
                    ids_1d = a[k][:] if a is given else a[k][:, :].rearrange("e a -> (e a)")
                    sp.dma_start(lying[k][:, 0:Q - 1, :], ids_1d[0:(Q - 1) * R * GE].rearrange("(q r c) -> r q c", q=Q - 1, r=R)).then_inc(sm("numbers_in"), 16)
                    sp.dma_start(lying[k][0:G - 1 - (Q - 1) * R, Q - 1, :], ids_1d[(Q - 1) * R * GE:(G - 1) * GE].rearrange("(r c) -> r c", c=GE)).then_inc(sm("numbers_in"), 16)
                    sp.dma_start(lying[k][G - 1 - (Q - 1) * R:G - (Q - 1) * R, Q - 1, :], ids_1d[E - GE:E].rearrange("(r c) -> r c", c=GE)).then_inc(sm("numbers_in"), 16)

            of_edges(load_numbers)

            def edges(a, i, off):
                k, n = off % U, i * U + off
                if off >= U:
                    sp.wait_ge(sm(f"dealt{k}"), turns(i, off, U) * (16 * T))
                if isinstance(n, int):
                    row = min(n * GE, E - GE)
                    view = a["edges"][row:row + GE, :].rearrange("(p j) f -> p j f", j=T)
                else:
                    view = a["edges"][0:(G - 1) * GE, :].rearrange("(g p j) f -> g p j f", p=P, j=T)[ds(n, 1), :, :, :].rearrange("a p j f -> (a p) j f")
                sp.dma_start(deal[:, k, :, 0:D], view).then_inc(sm(f"edges_in{k}"), 16)

            def load_notes(i, off):
                k, n = off % U, i * U + off
                if off >= 3:
                    sp.wait_ge(sm("dst_turned"), n - 2)
                    sp.sem_inc(sm("waited"), 1)
                g = sp.value_load(group_i["dst"][0:1, ds(n, 1)], min_val=0, max_val=G - 1)
                sp.dma_start(ring_target[:, k, :], rows_of(target_groups[ds(g, 1), :, :])).then_inc(sm(f"notes_in{k}"), 16)
                sp.dma_start(score_row[:, off % 3, :], score_rows[ds(g, 1), :, :].rearrange("g a e -> (g a) e")).then_inc(sm(f"notes_in{k}"), 16)

            def load_rows(a, i, off):
                k, n = off % U, i * U + off
                if off >= U:
                    sp.wait_ge(sm("dst_summed"), n - (U - 1))
                    sp.sem_inc(sm("waited"), 1)
                row = sp.value_load(row_i[0:1, ds(n, 1)], min_val=0, max_val=E - GE)
                sp.dma_start(ring[:, k, :, 0:D], a["edges"][ds(row, GE), :].rearrange("(p j) f -> p j f", j=T)).then_inc(sm(f"rows_in{k}"), 16)

            def store_sums(walk, i, off, width):
                n, r = i * BODY.get(walk, U) + off, off % U
                sp.wait_ge(sm(f"{walk}_added"), n + 1)
                sp.dma_start(rows_of(sums[walk][ds(n, 1), :, 0:width]), acc[:, r, 0:width]).then_inc(sm(f"sums_out{r}"), 16)

            def notes_written(i, off):
                sp.wait_ge(sm(f"note_out{off % U}"), (turns(i, off, U) + 1) * 16)
                if off >= U:
                    sp.sem_inc(sm("waited"), 1)

            def merged(a, i, off):
                if not isinstance(i, int) or off + 2 < G:
                    edges(a, i, off + 2)
                if off >= 2:
                    notes_written(i, off - 2)
                    load_notes(i, off - 2)
                if off >= 4:
                    load_rows(a, i, off - 4)

            def rest_step(a, i, off):
                if not isinstance(i, int) or off < S:
                    load_notes(i, off)
                load_rows(a, i, off - 2)

            sp.wait_ge(sm("tables_ready"), 2)

            def walk_by_target(a):
                edges(a, 0, 0)
                edges(a, 0, 1)
                for n in range(2 * U):
                    merged(a, 0, n)
                with sp.Fori(0, (G - 2 * U) // U - 1) as i:
                    for k in range(2 * U, 3 * U):
                        merged(a, i, k)
                for n in range(G - 1 - U, G):
                    merged(a, 0, n)
                notes_written(0, G - 2)
                notes_written(0, G - 1)
                rest_step(a, 0, G - 2)
                with sp.Fori(G // U - 2, S // U - 2) as i:
                    for k in range(2 * U, 3 * U):
                        rest_step(a, i, k)
                for s in range(S // U * U, S + 2):
                    rest_step(a, 0, s)

            of_edges(walk_by_target)

            for k in range(U):
                sp.wait_ge(sm(f"dealt{k}"), ((G - 1 - k) // U + 1) * (16 * T))
            sp.wait_ge(sm("dst_summed"), S)

            def load_by_source(i, off):
                n = i * (2 * U) + off
                if off >= 2 * U:
                    sp.wait_ge(sm("src_summed"), n - (2 * U - 1))
                    sp.sem_inc(sm("waited"), 1)
                g = sp.value_load(group_i["src"][0:1, ds(n, 1)], min_val=0, max_val=G - 1)
                sp.dma_start(source_rows(off).rearrange("p j f -> p (j f)"), rows_of(source_groups[ds(g, 1), :, :])).then_inc(source_rows_in(i, off)[0], 16)

            AFTER = 2 * U + 2

            def source_step(i, off):
                load_by_source(i, off)
                if off >= AFTER:
                    store_sums("src", i, off - AFTER, ROW)

            for s in range(4 * U):
                source_step(0, s)
            with sp.Fori(0, S // (2 * U) - 2) as i:
                for k in range(4 * U, 6 * U):
                    source_step(i, k)
            for s in range(S // (2 * U) * (2 * U), S):
                source_step(0, s)
            for s in range(S - AFTER, S):
                store_sums("src", 0, s, ROW)

            for r in range(U):
                sp.wait_ge(sm(f"sums_out{r}"), sums_before("msg", r))

            def sums_in(i, off):
                it, slot = i * 2 + off, off % 2
                if off >= 2:
                    sp.wait_ge(sm("chunk_used"), it - 1)
                    sp.sem_inc(sm("waited"), 1)
                for k in SIDES:
                    for j in range(CH):
                        at = sp.value_load(last_i[k][0:1, ds(it * CH + j, 1)], min_val=0, max_val=S - 1)
                        sp.dma_start(parts[slot][k][:, j, :], rows_of(sums[k][ds(at, 1), :, :])).then_inc(sm(f"chunk_in{slot}"), 16)

            sums_in(0, 0)
            sums_in(0, 1)
            with sp.Fori(0, NCH // 2 - 1) as i:
                for off in (2, 3):
                    sums_in(i, off)

            def load_messages(i, off):
                k, n = off % U, i * U + off
                if off >= U:
                    sp.wait_ge(sm("msg_summed"), n - (U - 1))
                    sp.sem_inc(sm("waited"), 1)
                g = sp.value_load(group_i["dst"][0:1, ds(n, 1)], min_val=0, max_val=G - 1)
                sp.wait_ge(sm("messages_stored"), g + 1)
                sp.dma_start(ring[:, k, :, 0:D], message_groups[ds(g, 1), :, :].rearrange("a p (j f) -> (a p) j f", j=T)).then_inc(sm(f"rows_in{k}"), 16)
                sp.dma_start(ring_target[:, k, :], rows_of(target_groups[ds(g, 1), :, :])).then_inc(sm(f"notes_in{k}"), 16)

            def message_step(i, off):
                load_messages(i, off)
                if off >= 3:
                    store_sums("msg", i, off - 3, D)

            for s in range(U):
                message_step(0, s)
            with sp.Fori(0, S // U - 1) as i:
                for k in range(U, 2 * U):
                    message_step(i, k)
            for s in range(S // U * U, S):
                message_step(0, s)
            for s in range(S - 3, S):
                store_sums("msg", 0, s, D)

            for r in range(U):
                sp.wait_ge(sm(f"sums_out{r}"), sums_before("end", r))

            def messages_in(i, off):
                it, slot = i * 2 + off, off % 2
                if off >= 2:
                    sp.wait_ge(sm("chunk_used"), it + (NCH - 1))
                    sp.sem_inc(sm("waited"), 1)
                for j in range(CH):
                    at = sp.value_load(last_i["dst"][0:1, ds(it * CH + j, 1)], min_val=0, max_val=S - 1)
                    sp.dma_start(parts[slot]["src"][:, j, 0:D], rows_of(sums["msg"][ds(at, 1), :, 0:D])).then_inc(sm(f"chunk_in{slot}"), 16)
                sp.dma_start(parts[slot]["dst"][:, :, 0:D], table_blocks[:, ds(it * CH, CH), :]).then_inc(sm(f"chunk_in{slot}"), 16)

            def result_out(i, off):
                it = i * 2 + off
                sp.wait_ge(sm("result_ready"), it + 1)
                sp.dma_start(out[0:(NCH - 1) * CH * P, :].rearrange("(b p) f -> p b f", p=P)[:, ds(it * CH, CH), :], agg[:, :, :]).then_inc(sm("result_out"), 16)

            messages_in(0, 0)
            messages_in(0, 1)
            with sp.Fori(0, NCH // 2 - 1) as i:
                for off in (2, 3):
                    messages_in(i, off)
                    result_out(i, off - 2)
            result_out(0, NCH - 2)
            sp.wait_ge(sm("result_ready"), NCH)
            b0 = (NCH - 1) * CH
            sp.dma_start(out[b0 * P:(NB - 1) * P, :].rearrange("(b p) f -> p b f", p=P), agg[:, 0:CH - 1, :]).then_inc(sm("result_out"), 16)
            sp.dma_start(out[(NB - 1) * P:N, :], agg[0:LAST_NODES, CH - 1, :]).then_inc(sm("result_out"), 16)
            sp.wait_ge(sm("no_node_out"), 16)
            sp.wait_ge(sm("result_out"), 16 * (NCH + 1))

        @block.gpsimd
        def _(pool):
            loose = dict(allow_small_or_imprecise_dtypes=True)
            pool.iota(iota_f[:, :], [[1, P]], base=0, channel_multiplier=0, **loose).then_inc(sm("iotas"), 1)
            pool.iota(iota_p[:, :], [[0, 1]], base=0, channel_multiplier=1, **loose).then_inc(sm("iotas"), 1)
            pool.iota(iota_s[:, :], [[1, S]], base=0, channel_multiplier=0, **loose).then_inc(sm("iotas"), 1)
            pool.iota(iota_b[:, :, :], [[1, NB], [0, T]], base=0, channel_multiplier=0, **loose).then_inc(sm("iotas"), 1)
            pool.iota(iota_n[:, :, :], [[1, P], [0, T]], base=0, channel_multiplier=0, **loose).then_inc(sm("iotas"), 1)
            pool.iota(spare[:, :], [[1, T]], base=E, channel_multiplier=T, **loose).then_inc(sm("iotas"), 1)
            pool.memset(half_n[:, :], -0.5).then_inc(sm("iotas"), 1)

            pool.wait_ge(sm("flag_ready"), 1)
            flag = pool.to_reg(pool.value_load(flag_i[0:1, 0:1], min_val=0, max_val=P))
            with pool.If_ne(flag, 0):
                with pool.Fori(0, OC) as c:
                    pool.wait_ge(sm("order_placed"), c + 1)
                    pool.wait_ge(sm("order_in"), c * 16 + 16)
                    pool.sem_inc(sm("waited"), 1)
                    place = bass.IndirectOffsetOnAxis(ap=pos[0:OP, 0, 0:1], axis=0)
                    for what, of in (("edges", prod[0:OP, 0, :]), ("dst", pos[0:OP, 0, 1:2]), ("src", pos[0:OP, 0, 2:3])):
                        pool.indirect_dma_start(out=ordered[what][:, :], out_offset=place, in_=of, in_offset=None).then_inc(sm(f"order_out_{what}"), 16)

            def deal_out(i, off):
                n, k = i * U + off, off % U
                pool.wait_ge(sm("sources_in_rows"), n + 1)
                pool.wait_ge(sm("placed"), n + 1)
                pool.sem_inc(sm("waited"), 1)
                for j in range(T):
                    pool.indirect_dma_start(
                        out=by_source[:, :], out_offset=bass.IndirectOffsetOnAxis(ap=pos[:, k, j:j + 1], axis=0),
                        in_=deal[:, k, j, :], in_offset=None).then_inc(sm(f"dealt{k}"), 16)

            with pool.Fori(0, G // U) as i:
                for k in range(U):
                    deal_out(i, k)
            for n in range(G // U * U, G):
                deal_out(0, n)

            def weights(i, off):
                n, b = i * U + off, off % 2
                if off >= 2:
                    pool.wait_ge(sm("src_turned_back"), n - 1)
                pool.wait_ge(sm("src_exps_ready"), n + 1)
                pool.tensor_tensor(wT[:, b, :], exp_hi[:, b, :], exp_lo[:, b, :], ALU.mult).then_inc(sm("src_weights_ready"), 1)

            for s in range(U):
                weights(0, s)
            with pool.Fori(0, S // U - 1) as i:
                for k in range(U, 2 * U):
                    weights(i, k)
            for s in range(S // U * U, S):
                weights(0, s)

            pool.wait_ge(sm("iotas"), 7)
            with pool.Fori(0, NCH) as it:
                pool.wait_ge(sm("deg_ready"), it + 1)
                pool.tensor_tensor(dinv[:, ds(it * CH, CH)], small[:, 3, :], half_n[:, :], ALU.pow).then_inc(sm("dinv_ready"), 1)
                pool.wait_ge(sm("var_ready"), it + 1)
                pool.tensor_tensor(small[:, 7, :], small[:, 6, :], half_n[:, :], ALU.pow).then_inc(sm("rstd_ready"), 1)

            for slot in range(2):
                pool.wait_ge(sm(f"table_out{slot}"), 16 * (NCH // 2))
            pool.wait_ge(sm("no_node_out"), 16)

            def gather(i, off):
                n, k = i * U + off, off % U
                if off >= U:
                    pool.wait_ge(sm(f"msg_out{k}"), turns(i, off, U) * 16)
                pool.wait_ge(sm("sources_ready"), n + 1)
                pool.sem_inc(sm("waited"), 1)
                for j in range(T):
                    pool.indirect_dma_start(
                        out=deal[:, k, j, 0:D], out_offset=None, in_=table[:, :],
                        in_offset=bass.IndirectOffsetOnAxis(ap=pos[:, k, j:j + 1], axis=0)).then_inc(sm(f"gathered{k}"), 16)

            for n in range(U):
                gather(0, n)
            with pool.Fori(0, G // U - 1) as i:
                for k in range(U, 2 * U):
                    gather(i, k)
            for n in range(G // U * U, G):
                gather(0, n)

            with pool.Fori(0, NCH) as it:
                pool.wait_ge(sm("var_ready"), it + (NCH + 1))
                pool.tensor_tensor(small[:, 7, :], small[:, 6, :], half_n[:, :], ALU.pow).then_inc(sm("rstd_ready"), 1)

        @block.scalar
        def _(act):
            def pick_places(i, off, final=False):
                n, b, k = i * U + off, off % 2, off % U
                act.wait_ge(sm("places_lifted"), n + 1)
                if off >= 1:
                    act.wait_ge(sm("places_picked"), n)
                for j in range(T):
                    ins = act.activation(picked[:, j, :], places[:, :, j], ACT.Relu, bias=minus_lift[:, 0:1], accum_out=posf[:, b, j:j + 1])
                ins.then_inc(sm("places_picked"), 1)
                if off >= U:
                    act.wait_ge(sm(f"dealt{k}"), turns(i, off, U) * (16 * T))
                act.wait_ge(sm("places_picked"), n + 1)
                if final:
                    for j in range(T):
                        ins = act.activation(pos[:, k, j:j + 1], posf[:, b, j:j + 1], ACT.Relu, bias=spare[:, j:j + 1])
                else:
                    ins = act.activation(pos[:, k, :], posf[:, b, :], ACT.Copy)
                ins.then_inc(sm("placed"), 1)

            def make_notes(i, off):
                n, k = i * U + off, off % U
                act.wait_ge(sm("scored"), n + 1)
                if off >= U:
                    act.wait_ge(sm(f"note_out{k}"), turns(i, off, U) * 16)
                cols = ds(n * T, T)
                act.activation(deal[:, k, :, SOURCE], ids["src"][:, cols], ACT.Copy).then_inc(sm("sources_in_rows"), 1)
                act.activation(note[:, k, 0, :], deal[:, k, :, SCORE], ACT.Copy)
                act.activation(note[:, k, 1, :], ids["dst"][:, cols], ACT.Copy).then_inc(sm("notes_made"), 1)
                act.wait_ge(sm("notes_made"), n + 1)
                act.dma_start(note_groups[ds(n, 1), :, :, :].rearrange("g p f j -> (g p) f j"), note[:, k, :, :]).then_inc(sm(f"note_out{k}"), 16)

            def exps(walk, i, off):
                n, b, c = i * BODY[walk] + off, off % 2, off % U
                scores = tbank[off % 3][:, :]
                act.wait_ge(sm(f"{walk}_bias_ready"), n + 1)
                if off >= 2:
                    act.wait_ge(sm(f"{walk}_weights_ready"), n - 1)
                if walk == "dst":
                    act.activation(exp_hi[:, b, :], scores, ACT.Exp, bias=bias_hi[:, c:c + 1])
                    act.activation(exp_lo[:, b, :], scores, ACT.Exp, bias=bias_lo[:, c:c + 1], scale=SLOPE)
                else:
                    act.activation(exp_hi[:, b, :], scores, ACT.Relu, bias=s_step[walk][:, ds(n, 1)]).then_inc(sm("src_relu"), 1)
                    act.activation(exp_lo[:, b, :], scores, ACT.Exp, bias=bias_lo[:, c:c + 1], scale=SLOPE)
                    act.wait_ge(sm("src_relu"), n + 1)
                    act.activation(exp_hi[:, b, :], exp_hi[:, b, :], ACT.Exp, bias=bias_hi[:, c:c + 1], scale=1.0 - SLOPE)
                act.activation(corr[:, c:c + 1], shift[:, c:c + 1], ACT.Exp).then_inc(sm(f"{walk}_exps_ready"), 1)

            def copy_weights(walk, i, off):
                n, b = i * BODY[walk] + off, off % 2
                act.wait_ge(sm(f"{walk}_turned_back"), n + 1)
                if off >= 2:
                    act.wait_ge(sm(f"{walk}_summed"), n - 1)
                act.activation(wgt[:, b, :], qbank[b][:, :], ACT.Copy).then_inc(sm(f"{walk}_weights_out"), 1)

            def walk_step(walk, i, off):
                exps(walk, i, off)
                if off >= BACK[walk]:
                    copy_weights(walk, i, off - BACK[walk])
                if off >= 4 and walk == "dst":
                    store_sums(i, off - 4)

            def store_sums(i, off):
                n, r = i * U + off, off % U
                act.wait_ge(sm("dst_added"), n + 1)
                act.dma_start(rows_of(sums["dst"][ds(n, 1), :, :]), acc[:, r, :]).then_inc(sm(f"sums_out{r}"), 16)

            def walk_end(walk):
                for s in range(S - BACK[walk], S):
                    copy_weights(walk, 0, s)
                if walk == "dst":
                    for s in range(S - 4, S):
                        store_sums(0, s)

            def merged(i, off):
                if off >= 1:
                    pick_places(i, off - 1)
                if off >= LAG:
                    walk_step("dst", i, off - LAG)
                make_notes(i, off)

            for n in range(2 * U):
                merged(0, n)
            with act.Fori(0, (G - 2 * U) // U) as i:
                for k in range(2 * U, 3 * U):
                    merged(i, k)
            merged(0, G - 1)
            pick_places(0, G - 1, True)
            for s in range(G - LAG, G - 1):
                walk_step("dst", 0, s)
            with act.Fori(G // U - 1, S // U - 1) as i:
                for k in range(U, 2 * U):
                    walk_step("dst", i, k)
            for s in range(S // U * U, S):
                walk_step("dst", 0, s)
            walk_end("dst")

            for s in range(2 * U):
                walk_step("src", 0, s)
            with act.Fori(0, S // (2 * U) - 1) as i:
                for k in range(2 * U, 4 * U):
                    walk_step("src", i, k)
            for s in range(S // (2 * U) * (2 * U), S):
                walk_step("src", 0, s)
            walk_end("src")

            def merge(it):
                act.wait_ge(sm("merge_ready"), it + 1)
                act.activation(scale2[:, :, :], scale2[:, :, :], ACT.Exp).then_inc(sm("merge_exp"), 1)

            def gelu(it):
                act.wait_ge(sm("agg_ready"), it + 1)
                act.activation(agg[:, :, :], agg[:, :, :], ACT.Gelu).then_inc(sm("gelu_done"), 1)

            def keep_result(it):
                act.wait_ge(sm("first_result_ready"), it + 1)
                act.activation(nodes[:, ds(it * CH, CH), :], sq[:, :, :], ACT.Copy).then_inc(sm("result_kept"), 1)

            def project(i, off):
                it, slot = i * 2 + off, off % 2
                act.wait_ge(sm("result_turned"), it + 1)
                act.activation(wT[:, 0, :], tbank[0][:, :], ACT.Copy)
                act.activation(wT[:, 1, 0:(CH - T) * P], tbank[1][:, 0:(CH - T) * P], ACT.Copy).then_inc(sm("result_copied"), 1)
                if off >= 2:
                    act.wait_ge(sm(f"table_out{slot}"), turns(i, off, 2, 2) * 16)
                act.wait_ge(sm("dinv_now_ready"), it + 1)
                act.wait_ge(sm("projection_ready"), it + 1)
                for j in range(CH):
                    ins = act.activation(projected[:, slot, j, :], qbank[j // T][:, j % T * P:(j % T + 1) * P], ACT.Copy, scale=dinv_now[:, slot, j:j + 1])
                ins.then_inc(sm("projected"), 1)
                act.wait_ge(sm("projected"), it + 1)
                act.dma_start(table_blocks[:, ds(it * CH, CH), :], projected[:, slot, :, :]).then_inc(sm(f"table_out{slot}"), 16)

            merge(0)
            for n in range(2):
                gelu(n)
                merge(n + 1)
                keep_result(n)
                project(0, n)
            with act.Fori(0, NCH // 2 - 2) as i:
                for off in (2, 3):
                    gelu(i * 2 + off)
                    merge(i * 2 + (off + 1))
                    keep_result(i * 2 + off)
                    project(i, off)
            for n in range(NCH - 2, NCH):
                gelu(n)
                if n + 1 < NCH:
                    merge(n + 1)
                keep_result(n)
                project(0, n)

            def sources(i, off):
                n, k = i * U + off, off % U
                if off >= U:
                    act.wait_ge(sm(f"gathered{k}"), turns(i, off, U) * (16 * T))
                act.activation(pos[:, k, :], ids["src"][:, ds(n * T, T)], ACT.Copy).then_inc(sm("sources_ready"), 1)

            def message_out(i, off):
                n, k = i * U + off, off % U
                act.wait_ge(sm(f"gathered{k}"), (turns(i, off, U) + 1) * (16 * T))
                act.dma_start(message_groups[ds(n, 1), :, :].rearrange("a p (j f) -> (a p) j f", j=T), deal[:, k, :, 0:D]).then_inc(sm(f"msg_out{k}"), 16)

            def message_stored(i, off):
                act.wait_ge(sm(f"msg_out{off % U}"), (turns(i, off, U) + 1) * 16)
                act.sem_inc(sm("messages_stored"), 1)

            for k in range(U):
                act.wait_ge(sm(f"dealt{k}"), ((G - 1 - k) // U + 1) * (16 * T))
            for n in range(3):
                sources(0, n)
            for n in range(U - 3):
                message_out(0, n)
                if n >= 1:
                    message_stored(0, n - 1)
                sources(0, n + 3)
            with act.Fori(0, G // U - 1) as i:
                for k in range(U, 2 * U):
                    message_out(i, k - 3)
                    message_stored(i, k - 4)
                    sources(i, k)
            for n in range(G // U * U, G):
                message_out(0, n - 3)
                message_stored(0, n - 4)
                sources(0, n)
            for n in range(G - 3, G):
                message_out(0, n)
                message_stored(0, n - 1)
            message_stored(0, G - 1)

        @block.tensor
        def _(pe):
            pe.wait_ge(sm("constants_ready"), 1)
            pe.wait_ge(sm("apart_ready"), 1)
            pe.matmul(bank[0][0:1, 0:1], unsorted[:, :], ones[:, 0:1], start=True, stop=True).then_inc(sm("flag_summed"), 1)
            pe.wait_ge(sm("flag_ready"), 1)
            flag = pe.to_reg(pe.value_load(flag_i[0:1, 0:1], min_val=0, max_val=P))

            with pe.If_ne(flag, 0):
                pe.wait_ge(sm("order_counted"), OC)
                pe.matmul(bank[0][0:NB, 0:1], total[0:OP, :, 0], ones[0:OP, 0:1], start=True, stop=True).then_inc(sm("order_totals"), 1)
                pe.wait_ge(sm("order_totals_out"), 1)
                pe.matmul(bank[1][0:OP, 0:NB], below[0:OP, 0:OP], total[0:OP, :, 0], start=True, stop=False)
                pe.matmul(bank[1][0:OP, 0:NB], s_nodeT[0:NB, 0:OP], below[0:NB, 0:NB], start=False, stop=True).then_inc(sm("order_starts"), 1)

            pe.wait_ge(sm("numbers_ready"), 2)
            for w, k in enumerate(SIDES):
                for q in range(Q):
                    for j in range(T):
                        ins = pe.transpose(bank[w * Q + q][:, j * R:(j + 1) * R],
                                           lying[k][:, q, :].bitcast(F32).rearrange("r (p j) -> r j p", j=T)[:, j, :], ident[0:R, 0:R])
                    ins.then_inc(sm("numbers_turned"), 1)

            def count_group(i, off, first=False, stop=False):
                b = off % 3
                pe.wait_ge(sm("hot_ready"), i * U + off + 1)
                pe.matmul(bank[0][:, 0:NB * T], onesb[:, :], hot[:, b, :, :].rearrange("p b j -> p (b j)"), start=first, stop=stop).then_inc(sm("hot_used"), 1)

            pe.wait_ge(sm("numbers_out"), 1)
            count_group(0, 0, first=True)
            for n in range(1, U):
                count_group(0, n)
            with pe.Fori(1, G // U) as i:
                for k in range(U):
                    count_group(i, k)
            count_group(0, G - 1, stop=True)

            pe.wait_ge(sm("starts_ready"), 1)
            pe.matmul(placebank[:, 0:NB * T], ident[:, :], total[:, :, :].rearrange("p b j -> p (b j)"), start=True, stop=True)
            for q in range(Q):
                ins = pe.matmul(bank[1][:, 0:NB], ones[0:R, 0:P], passed[:, q, :], start=q == 0, stop=q == Q - 1)
            ins.then_inc(sm("passed_summed"), 1)
            pe.wait_ge(sm("lasts_ready"), 1)
            for w, k in enumerate(SIDES):
                ins = pe.transpose(bank[2][0:NB, w * P:(w + 1) * P], last[k][:, :], ident[:, :])
            ins.then_inc(sm("lasts_turned"), 1)
            pe.wait_ge(sm("node_scores_ready"), NCH)
            pe.transpose(bank[3][0:NB, 0:P], s_node[:, :], ident[:, :]).then_inc(sm("node_scores_turned"), 1)
            pe.wait_ge(sm("done_ready"), 1)
            for w, k in enumerate(SIDES):
                ins = pe.matmul(bank[4 + w][:, 0:S], ones[0:NB, 0:P], done[0:NB, w, :], start=True, stop=True)
            ins.then_inc(sm("steps_ready"), 1)
            pe.wait_ge(sm("step_blocks_ready"), 1)
            for w, k in enumerate(SIDES):
                ins = pe.matmul(bank[w][:, 0:S], s_nodeT[0:NB, :], done[0:NB, w, :], start=True, stop=True)
            ins.then_inc(sm("step_scores_ready"), 1)

            flat = hot[:, :, :, :].rearrange("p r b j -> p r (b j)")

            def lift_places(i, off):
                n, b = i * U + off, off % 3
                pe.wait_ge(sm("hot_ready"), n + (G + 1))
                pe.matmul(placebank[:, 0:NB * T], lifted[:, :], flat[:, b, :], start=False, stop=True, skip_group_check=True).then_inc(sm("places_lifted"), 1)

            def count_on(i, off):
                n, b = i * U + off, off % 3
                pe.wait_ge(sm("places_picked"), n + 1)
                pe.matmul(placebank[:, 0:NB * T], rest[:, :], flat[:, b, :], start=False, stop=False, skip_group_check=True)
                pe.matmul(placebank[:, 0:NB * T], lower[:, :], flat[:, b, :], start=False, stop=True, skip_group_check=True).then_inc(sm("hot_used"), 1)

            def turn(walk, i, off):
                n, b, c = i * BODY[walk] + off, off % 2, off % 3
                pe.wait_ge(sm(f"{walk}_scores_ready"), n + 1)
                if off >= 3:
                    pe.wait_ge(sm(f"{walk}_exps_ready"), n - 2)
                if walk == "dst":
                    pe.matmul(tbank[c][:, :], ones[0:1, 0:P], score_row[:, c, :].rearrange("a (p j) -> a j p", j=T), start=True, stop=False)
                    for j in range(T):
                        ins = pe.matmul(tbank[c][:, j * P:(j + 1) * P], away[:, off % U, :, j], minus_big[:, :], start=False, stop=j == T - 1)
                else:
                    for j in range(T):
                        ins = pe.transpose(tbank[c][:, j * P:(j + 1) * P], masked[:, b, :, j], ident[:, :])
                ins.then_inc(sm(f"{walk}_turned"), 1)

            def turn_back(walk, i, off):
                n, b = i * BODY[walk] + off, off % 2
                pe.wait_ge(sm(f"{walk}_weights_ready"), n + 1)
                if off >= 2:
                    pe.wait_ge(sm(f"{walk}_weights_out"), n - 1)
                for j in range(T):
                    ins = pe.transpose(qbank[b][:, j * P:(j + 1) * P], wT[:, b, j * P:(j + 1) * P], ident[:, :])
                ins.then_inc(sm(f"{walk}_turned_back"), 1)

            def sum_rows(walk, i, off):
                n, b = i * BODY[walk] + off, off % 2
                pe.wait_ge(sm(f"{walk}_weights_out"), n + 1)
                if off >= 2:
                    pe.wait_ge(sm(f"{walk}_added"), n - 1)
                rows = source_rows(off) if walk == "src" else ring[:, off % U, :, :]
                if walk == "dst":
                    pe.wait_ge(sm(f"rows_in{off % U}"), (turns(i, off, U) + 1) * 16)
                for j in range(T):
                    ins = pe.matmul(obank[b][:, 0:D + 1], wgt[:, b, j * P:(j + 1) * P], rows[:, j, 0:D + 1], start=j == 0, stop=j == T - 1)
                if walk == "dst":
                    degree = obank[b][:, DEGREE:DEGREE + 1]
                    pe.matmul(degree, onesb[:, :], counts[:, 1:2], start=True, stop=False)
                    for j in range(T):
                        ins = pe.matmul(degree, away[:, off % U, :, j], counts[:, 0:1], start=False, stop=j == T - 1)
                ins.then_inc(sm(f"{walk}_summed"), 1)

            def walk_step(walk, i, off, more=True):
                if isinstance(i, int) and off == 0:
                    turn(walk, i, 0)
                    turn(walk, i, 1)
                if more:
                    turn(walk, i, off + 2)
                if off >= BACK[walk]:
                    turn_back(walk, i, off - BACK[walk])
                if off >= BACK[walk] + 1:
                    sum_rows(walk, i, off - BACK[walk] - 1)

            def walk_end(walk):
                for s in range(S - BACK[walk], S):
                    turn_back(walk, 0, s)
                    sum_rows(walk, 0, s - 1)
                sum_rows(walk, 0, S - 1)

            def merged(i, off):
                if off >= LAG:
                    walk_step("dst", i, off - LAG)
                if off >= 1:
                    count_on(i, off - 1)
                lift_places(i, off)

            pe.wait_ge(sm("step_scores_out"), 1)
            for n in range(2 * U):
                merged(0, n)
            with pe.Fori(0, (G - 2 * U) // U) as i:
                for k in range(2 * U, 3 * U):
                    merged(i, k)
            merged(0, G - 1)
            for s in range(G - LAG, G - 1):
                walk_step("dst", 0, s)
            with pe.Fori(G // U - 1, S // U - 1) as i:
                for k in range(U, 2 * U):
                    walk_step("dst", i, k)
            for s in range(S // U * U, S):
                walk_step("dst", 0, s, s + 2 < S)
            walk_end("dst")

            pe.wait_ge(sm("dst_added"), S)
            for s in range(2 * U):
                walk_step("src", 0, s)
            with pe.Fori(0, S // (2 * U) - 1) as i:
                for k in range(2 * U, 4 * U):
                    walk_step("src", i, k)
            for s in range(S // (2 * U) * (2 * U), S):
                walk_step("src", 0, s, s + 2 < S)
            walk_end("src")

            with pe.Fori(0, NCH) as it:
                pe.wait_ge(sm("first_result_ready"), it + 1)
                for j in range(CH):
                    ins = pe.transpose(tbank[j // T][:, j % T * P:(j % T + 1) * P], sq[:, j, :], ident[:, :])
                ins.then_inc(sm("result_turned"), 1)
                pe.wait_ge(sm("result_copied"), it + 1)
                for j in range(CH):
                    ins = pe.matmul(qbank[j // T][:, j % T * P:(j % T + 1) * P], wT[:, j // T, j % T * P:(j % T + 1) * P], w_proj[:, :], start=True, stop=True)
                ins.then_inc(sm("projection_ready"), 1)

            def sum_messages(i, off):
                n, b = i * U + off, off % 2
                pe.wait_ge(sm("msg_hot"), n + 1)
                k = off % U
                pe.wait_ge(sm(f"rows_in{k}"), (turns(i, off, U) + 1) * 16 + before_messages(k))
                if off >= 2:
                    pe.wait_ge(sm("msg_added"), n - 1)
                for j in range(T):
                    ins = pe.matmul(obank[b][:, 0:D], hot_rows[:, b, j, :], ring[:, off % U, j, 0:D], start=j == 0, stop=j == T - 1)
                ins.then_inc(sm("msg_summed"), 1)

            sum_messages(0, 0)
            sum_messages(0, 1)
            with pe.Fori(0, (S - 2) // U) as i:
                for k in range(2, U + 2):
                    sum_messages(i, k)

        @block.vector
        def _(dve):
            c = Chain(dve, "setup")
            c(dve.memset(ones[:, :], 1.0))
            for t in (here, there):
                dve.memset(t[:, CHECK:CHECK + TAIL_C], 0).then_inc(sm("pads_set"), 1)
            for k in SIDES:
                dve.memset(lying[k][R - 2:R, Q - 1, :], NO_NODE).then_inc(sm("pads_set"), 1)
            dve.memset(nodes[P // 2:P, NB - 1, :], 0.0)
            dve.memset(agg[:, 0, :], 0.0).then_inc(sm("pads_set"), 1)
            dve.memset(deal[:, :, :, D:ROW], 1.0)
            dve.memset(ring[:, :, :, D:ROW], 1.0)
            dve.memset(onesb[:, :], 1.0)
            dve.memset(counts[:, 0:1], -1.0)
            dve.memset(counts[:, 1:2], float(T))
            dve.memset(minus_lift[:, :], -LIFT)
            dve.memset(acc[:, :, :], 0.0)
            dve.memset(top[:, :], 0.0)
            dve.memset(least[:, :], 0.0)
            for k in SIDES:
                dve.memset(keep[k][:, 0:1], 0.0)
            dve.wait_ge(sm("iotas"), 7)
            for m, op in ((ident, ALU.is_equal), (below, ALU.is_gt), (rest, ALU.is_le)):
                dve.tensor_scalar(m[:, :], iota_f[:, :], iota_p[:, 0:1], None, op)
            c(dve.tensor_scalar(lower[:, :], iota_f[:, :], iota_p[:, 0:1], -LIFT, ALU.is_equal, ALU.mult))
            dve.tensor_scalar(minus_big[:, :], iota_f[:, :], iota_p[:, 0:1], -BIG, ALU.is_equal, ALU.mult)
            c(dve.tensor_tensor(lifted[:, :], below[:, :], lower[:, :], ALU.subtract))
            c(dve.tensor_scalar(first_of[:, :], iota_p[:, :], float(AGAIN_P), None, ALU.is_lt))
            c(dve.tensor_scalar(spare[:, :], spare[:, :], first_of[:, 0:1], None, ALU.mult))
            c(dve.tensor_scalar(first_of[:, :], iota_p[:, :], float(P), None, ALU.mult))
            dve.sem_inc(sm("constants_ready"), 1)

            dve.wait_ge(sm("check_in"), 64)
            c(dve.tensor_tensor(apart[:, 0:CHECK + TAIL_C], here[:, 0:CHECK + TAIL_C], there[:, 0:CHECK + TAIL_C], ALU.is_gt))
            dve.reduce_max(unsorted[:, :], apart[:, 0:CHECK + TAIL_C], AX.X).then_inc(sm("apart_ready"), 1)
            dve.wait_ge(sm("flag_summed"), 1)
            dve.tensor_copy(flag_i[0:1, 0:1], bank[0][0:1, 0:1]).then_inc(sm("flag_ready"), 1)
            dve.wait_ge(sm("flag_ready"), 1)
            flag = dve.to_reg(dve.value_load(flag_i[0:1, 0:1], min_val=0, max_val=P))

            with dve.If_ne(flag, 0):
                c2 = Chain(dve, "order_chain")
                dve.wait_ge(sm("order_ids"), 32)
                c2(dve.tensor_scalar(apart[0:OP, :].bitcast(I32), here[0:OP, :], LOG_P, None, ALU.arith_shift_right))
                c2(dve.tensor_copy(apart[0:OP, :], apart[0:OP, :].bitcast(I32)))
                c2(dve.memset(total[:, :, :], 0.0))
                edge_block = apart[0:OP, :]
                start, tally = total[0:OP, :, 0], iota_f[0:OP, 0:NB]
                dve.scalar_tensor_tensor(start, tally, edge_block[:, 0:1], start, ALU.is_equal, ALU.add).then_inc(sm("order_counted"), 1)
                with dve.Fori(1, OC) as col:
                    dve.wait_ge(sm("order_counted"), col)
                    dve.scalar_tensor_tensor(start, tally, edge_block[:, ds(col, 1)], start, ALU.is_equal, ALU.add).then_inc(sm("order_counted"), 1)
                dve.wait_ge(sm("order_totals"), 1)
                c2(dve.tensor_copy(unsorted[0:NB, :], bank[0][0:NB, 0:1]))
                dve.tensor_scalar(s_nodeT[0:NB, 0:OP], ones[0:NB, 0:OP], unsorted[0:NB, 0:1], None, ALU.mult).then_inc(sm("order_totals_out"), 1)
                dve.wait_ge(sm("order_starts"), 1)
                c2(dve.tensor_copy(start, bank[1][0:OP, 0:NB]))

                def order_column(at, done_before):
                    col = edge_block[:, ds(at, 1)]
                    if done_before:
                        dve.wait_ge(sm("order_next"), at)
                        for what in ("edges", "dst", "src"):
                            dve.wait_ge(sm(f"order_out_{what}"), at * 16)
                    dve.scalar_tensor_tensor(upto[0:OP, :, 0], tally, col, start, ALU.is_equal, ALU.mult, accum_out=posf[0:OP, 0, 0:1]).then_inc(sm("order_picked"), 1)
                    dve.scalar_tensor_tensor(start, tally, col, start, ALU.is_equal, ALU.add).then_inc(sm("order_next"), 1)
                    dve.tensor_copy(pos[0:OP, 0, 1:2], here[0:OP, ds(at, 1)])
                    dve.tensor_copy(pos[0:OP, 0, 2:3], there[0:OP, ds(at, 1)])
                    dve.wait_ge(sm("order_picked"), at + 1)
                    dve.tensor_copy(pos[0:OP, 0, 0:1], posf[0:OP, 0, 0:1]).then_inc(sm("order_placed"), 1)

                order_column(0, False)
                with dve.Fori(1, OC) as col:
                    order_column(col, True)

            dve.wait_ge(sm("numbers_in"), 96)
            c(dve.tensor_scalar(ends_i[:, :], lying["dst"][:, :, GE - 1], LOG_P, None, ALU.arith_shift_right))
            c(dve.tensor_copy(ends[:, :], ends_i[:, :]))
            for k in SIDES:
                dve.tensor_copy(lying[k][:, :, :].bitcast(F32), lying[k][:, :, :]).then_inc(sm("numbers_ready"), 1)
            for w, k in enumerate(SIDES):
                for q in range(Q):
                    dve.wait_ge(sm("numbers_turned"), w * Q + q + 1)
                    ins = dve.tensor_copy(ids[k][:, q * R * T:(q + 1) * R * T].rearrange("p (g j) -> p j g", j=T),
                                          bank[w * Q + q][:, 0:R * T].rearrange("p (j g) -> p j g", j=T))
            c(ins)
            dve.sem_inc(sm("numbers_out"), 1)
            for k in SIDES:
                c(dve.memset(ids[k][0:AGAIN_P, (G - 1) * T:G * T], float(NO_NODE)))
            width = Q * R * T
            c(dve.tensor_copy(here[:, 0:width], ids["src"][:, :]))
            c(dve.tensor_scalar(here[:, 0:width], here[:, 0:width], LOG_P, None, ALU.arith_shift_right))
            c(dve.tensor_copy(blk[:, :], here[:, 0:width]))

            def hot_group(i, off, again):
                n, b = i * U + off, off % 3
                if off >= 3:
                    dve.wait_ge(sm("hot_used"), n + (G - 2) if again else n - 2)
                dve.tensor_tensor(hot[:, b, :, :], iota_b[:, :, :], pair(blk[:, ds(n * T, T)], NB, T), ALU.is_equal).then_inc(sm("hot_ready"), 1)

            for n in range(U):
                hot_group(0, n, False)
            with dve.Fori(0, G // U - 1) as i:
                for k in range(U, 2 * U):
                    hot_group(i, k, False)
            hot_group(0, G - 1, False)

            dve.wait_ge(sm("weights_in"), 80)
            dve.wait_ge(sm("nodes_in"), 32)
            with dve.Fori(0, NCH) as it:
                chunk = ds(it * CH, CH)
                c2 = Chain(dve, "node_score", it * 2)
                c2(dve.tensor_tensor(sq[:, :, :], nodes[:, chunk, :], pair(w_node[:, :], CH, D), ALU.mult))
                c2(dve.reduce_sum(small[:, 0, :], sq[:, :, :], AX.X))
                dve.tensor_scalar(s_node[:, chunk], small[:, 0, :], att_bias[:, 0:1], None, ALU.add).then_inc(sm("node_scores_ready"), 1)

            for q in range(Q):
                dve.tensor_scalar(passed[:, q, :], iota_f[0:R, 0:NB], ends[:, q:q + 1], None, ALU.is_ge)
            dve.wait_ge(sm("hot_used"), G)
            c(dve.tensor_copy(total[:, :, :].rearrange("p b j -> p (b j)"), bank[0][:, 0:NB * T]))
            c(dve.tensor_tensor_scan(upto[:, :, :].rearrange("p b j -> p (b j)"), ones[:, 0:NB * T], total[:, :, :].rearrange("p b j -> p (b j)"), 0.0, ALU.mult, ALU.add))
            dve.tensor_tensor(total[:, :, :], upto[:, :, :], total[:, :, :], ALU.subtract).then_inc(sm("starts_ready"), 1)
            c(dve.tensor_copy(cum_i[:, :], upto[:, :, T - 1]))
            c(dve.tensor_scalar(cum_i[:, :], cum_i[:, :], LOG_GE, None, ALU.arith_shift_right))
            c(dve.tensor_copy(last["src"][:, :], cum_i[:, :]))
            dve.wait_ge(sm("passed_summed"), 1)
            c(dve.tensor_copy(last["dst"][:, :], bank[1][:, 0:NB]))
            for k in SIDES:
                c(dve.scalar_tensor_tensor(last[k][:, :], last[k][:, :], float(G - 1), iota_f[:, 0:NB], ALU.min, ALU.add))
                dve.tensor_copy(last_i[k][0:1, :], last[k][0:1, :])
            dve.sem_inc(sm("lasts_ready"), 1)
            dve.wait_ge(sm("lasts_turned"), 1)
            for w, k in enumerate(SIDES):
                c(dve.tensor_copy(last_col[k][0:NB, :], bank[2][0:NB, w * P:w * P + 1]))
                ins = dve.tensor_scalar(done[0:NB, w, :], iota_s[0:NB, :], last_col[k][0:NB, 0:1], None, ALU.is_gt)
            ins.then_inc(sm("done_ready"), 1)
            dve.wait_ge(sm("node_scores_turned"), 1)
            c(dve.tensor_copy(s_nodeT[0:NB, :], bank[3][0:NB, 0:P]))
            dve.wait_ge(sm("steps_ready"), 1)
            for w, k in enumerate(SIDES):
                c(dve.tensor_scalar(first_node[k][:, :], bank[4 + w][:, 0:S], float(P), None, ALU.mult))
                c(dve.tensor_tensor(keep[k][:, 1:S], first_node[k][:, 1:S], first_node[k][:, 0:S - 1], ALU.is_equal))
                dve.tensor_scalar(limit[k][:, :], keep[k][:, :], BIG, FLOOR, ALU.mult, ALU.add)
                c(dve.scalar_tensor_tensor(s_step[k][0:1, :], first_node[k][0:1, :], -1.0 / P, iota_s[0:1, :], ALU.mult, ALU.add))
                if k == "dst":
                    dve.tensor_scalar(row_i[0:1, :], s_step[k][0:1, :], float(GE), float(E - GE), ALU.mult, ALU.min)
                c(dve.tensor_copy(group_i[k][0:1, :], s_step[k][0:1, :]))
                dve.sem_inc(sm("tables_ready"), 1)
                ins = dve.tensor_scalar(done[0:NB, w, :], first_node[k][0:NB, :], first_of[0:NB, 0:1], None, ALU.is_equal)
            ins.then_inc(sm("step_blocks_ready"), 1)
            dve.wait_ge(sm("step_scores_ready"), 1)
            for w, k in enumerate(SIDES):
                c(dve.tensor_copy(s_step[k][:, :], bank[w][:, 0:S]))
            dve.sem_inc(sm("step_scores_out"), 1)

            def score(i, off):
                n, k = i * U + off, off % U
                dve.wait_ge(sm(f"edges_in{k}"), (turns(i, off, U) + 1) * 16)
                if off >= 1:
                    dve.wait_ge(sm("scored"), n)
                for j in range(T):
                    ins = dve.scalar_tensor_tensor(prod[:, j, :], deal[:, k, j, 0:D], 1.0, w_edge[:, :], ALU.mult, ALU.mult,
                                                   accum_out=deal[:, k, j, SCORE:SCORE + 1])
                ins.then_inc(sm("scored"), 1)

            class Step:

                def __init__(self, walk, i, off):
                    self.walk, self.i, self.off = walk, i, off
                    self.n, self.m = i * BODY[walk] + off, i * BODY[walk] + off + BEFORE[walk]
                    self.b, self.k, self.o = off % 2, off % U, (off - 1) % U
                    self.now, self.old = slice(off % U, off % U + 1), slice((off - 1) % U, (off - 1) % U + 1)

                def nodes_of_edges(self):
                    walk, k = self.walk, self.k
                    if walk == "src":
                        of = source_rows(self.off)[:, :, SOURCE]
                        here_sem, count = source_rows_in(self.i, self.off)
                        dve.wait_ge(here_sem, count)
                    else:
                        of = ring_target[:, k, :]
                        dve.wait_ge(sm(f"notes_in{k}"), (turns(self.i, self.off, U) + 1) * 32)
                    dve.tensor_scalar(local[:, self.b, :], of, first_node[walk][:, ds(self.n, 1)], None, ALU.subtract).then_inc(sm("walk_local"), 1)

                def whose(self):
                    if self.walk == "dst" and self.off >= U:
                        dve.wait_ge(sm("dst_summed"), self.n - (U - 1))
                    dve.wait_ge(sm("walk_local"), self.m + 1)
                    dve.tensor_tensor(away[:, self.k, :, :], iota_n[:, :, :], pair(local[:, self.b, :], P, T), ALU.not_equal).then_inc(sm("dst_scores_ready" if self.walk == "dst" else "walk_away"), 1)

                def scores(self):
                    if self.walk == "src":
                        if self.off >= 2:
                            dve.wait_ge(sm("src_turned"), self.n - 1)
                        dve.wait_ge(sm("walk_away"), self.n + 1)
                        dve.scalar_tensor_tensor(masked[:, self.b, :, :], away[:, self.k, :, :], -BIG, pair(source_rows(self.off)[:, :, SCORE], P, T), ALU.mult, ALU.add).then_inc(sm("src_scores_ready"), 1)

                def maxima(self):
                    dve.wait_ge(sm(f"{self.walk}_turned"), self.n + 1)
                    dve.reduce_max(mx[:, self.now], tbank[self.off % 3][:, :], AX.X).then_inc(sm("walk_max"), 1)

                def tops(self):
                    dve.wait_ge(sm("walk_max"), self.m + 1)
                    dve.scalar_tensor_tensor(top[:, self.now], top[:, self.old], limit[self.walk][:, ds(self.n, 1)], mx[:, self.now], ALU.min, ALU.max).then_inc(sm("walk_top"), 1)

                def lift(self):
                    dve.wait_ge(sm("walk_top"), self.m + 1)
                    dve.tensor_scalar(zneg[:, self.now], top[:, self.now], s_step[self.walk][:, ds(self.n, 1)], -1.0, ALU.add, ALU.mult).then_inc(sm("walk_zneg"), 1)

                def bend(self):
                    dve.wait_ge(sm("walk_zneg"), self.m + 1)
                    dve.scalar_tensor_tensor(least[:, self.now], zneg[:, self.now], SLOPE, zneg[:, self.now], ALU.mult, ALU.min).then_inc(sm("walk_least"), 1)

                def biases(self):
                    walk, k, now = self.walk, self.k, self.now
                    node, neg = s_step[walk][:, ds(self.n, 1)], least[:, now]
                    dve.wait_ge(sm("walk_least"), self.m + 1)
                    if walk == "dst":
                        dve.tensor_tensor(bias_hi[:, now], node, neg, ALU.add)
                        dve.scalar_tensor_tensor(bias_lo[:, now], node, SLOPE, neg, ALU.mult, ALU.add)
                    else:
                        dve.scalar_tensor_tensor(bias_hi[:, now], zneg[:, now], -SLOPE, neg, ALU.mult, ALU.add)
                        dve.tensor_scalar(bias_lo[:, now], top[:, now], -SLOPE, None, ALU.mult)
                    dve.tensor_scalar(shift[:, now], neg, least[:, self.old], limit[walk][:, ds(self.n, 1)], ALU.subtract, ALU.min).then_inc(sm(f"{walk}_bias_ready"), 1)

                def weights(self):
                    walk, n, b = self.walk, self.n, self.b
                    dve.wait_ge(sm(f"{walk}_exps_ready"), n + 1)
                    if self.off >= 2:
                        dve.wait_ge(sm(f"{walk}_turned_back"), n - 1)
                    dve.tensor_tensor(wT[:, b, :], exp_hi[:, b, :], exp_lo[:, b, :], ALU.max).then_inc(sm(f"{walk}_weights_ready"), 1)

                def add(self):
                    walk, n, r, before = self.walk, self.n, self.off % U, (self.off - 1) % U
                    dve.wait_ge(sm(f"{walk}_summed"), n + 1)
                    if self.off >= U:
                        dve.wait_ge(sm(f"sums_out{r}"), turns(self.i, self.off, U, BODY[walk]) * 16 + sums_before(walk, r))
                    if self.off >= 1:
                        dve.wait_ge(sm(f"{walk}_added"), n)
                    dve.scalar_tensor_tensor(acc[:, r, 0:D + 1], acc[:, before, 0:D + 1], corr[:, self.now], obank[self.b][:, 0:D + 1], ALU.mult, ALU.add)

                def add_columns(self):
                    walk, n, r, before = self.walk, self.n, self.off % U, (self.off - 1) % U
                    if walk == "dst":
                        dve.scalar_tensor_tensor(acc[:, r, DEGREE:DEGREE + 1], acc[:, before, DEGREE:DEGREE + 1], keep[walk][:, ds(n, 1)], obank[self.b][:, DEGREE:DEGREE + 1], ALU.mult, ALU.add)
                    dve.tensor_copy(acc[:, r, LEAST:LEAST + 1], least[:, self.now]).then_inc(sm(f"{walk}_added"), 1)

            def walk_step(walk, i, off, more=True):
                now = Step(walk, i, off)
                if isinstance(i, int) and off == 0:
                    for s in range(2):
                        first = Step(walk, i, s)
                        first.nodes_of_edges()
                        first.whose()
                        first.scores()
                later = Step(walk, i, off + 2)
                summed = Step(walk, i, off - BACK[walk] - 3) if off >= BACK[walk] + 3 else None
                now.maxima()
                if summed:
                    summed.add()
                now.tops()
                if summed:
                    summed.add_columns()
                if more:
                    later.nodes_of_edges()
                now.lift()
                if more:
                    later.whose()
                now.bend()
                if more:
                    later.scores()
                if off >= 1 and walk == "dst":
                    Step(walk, i, off - 1).weights()
                now.biases()

            def walk_end(walk):
                if walk == "dst":
                    Step(walk, 0, S - 1).weights()
                for s in range(S - BACK[walk] - 3, S):
                    Step(walk, 0, s).add()
                    Step(walk, 0, s).add_columns()

            def merged(i, off):
                hot_group(i, off, True)
                score(i, off)
                if off >= LAG:
                    walk_step("dst", i, off - LAG)

            for n in range(3 * U):
                merged(0, n)
            with dve.Fori(0, (G - 3 * U) // U) as i:
                for k in range(3 * U, 4 * U):
                    merged(i, k)
            merged(0, G - 1)
            for s in range(G - LAG, G - 1):
                walk_step("dst", 0, s)
            with dve.Fori(G // U - 2, S // U - 2) as i:
                for k in range(2 * U, 3 * U):
                    walk_step("dst", i, k)
            for s in range(S // U * U, S):
                walk_step("dst", 0, s, s + 2 < S)
            walk_end("dst")

            for r in range(U):
                dve.wait_ge(sm(f"sums_out{r}"), sums_before("src", r))
            for s in range(2 * U):
                walk_step("src", 0, s)
            with dve.Fori(0, S // (2 * U) - 1) as i:
                for k in range(2 * U, 4 * U):
                    walk_step("src", i, k)
            for s in range(S // (2 * U) * (2 * U), S):
                walk_step("src", 0, s, s + 2 < S)
            walk_end("src")

            def first_nodes(i, off):
                it, slot = i * 2 + off, off % 2
                part = parts[slot]
                c = Chain(dve, "first_nodes", it * 11)
                dve.wait_ge(sm(f"chunk_in{slot}"), (turns(i, off, 2, 2) + 1) * (32 * CH))
                c(dve.tensor_tensor(small[:, 0, :], part["src"][:, :, LEAST], part["dst"][:, :, LEAST], ALU.min))
                if off >= 1:
                    dve.wait_ge(sm("gelu_done"), it)
                for w, k in enumerate(SIDES):
                    ins = dve.tensor_tensor(scale2[:, w, :], small[:, 0, :], part[k][:, :, LEAST], ALU.subtract)
                ins.then_inc(sm("merge_ready"), 1)
                dve.tensor_scalar(small[:, 3, :], part["dst"][:, :, DEGREE], 1.0, None, ALU.add).then_inc(sm("deg_ready"), 1)
                dve.wait_ge(sm("merge_exp"), it + 1)
                for w, k in enumerate(SIDES):
                    ins = dve.tensor_tensor(small[:, 1 + w, :], scale2[:, w, :], part[k][:, :, ONE], ALU.mult)
                c(ins)
                c(dve.tensor_tensor(small[:, 1, :], small[:, 1, :], small[:, 2, :], ALU.add))
                dve.tensor_scalar(keeps[:, :], small[:, 1, :], 0.0, 1.0, ALU.is_equal, ALU.add)
                c(dve.scalar_tensor_tensor(small[:, 2, :], small[:, 1, :], 0.0, small[:, 1, :], ALU.is_equal, ALU.add))
                c(dve.reciprocal(small[:, 2, :], small[:, 2, :]))
                c(dve.tensor_tensor(scale2[:, :, :], scale2[:, :, :], pair(small[:, 2, :], 2, CH), ALU.mult))
                c(dve.tensor_tensor(part["dst"][:, :, 0:D], part["dst"][:, :, 0:D], spread(scale2[:, 1, :], CH, D), ALU.mult))
                for j in range(CH):
                    ins = dve.scalar_tensor_tensor(agg[:, j, :], part["src"][:, j, 0:D], scale2[:, 0, j:j + 1], part["dst"][:, j, 0:D], ALU.mult, ALU.add)
                ins.then_inc(sm("agg_ready"), 1)
                dve.wait_ge(sm("dinv_ready"), it + 1)
                if off >= 2:
                    dve.wait_ge(sm("projected"), it - 1)
                dve.tensor_scalar(dinv_now[:, slot, :], dinv[:, ds(it * CH, CH)], 1.0, None, ALU.mult).then_inc(sm("dinv_now_ready"), 1)
                if off >= 1:
                    dve.wait_ge(sm("result_kept"), it)
                    dve.wait_ge(sm("result_turned"), it)
                dve.wait_ge(sm("agg_ready"), it + 1)
                dve.sem_inc(sm("chunk_used"), 1)
                dve.wait_ge(sm("gelu_done"), it + 1)
                for j in range(CH):
                    ins = dve.scalar_tensor_tensor(sq[:, j, :], nodes[:, ds(it * CH + j, 1), :].rearrange("p a f -> p (a f)"), keeps[:, j:j + 1], agg[:, j, :], ALU.mult, ALU.add,
                                                   accum_out=small[:, 4, j:j + 1])
                c(ins)
                c(dve.tensor_scalar(small[:, 4, :], small[:, 4, :], -1.0 / D, None, ALU.mult))
                c(dve.tensor_tensor(sq[:, :, :], sq[:, :, :], spread(small[:, 4, :], CH, D), ALU.add))
                for j in range(CH):
                    ins = dve.scalar_tensor_tensor(agg[:, j, :], sq[:, j, :], 1.0, sq[:, j, :], ALU.mult, ALU.mult, accum_out=small[:, 5, j:j + 1])
                c(ins)
                dve.tensor_scalar(small[:, 6, :], small[:, 5, :], 1.0 / D, EPS, ALU.mult, ALU.add).then_inc(sm("var_ready"), 1)
                dve.wait_ge(sm("rstd_ready"), it + 1)
                dve.tensor_tensor(sq[:, :, :], sq[:, :, :], spread(small[:, 7, :], CH, D), ALU.mult).then_inc(sm("first_result_ready"), 1)

            first_nodes(0, 0)
            first_nodes(0, 1)
            with dve.Fori(0, NCH // 2 - 1) as i:
                for off in (2, 3):
                    first_nodes(i, off)

            def hot_targets(i, off):
                n, b, k = i * U + off, off % 2, off % U
                dve.wait_ge(sm(f"notes_in{k}"), (turns(i, off, U) + 1) * 16 + 32 * fillings(k, S))
                dve.tensor_scalar(local[:, b, :], ring_target[:, k, :], first_node["dst"][:, ds(n, 1)], None, ALU.subtract).then_inc(sm("msg_local"), 1)
                if off >= 2:
                    dve.wait_ge(sm("msg_summed"), n - 1)
                dve.wait_ge(sm("msg_local"), n + 1)
                dve.tensor_tensor(hot_rows[:, b, :, :], pair(iota_f[:, :], T, P), spread(local[:, b, :], T, P), ALU.is_equal).then_inc(sm("msg_hot"), 1)

            def add_messages(i, off):
                n, b, r = i * U + off, off % 2, off % U
                dve.wait_ge(sm("msg_summed"), n + 1)
                if off >= U:
                    dve.wait_ge(sm(f"sums_out{r}"), turns(i, off, U) * 16 + sums_before("msg", r))
                if off >= 1:
                    dve.wait_ge(sm("msg_added"), n)
                dve.scalar_tensor_tensor(acc[:, r, 0:D], acc[:, (off - 1) % U, 0:D], keep["dst"][:, ds(n, 1)], obank[b][:, 0:D], ALU.mult, ALU.add).then_inc(sm("msg_added"), 1)

            for r in range(U):
                dve.wait_ge(sm(f"sums_out{r}"), sums_before("msg", r))
            for s in range(2 * U):
                hot_targets(0, s)
                if s:
                    add_messages(0, s - 1)
            with dve.Fori(0, S // U - 2) as i:
                for k in range(2 * U, 3 * U):
                    hot_targets(i, k)
                    add_messages(i, k - 1)
            for s in range(S // U * U, S):
                hot_targets(0, s)
                add_messages(0, s - 1)
            add_messages(0, S - 1)

            def second_nodes(i, off):
                it, slot = i * 2 + off, off % 2
                part = parts[slot]
                c = Chain(dve, "second_nodes", it * 6)
                if off >= 1:
                    dve.wait_ge(sm("result_ready"), it)
                dve.wait_ge(sm(f"chunk_in{slot}"), (turns(i, off, 2, 2) + 1) * (16 * (CH + 1)) + NCH // 2 * (32 * CH))
                c(dve.tensor_tensor(sq[:, :, :], part["src"][:, :, 0:D], part["dst"][:, :, 0:D], ALU.add))
                dve.sem_inc(sm("chunk_used"), 1)
                for j in range(CH):
                    ins = dve.scalar_tensor_tensor(sq[:, j, :], sq[:, j, :], dinv[:, ds(it * CH + j, 1)], out_bias[:, :], ALU.mult, ALU.add)
                c(ins)
                for j in range(CH):
                    ins = dve.scalar_tensor_tensor(sq[:, j, :], sq[:, j, :], 0.0, nodes[:, ds(it * CH + j, 1), :].rearrange("p a f -> p (a f)"), ALU.max, ALU.add,
                                                   accum_out=small[:, 4, j:j + 1])
                c(ins)
                c(dve.tensor_scalar(small[:, 4, :], small[:, 4, :], -1.0 / D, None, ALU.mult))
                c(dve.tensor_tensor(sq[:, :, :], sq[:, :, :], spread(small[:, 4, :], CH, D), ALU.add))
                for j in range(CH):
                    ins = dve.scalar_tensor_tensor(projected[:, 0, j, :], sq[:, j, :], 1.0, sq[:, j, :], ALU.mult, ALU.mult, accum_out=small[:, 5, j:j + 1])
                c(ins)
                dve.tensor_scalar(small[:, 6, :], small[:, 5, :], 1.0 / D, EPS, ALU.mult, ALU.add).then_inc(sm("var_ready"), 1)
                dve.wait_ge(sm("rstd_ready"), it + (NCH + 1))
                if off >= 1:
                    dve.wait_ge(sm("result_out"), it * 16)
                dve.tensor_tensor(agg[:, :, :], sq[:, :, :], spread(small[:, 7, :], CH, D), ALU.mult).then_inc(sm("result_ready"), 1)

            second_nodes(0, 0)
            second_nodes(0, 1)
            with dve.Fori(0, NCH // 2 - 1) as i:
                for off in (2, 3):
                    second_nodes(i, off)

    return nc


_INS = ["x", "src", "dst", "edge_attr_128", "L0_gnn_W_att_w", "L0_gnn_W_att_b", "L1_gnn_W", "L1_gnn_b"]


def kernel(**inputs):
    import numpy as _np
    import concourse.bacc as _bacc
    from concourse import mybir as _mybir
    from concourse.bass_utils import run_bass_kernel_spmd as _run

    nc = _bacc.Bacc("TRN2", target_bir_lowering=False, num_devices=1)
    arrays, args = {}, []
    for name in _INS:
        a = _np.ascontiguousarray(inputs[name])
        arrays[f"in_{name}"] = a
        args.append(nc.dram_tensor(f"in_{name}", a.shape, _mybir.dt.from_np(a.dtype), kind="ExternalInput").ap())
    args.append(nc.dram_tensor("out_nodes", (N, D), F32, kind="ExternalOutput").ap())
    resnorm_gnn_kernel(nc, *args)
    return _run(nc, [arrays], core_ids=[0]).results[0]["out_nodes"]
```
